# Optimizing a Trainium2 kernel written in Bass

```python
import numpy as np
import jax
import jax.numpy as jnp

def _softmax(x, axis=-1):
    return jax.nn.softmax(x, axis=axis)

def _gelu(x):
    return jax.nn.gelu(x, approximate=True)

def _silu(x):
    return jax.nn.silu(x)

def _sigmoid(x):
    return jax.nn.sigmoid(x)

def _layernorm(x, axis=-1, eps=1e-05):
    m = jnp.mean(x, axis=axis, keepdims=True)
    v = jnp.var(x, axis=axis, keepdims=True)
    return (x - m) / jnp.sqrt(v + eps)

def _scatter_add(tgt, idx, src, axis=0):
    return tgt.at[idx].add(src)

def _segment_sum(src, seg, n):
    return jax.ops.segment_sum(src, seg, n)
kernel_name = 'mk_gnn_resnorm_d4_gnn_r8_2c1adf'

def setup_inputs(seed: int=0):
    np.random.seed(seed)
    _w = jnp.asarray

    def _rec_inputs():
        import jax
        import jax.numpy as jnp
        _gk = jax.random.key(seed)
        x = -0.000202 + 1 * jax.random.normal(jax.random.fold_in(_gk, 1), (6250, 128), jnp.float32)
        _s = jax.random.randint(jax.random.fold_in(_gk, 2), (50000,), 0, 6250, jnp.int32)
        _d = jax.random.randint(jax.random.fold_in(_gk, 3), (50000,), 0, 6250, jnp.int32)
        _loop = jnp.arange(6250, dtype=jnp.int32)
        src = jnp.concatenate([_s, _d, _loop])
        dst = jnp.concatenate([_d, _s, _loop])
        _o = jnp.argsort(dst, stable=True)
        src = src[_o]
        dst = dst[_o]
        edge_attr_128 = -5.16925e-05 + 1.00005 * jax.random.normal(jax.random.fold_in(_gk, 13), (106250, 128), jnp.float32)
        edge_type_4 = jax.random.randint(jax.random.fold_in(_gk, 15), (106250,), 0, 4, jnp.int32)
        edge_weight = jax.random.uniform(jax.random.fold_in(_gk, 16), (106250,), jnp.float32, 0.0, 0.999996)
        return (x, src, dst, edge_attr_128, edge_type_4, edge_weight)
    x, src, dst, edge_attr_128, edge_type_4, edge_weight = _rec_inputs()

    def _L0_gnn_setup():
        import jax, jax.numpy as jnp
        import numpy as np
        N_NODES = 6250
        N_EDGES = 100000
        N_GRAPHS = 64
        D_NODE = 128
        D_EDGE = 128
        D_GLOBAL = 128
        D_HIDDEN = 256
        D_OUT1 = 128
        D_OUT2 = 128
        key = jax.random.key(seed)
        ks = jax.random.split(key, 12)
        x = jax.random.normal(ks[0], (N_NODES, D_NODE), dtype=jnp.float32)
        edge_index = jax.random.randint(ks[1], (2, N_EDGES), 0, N_NODES, dtype=jnp.int64)
        edge_attr = jax.random.normal(ks[2], (N_EDGES, D_EDGE), dtype=jnp.float32)
        u = jax.random.normal(ks[3], (N_GRAPHS, D_GLOBAL), dtype=jnp.float32)
        batch = jnp.sort(jax.random.randint(ks[4], (N_NODES,), 0, N_GRAPHS, dtype=jnp.int64))
        s1 = 1.0 / np.sqrt(D_NODE + D_EDGE)
        W1a = jax.random.uniform(ks[5], (D_NODE + D_EDGE, D_HIDDEN), jnp.float32, -s1, s1)
        b1a = jax.random.uniform(ks[6], (D_HIDDEN,), jnp.float32, -s1, s1)
        s2 = 1.0 / np.sqrt(D_HIDDEN)
        W1b = jax.random.uniform(ks[7], (D_HIDDEN, D_OUT1), jnp.float32, -s2, s2)
        b1b = jax.random.uniform(ks[8], (D_OUT1,), jnp.float32, -s2, s2)
        s3 = 1.0 / np.sqrt(D_NODE + D_OUT1 + D_GLOBAL)
        W2a = jax.random.uniform(ks[9], (D_NODE + D_OUT1 + D_GLOBAL, D_HIDDEN), jnp.float32, -s3, s3)
        b2a = jax.random.uniform(ks[10], (D_HIDDEN,), jnp.float32, -s3, s3)
        W2b = jax.random.uniform(ks[11], (D_HIDDEN, D_OUT2), jnp.float32, -s2, s2)
        b2b = jnp.zeros((D_OUT2,), dtype=jnp.float32)
        return {'x': x, 'edge_index': edge_index, 'edge_attr': edge_attr, 'u': u, 'batch': batch, 'W1a': W1a, 'b1a': b1a, 'W1b': W1b, 'b1b': b1b, 'W2a': W2a, 'b2a': b2a, 'W2b': W2b, 'b2b': b2b}
    _L0_gnn_all = _L0_gnn_setup()
    _L0_gnn_in = {k: v for k, v in _L0_gnn_all.items() if k in ('u', 'W1a', 'b1a', 'W1b', 'b1b', 'W2a', 'b2a', 'W2b', 'b2b')}
    del _L0_gnn_all

    def _L1_gnn_setup():
        import jax, jax.numpy as jnp
        import numpy as np
        N_NODES = 6250
        N_EDGES = 100000
        D_IN = 128
        D_OUT = 128
        BN_EPS = 1e-05
        key = jax.random.key(seed)
        ks = jax.random.split(key, 8)
        node_feats = jax.random.normal(ks[0], (N_NODES, D_IN), dtype=jnp.float32)
        src = jax.random.randint(ks[1], (N_EDGES,), 0, N_NODES, dtype=jnp.int32)
        dst = jax.random.randint(ks[2], (N_EDGES,), 0, N_NODES, dtype=jnp.int32)
        scale = 1.0 / np.sqrt(D_IN)
        W = jax.random.normal(ks[3], (D_IN, D_OUT), dtype=jnp.float32) * scale
        b = jnp.zeros((D_OUT,), dtype=jnp.float32)
        Wr = jax.random.normal(ks[4], (D_IN, D_OUT), dtype=jnp.float32) * scale
        br = jnp.zeros((D_OUT,), dtype=jnp.float32)
        gamma = jnp.ones((D_OUT,), dtype=jnp.float32)
        beta = jnp.zeros((D_OUT,), dtype=jnp.float32)
        return {'node_feats': node_feats, 'src': src, 'dst': dst, 'W': W, 'b': b, 'Wr': Wr, 'br': br, 'gamma': gamma, 'beta': beta}
    _L1_gnn_all = _L1_gnn_setup()
    _L1_gnn_in = {k: v for k, v in _L1_gnn_all.items() if k in ('W', 'b', 'Wr', 'br', 'gamma', 'beta')}
    del _L1_gnn_all

    def _L2_gnn_setup():
        import jax, jax.numpy as jnp
        import numpy as np
        N_NODES = 5000
        N_EDGES = 80000
        IN_DIM = 128
        OUT_DIM = 128
        key = jax.random.key(seed)
        k1, k2, k3, k4, k5 = jax.random.split(key, 5)
        x = jax.random.normal(k1, (N_NODES, IN_DIM), dtype=jnp.float32)
        edge_src = jax.random.randint(k2, (N_EDGES,), 0, N_NODES, dtype=jnp.int32)
        edge_dst = jax.random.randint(k3, (N_EDGES,), 0, N_NODES, dtype=jnp.int32)
        W = jax.random.normal(k4, (IN_DIM, OUT_DIM), dtype=jnp.float32) * (1.0 / np.sqrt(IN_DIM))
        b = jax.random.normal(k5, (OUT_DIM,), dtype=jnp.float32) * 0.01
        return {'x': x, 'edge_src': edge_src, 'edge_dst': edge_dst, 'W': W, 'b': b}
    _L2_gnn_all = _L2_gnn_setup()
    _L2_gnn_in = {k: v for k, v in _L2_gnn_all.items() if k in ('W', 'b')}
    del _L2_gnn_all

    def _L3_gnn_setup():
        import jax, jax.numpy as jnp
        import numpy as np
        NUM_RELATIONS = 4
        N_NODES = 2500
        N_EDGES = 40000
        F_IN = 128
        HID = 128
        EMB = 128

        def _rgcn_conv(x, src, dst, edge_type, edge_weight, W, root, bias):
            xj = x[src]
            m = jnp.zeros((xj.shape[0], W.shape[2]), dtype=x.dtype)
            for r in range(W.shape[0]):
                mask = (edge_type == r).astype(x.dtype)[:, None]
                m = m + mask * (xj @ W[r])
            m = m * edge_weight[:, None]
            out = jax.ops.segment_sum(m, dst, num_segments=x.shape[0])
            return out + x @ root + bias
        key = jax.random.key(seed)
        ks = jax.random.split(key, 10)
        return {'x': jax.random.normal(ks[0], (N_NODES, F_IN), dtype=jnp.float32), 'edge_index': jax.random.randint(ks[1], (2, N_EDGES), 0, N_NODES, dtype=jnp.int64 if jax.config.jax_enable_x64 else jnp.int32).astype(jnp.int32), 'edge_type': jax.random.randint(ks[2], (N_EDGES,), 0, NUM_RELATIONS).astype(jnp.int32), 'edge_weight': jax.random.uniform(ks[3], (N_EDGES,), dtype=jnp.float32), 'W1': jax.random.normal(ks[4], (NUM_RELATIONS, F_IN, HID), dtype=jnp.float32) * 0.05, 'root1': jax.random.normal(ks[5], (F_IN, HID), dtype=jnp.float32) * 0.05, 'b1': jax.random.normal(ks[6], (HID,), dtype=jnp.float32) * 0.05, 'W2': jax.random.normal(ks[7], (NUM_RELATIONS, HID, EMB), dtype=jnp.float32) * 0.05, 'root2': jax.random.normal(ks[8], (HID, EMB), dtype=jnp.float32) * 0.05, 'b2': jax.random.normal(ks[9], (EMB,), dtype=jnp.float32) * 0.05}
    _L3_gnn_all = _L3_gnn_setup()
    _L3_gnn_in = {k: v for k, v in _L3_gnn_all.items() if k in ('W1', 'root1', 'b1', 'W2', 'root2', 'b2')}
    del _L3_gnn_all
    return {'x': x, 'src': src, 'dst': dst, 'edge_attr_128': edge_attr_128, 'edge_type_4': edge_type_4, 'edge_weight': edge_weight, 'L0_gnn_u': _L0_gnn_in['u'], 'L0_gnn_W1a': _L0_gnn_in['W1a'], 'L0_gnn_b1a': _L0_gnn_in['b1a'], 'L0_gnn_W1b': _L0_gnn_in['W1b'], 'L0_gnn_b1b': _L0_gnn_in['b1b'], 'L0_gnn_W2a': _L0_gnn_in['W2a'], 'L0_gnn_b2a': _L0_gnn_in['b2a'], 'L0_gnn_W2b': _L0_gnn_in['W2b'], 'L0_gnn_b2b': _L0_gnn_in['b2b'], 'L1_gnn_W': _L1_gnn_in['W'], 'L1_gnn_b': _L1_gnn_in['b'], 'L1_gnn_Wr': _L1_gnn_in['Wr'], 'L1_gnn_br': _L1_gnn_in['br'], 'L1_gnn_gamma': _L1_gnn_in['gamma'], 'L1_gnn_beta': _L1_gnn_in['beta'], 'L2_gnn_W': _L2_gnn_in['W'], 'L2_gnn_b': _L2_gnn_in['b'], 'L3_gnn_W1': _L3_gnn_in['W1'], 'L3_gnn_root1': _L3_gnn_in['root1'], 'L3_gnn_b1': _L3_gnn_in['b1'], 'L3_gnn_W2': _L3_gnn_in['W2'], 'L3_gnn_root2': _L3_gnn_in['root2'], 'L3_gnn_b2': _L3_gnn_in['b2']}

def reference(x, src, dst, edge_attr_128, edge_type_4, edge_weight, L0_gnn_u, L0_gnn_W1a, L0_gnn_b1a, L0_gnn_W1b, L0_gnn_b1b, L0_gnn_W2a, L0_gnn_b2a, L0_gnn_W2b, L0_gnn_b2b, L1_gnn_W, L1_gnn_b, L1_gnn_Wr, L1_gnn_br, L1_gnn_gamma, L1_gnn_beta, L2_gnn_W, L2_gnn_b, L3_gnn_W1, L3_gnn_root1, L3_gnn_b1, L3_gnn_W2, L3_gnn_root2, L3_gnn_b2):
    import jax
    import jax.numpy as jnp

    def _L0_gnn_ref(x, edge_index, edge_attr, u, batch, W1a, b1a, W1b, b1b, W2a, b2a, W2b, b2b):
        import jax, jax.numpy as jnp
        import numpy as np
        N_NODES = 6250
        N_EDGES = 100000
        N_GRAPHS = 64
        D_NODE = 128
        D_EDGE = 128
        D_GLOBAL = 128
        D_HIDDEN = 256
        D_OUT1 = 128
        D_OUT2 = 128
        row, col = (edge_index[0], edge_index[1])
        h = jnp.concatenate([x[row], edge_attr], axis=1)
        h = jax.nn.relu(h @ W1a + b1a) @ W1b + b1b
        summed = jax.ops.segment_sum(h, col, num_segments=x.shape[0])
        cnt = jax.ops.segment_sum(jnp.ones((h.shape[0],), h.dtype), col, num_segments=x.shape[0])
        agg = summed / jnp.maximum(cnt, 1.0)[:, None]
        z = jnp.concatenate([x, agg, u[batch]], axis=1)
        return jax.nn.relu(z @ W2a + b2a) @ W2b + b2b

    def _L1_gnn_ref(node_feats, src, dst, W, b, Wr, br, gamma, beta):
        import jax, jax.numpy as jnp
        import numpy as np
        N_NODES = 6250
        N_EDGES = 100000
        D_IN = 128
        D_OUT = 128
        BN_EPS = 1e-05
        N = node_feats.shape[0]
        ones_e = jnp.ones(src.shape[0], dtype=node_feats.dtype)
        deg_out = jnp.clip(jax.ops.segment_sum(ones_e, src, num_segments=N), 1.0)
        deg_in = jnp.clip(jax.ops.segment_sum(ones_e, dst, num_segments=N), 1.0)
        h = node_feats * jax.lax.rsqrt(deg_out)[:, None]
        agg = jax.ops.segment_sum(h[src], dst, num_segments=N)
        agg = agg * jax.lax.rsqrt(deg_in)[:, None]
        gcn = jax.nn.relu(agg @ W + b)
        res = jax.nn.relu(node_feats @ Wr + br)
        y = gcn + res
        mean = jnp.mean(y, axis=0)
        var = jnp.mean(jnp.square(y - mean), axis=0)
        out = (y - mean) * jax.lax.rsqrt(var + BN_EPS) * gamma + beta
        return out

    def _L2_gnn_ref(x, edge_src, edge_dst, W, b):
        import jax, jax.numpy as jnp
        import numpy as np
        N_NODES = 5000
        N_EDGES = 80000
        IN_DIM = 128
        OUT_DIM = 128
        n_nodes = x.shape[0]
        msgs = x[edge_src]
        summed = jax.ops.segment_sum(msgs, edge_dst, num_segments=n_nodes)
        deg = jax.ops.segment_sum(jnp.ones_like(edge_dst, dtype=x.dtype), edge_dst, num_segments=n_nodes)
        mean_neigh = summed / jnp.maximum(deg, 1.0)[:, None]
        return jax.nn.elu(mean_neigh @ W + b)

    def _L3_gnn_ref(x, edge_index, edge_type, edge_weight, W1, root1, b1, W2, root2, b2):
        import jax, jax.numpy as jnp
        import numpy as np
        NUM_RELATIONS = 4
        N_NODES = 2500
        N_EDGES = 40000
        F_IN = 128
        HID = 128
        EMB = 128

        def _rgcn_conv(x, src, dst, edge_type, edge_weight, W, root, bias):
            xj = x[src]
            m = jnp.zeros((xj.shape[0], W.shape[2]), dtype=x.dtype)
            for r in range(W.shape[0]):
                mask = (edge_type == r).astype(x.dtype)[:, None]
                m = m + mask * (xj @ W[r])
            m = m * edge_weight[:, None]
            out = jax.ops.segment_sum(m, dst, num_segments=x.shape[0])
            return out + x @ root + bias
        src, dst = (edge_index[0], edge_index[1])
        ew = (edge_weight - edge_weight.min()) / (edge_weight.max() - edge_weight.min() + 1e-08)
        h = jax.nn.relu(_rgcn_conv(x, src, dst, edge_type, ew, W1, root1, b1))
        h = _rgcn_conv(h, src, dst, edge_type, ew, W2, root2, b2)
        return h
    edge_index = jnp.stack([src, dst])
    batch0 = jnp.zeros((6250,), jnp.int32)
    x = _layernorm(x + _L0_gnn_ref(x, edge_index, edge_attr_128, L0_gnn_u, batch0, L0_gnn_W1a, L0_gnn_b1a, L0_gnn_W1b, L0_gnn_b1b, L0_gnn_W2a, L0_gnn_b2a, L0_gnn_W2b, L0_gnn_b2b), axis=-1)
    x = _layernorm(x + _L1_gnn_ref(x, src, dst, L1_gnn_W, L1_gnn_b, L1_gnn_Wr, L1_gnn_br, L1_gnn_gamma, L1_gnn_beta), axis=-1)
    x = _layernorm(x + _L2_gnn_ref(x, src, dst, L2_gnn_W, L2_gnn_b), axis=-1)
    x = _layernorm(x + _L3_gnn_ref(x, edge_index, edge_type_4, edge_weight, L3_gnn_W1, L3_gnn_root1, L3_gnn_b1, L3_gnn_W2, L3_gnn_root2, L3_gnn_b2), axis=-1)
    return x

_drawn_inputs = setup_inputs


def setup_inputs(seed=0):
    import zlib

    import numpy as np

    out = dict(_drawn_inputs(seed))
    spreads = {'L0_gnn_b2b': (0.0, 0.1),
     'L1_gnn_b': (0.0, 0.304),
     'L1_gnn_br': (0.0, 0.1),
     'L1_gnn_gamma': (1.0, 0.2),
     'L1_gnn_beta': (0.0, 0.1)}
    factors = {'edge_attr_128': 8.0,
     'L0_gnn_W1a': 8.0,
     'L0_gnn_b1a': 33.849,
     'L0_gnn_b1b': 8.0,
     'L0_gnn_b2a': 3.668,
     'L2_gnn_b': 3.2,
     'L3_gnn_b2': 2.941}
    for name, (base, spread) in spreads.items():
        noise = np.random.default_rng([zlib.crc32(name.encode()), seed]).standard_normal(out[name].shape)
        drawn = base * np.exp(spread * noise) if base else spread * noise
        out[name] = jnp.asarray(drawn.astype(out[name].dtype))
    for name, factor in factors.items():
        out[name] = (out[name] * factor).astype(out[name].dtype)
    return out
```

```python
from contextlib import ExitStack

import numpy as np

import concourse.bass as bass
from concourse import mybir

P = 128
N = 6250
E = 106250
F = 128
HID = 256
RELS = 4
U = 4
SLOTS = 4
GE = U * P
ITERS = -(-E // (GE * SLOTS))
GROUPS = ITERS * SLOTS
TILES = GROUPS * U
EP = TILES * P
WIN = 64
WINDOWS = -(-N // WIN)
CT = 5
CH = CT * P
CHUNKS = -(-N // (2 * CH)) * 2
NP = CHUNKS * CH
NT = NP // P
SUB = CH // 2
ACC = NP + WIN
PRIME_SLOT = SLOTS
PRIME_BANK = 2
PRIME_PAIR = 4
EPS = 1e-5

F32 = mybir.dt.float32
BF16 = mybir.dt.bfloat16
I32 = mybir.dt.int32
U32 = mybir.dt.uint32
ALU = mybir.AluOpType
ACT = mybir.ActivationFunctionType
AX_X = mybir.AxisListType.X


def gnn(nc, x_rows, x_cols, src, dst, first, etype, eweight, ea_cols, u0, W1a, b1a, W1b, b1b, W2a, b2a, W2b, b2b,
        gW, gb, gWr, gbr, gamma, beta, mW, mb, rW1, rroot1, rb1, rW2, rroot2, rb2, out):
    with ExitStack() as ctx:
        def sb(name, shape, dt=F32):
            return ctx.enter_context(nc.sbuf_tensor(name, shape, dt))

        def sem(name):
            return ctx.enter_context(nc.semaphore(name))

        def sems(name, n):
            return [sem(f"{name}{i}") for i in range(n)]

        tables = [nc.dram_tensor("table_pre", [NP, HID], F32).ap(),
                  nc.dram_tensor("table_gcn", [NP, F], F32).ap(),
                  nc.dram_tensor("table_mean", [NP, F], F32).ap(),
                  nc.dram_tensor("table_rel1", [NP * RELS, F], F32).ap(),
                  nc.dram_tensor("table_rel2", [NP * RELS, F], F32).ap()]

        acc = sb("acc", [P, 3, ACC])
        rest = acc[:, 1, 0:NP]
        X = sb("X", [P, NT, F])
        srci = sb("srci", [P, TILES + SLOTS * U], I32)
        reli = sb("reli", [P, TILES + SLOTS * U], I32)
        dstf = sb("dstf", [P, TILES])
        local = sb("local", [P, TILES])
        src_lo = sb("src_lo", [P, TILES])
        src_hi = sb("src_hi", [P, TILES])
        ew = sb("ew", [P, TILES])
        firstf = sb("firstf", [P, GROUPS])
        base = sb("base", [P, GROUPS])
        basei = sb("basei", [1, GROUPS], I32)
        slot_idx = sb("slot_idx", [P, SLOTS, U], I32)
        ident = sb("ident", [P, P])
        iota = sb("iota", [P, P])
        iota_b = sb("iota_b", [P, P], BF16)
        ones_b = sb("ones_b", [P, P], BF16)
        zeros_b = sb("zeros_b", [P, P], BF16)
        w1a = sb("w1a", [P, 2, HID])
        w1b = sb("w1b", [P, 2, F])
        w2a = sb("w2a", [P, 3, HID])
        w2b = sb("w2b", [P, 2, F])
        w_gcn = sb("w_gcn", [P, F])
        w_res = sb("w_res", [P, F])
        w_mean = sb("w_mean", [P, F])
        w_rel = [sb("w_rel1", [P, RELS, F]), sb("w_rel2", [P, RELS, F])]
        w_root = [sb("w_root1", [P, F]), sb("w_root2", [P, F])]
        bias = sb("bias", [P, 16])
        B1B, B2A0, B2A1, GB, GBR, GAMMA, BETA, MB, RB1, RB2, U0 = range(11)
        b1a_row = sb("b1a_row", [P, HID])
        b2b_row = sb("b2b_row", [P, F])
        c2 = sb("c2", [P, 2])
        stat = sb("stat", [P, 32])
        MINL, MAXL, SLOW, FAST, STEP, WOFF, EPSC, NMEAN, SSQ, VAR, RSTD, SCALE, SHIFT, WMIN, WMAX, WNEG, RNDS, STDB, WMAXP, WNEGP = range(20)
        roundsi = sb("roundsi", [1, 1], I32)
        dsc = sb("dsc", [P, NT])
        dtmp = sb("dtmp", [P, NT])
        bn = sb("bn", [P, 2, CT, 6])
        mv = sb("mv", [P, NT, 2])
        mv_slot = sb("mv_slot", [P, 2, CT, 2])
        std = sb("std", [P, NT])
        rstd = sb("rstd", [P, NT])

        work = sb("work", [P, 12800])

        def view(at, *shape):
            size = int(np.prod(shape))
            names = "abc"[:len(shape)]
            return work[:, at:at + size].rearrange(
                f"p ({' '.join(names)}) -> p {' '.join(names)}", **dict(zip(names, shape)))

        gat = view(0, SLOTS, U, HID)
        hid = view(4096, SLOTS, U * HID)
        ea = view(8192, SLOTS, GE)
        hot = view(10240, SLOTS, U * WIN)
        hot_lo = work[:, 11264:12288].bitcast(BF16).rearrange("p (s u w) -> p s u w", s=SLOTS, u=U)
        hot_hi = work[:, 12288:12288 + SLOTS * U * NT // 2].bitcast(BF16).rearrange("p (s u w) -> p s u w", s=SLOTS, u=U)
        rdeg = view(0, 2, CH)
        mean = view(1280, 2, 2 * CH)
        aggT = view(3840, 2, CH)
        xT = view(5120, 2, CH)
        h2T = view(6400, 2, 2 * CH)
        xT0 = view(11264, 2, CH)
        pre_rows = view(4096, 2, CT, HID)
        xb = view(8960, 2, CH)
        tsum = view(10240, 2, CT, F)
        rows = view(11520, 2, CT, F)
        ratio = view(8960, 2, CH)
        rel_rows = view(0, 2, CT, RELS * F)
        junk = work[:, 0:N]
        staging_a = work[:, 0:TILES].bitcast(I32)
        staging_b = work[:, 1024:1024 + TILES].bitcast(I32)
        staging_c = work[:, 2048:2048 + GROUPS].bitcast(I32)
        staging_d = work[:, 3072:3072 + TILES].bitcast(I32)
        staging_e = work[:, 10240:10240 + TILES]

        bank = [ctx.enter_context(nc.psum_tensor(f"bank{i}", [P, 512], F32)) for i in range(8)]
        HIST = 6

        s_idx, s_param, s_weight = sem("s_idx"), sem("s_param"), sem("s_weight")
        s_const, s_ident, s_prep, s_vote, s_all = sem("s_const"), sem("s_ident"), sem("s_prep"), sem("s_vote"), sem("s_all")
        s_rounds = sem("s_rounds")
        gate = sem("gate")
        idx_ready = sems("idx_ready", 5)
        gathered = [sems(f"gathered{p}_", SLOTS) for p in range(5)]
        hot_ready, seg_done, accumulated = sems("hot_ready", 5), sems("seg_done", 5), sems("accumulated", 5)
        setup_step = sems("setup_step", 5)
        pass_done, acc_zero = sems("pass_done", 5), sems("acc_zero", 5)
        table_stored = [sems(f"table{p}_stored", 2) for p in range(5)]
        STORED = 16 * CHUNKS // 2
        ea_ready = sems("ea_ready", SLOTS)
        pre_done, pre_added, relu_done = sem("pre_done"), sem("pre_added"), sem("relu_done")
        block = ctx.enter_context(nc.Block())

        def chunks(eng, body):
            body(0, 0, False)
            body(1, 1, False)
            with eng.Fori(1, CHUNKS // 2 - 1) as it:
                body(it * 2, 0, False)
                body(it * 2 + 1, 1, False)
            body(CHUNKS - 2, 0, False)
            body(CHUNKS - 1, 1, True)

        def later(k, n):
            return not isinstance(k, int) or k >= n

        def cols(k, sub=None):
            return bass.ds(k * CH, CH) if sub is None else bass.ds(k * CH + sub * SUB, SUB)

        def node_rows(table, k):
            return table.rearrange("(t p) c -> p t c", p=P)[:, bass.ds(k * CT, CT), :]

        xT0_ready = sems("xT0_ready", 2)
        y_done, y_added = sem("y_done"), sem("y_added")

        def start_sp(sp):
            sp.dma_start(w1a[:, :, :], W1a.rearrange("(c p) n -> p c n", p=P)).then_inc(s_weight, 16)
            sp.dma_start(b1a_row[:, :], b1a.partition_broadcast(P)).then_inc(s_weight, 16)

            def load(k, s, last):
                if later(k, 2):
                    sp.wait_ge(y_done, k - 1)
                sp.sem_inc(gate, 1)
                sp.dma_start(xT0[:, s, :], x_cols[:, cols(k)]).then_inc(xT0_ready[s], 16)
            chunks(sp, load)

        def start_act_loads(act):
            act.dma_start(staging_a, dst).then_inc(s_idx, 16)
            act.dma_start(staging_c, first.partition_broadcast(P)).then_inc(s_idx, 16)
            act.dma_start(srci[:, :], src).then_inc(s_idx, 16)
            act.dma_start(staging_b, etype).then_inc(s_idx, 16)
            act.dma_start(staging_e, eweight).then_inc(s_idx, 16)
            for c, b in ((B1B, b1b), (GB, gb), (GBR, gbr), (GAMMA, gamma), (BETA, beta), (MB, mb), (RB1, rb1), (RB2, rb2)):
                act.dma_start(bias[:, c:c + 1], b.rearrange("(f o) -> f o", o=1)).then_inc(s_param, 16)
            act.dma_start(bias[:, B2A0:B2A0 + 1], b2a[0:F].rearrange("(f o) -> f o", o=1)).then_inc(s_param, 16)
            act.dma_start(bias[:, B2A1:B2A1 + 1], b2a[F:HID].rearrange("(f o) -> f o", o=1)).then_inc(s_param, 16)
            act.dma_start(bias[:, U0:U0 + 1], u0.rearrange("(f o) -> f o", o=1)).then_inc(s_param, 16)
            act.dma_start(b2b_row[:, :], b2b.partition_broadcast(P)).then_inc(s_param, 16)
            act.dma_start(w1b[:, :, :], W1b.rearrange("(c p) n -> p c n", p=P)).then_inc(s_param, 16)
            act.dma_start(w2a[:, :, :], W2a.rearrange("(c p) n -> p c n", p=P)).then_inc(s_param, 16)
            act.dma_start(w2b[:, :, :], W2b.rearrange("(c p) n -> p c n", p=P)).then_inc(s_param, 16)
            act.dma_start(w_gcn[:, :], gW).then_inc(s_param, 16)
            act.dma_start(w_res[:, :], gWr).then_inc(s_param, 16)
            act.dma_start(w_mean[:, :], mW).then_inc(s_param, 16)
            for i, (w, r) in enumerate(((rW1, rroot1), (rW2, rroot2))):
                act.dma_start(w_rel[i][:, :, :], w.rearrange("r i o -> i r o")).then_inc(s_param, 16)
                act.dma_start(w_root[i][:, :], r).then_inc(s_param, 16)
            act.dma_start(X[:, :, :], x_rows.rearrange("(t p) f -> p t f", p=P)).then_inc(s_param, 16)
        PARAMS = 16 * 23

        def start_pe(pe):
            pe.wait_ge(s_weight, 32)

            def body(k, s, last):
                pe.wait_ge(xT0_ready[s], (k - s) * 8 + 16)
                if later(k, 1):
                    pe.wait_ge(y_added, k * 3)
                for t in range(CT):
                    mm = pe.matmul(bank[t // 2][:, t % 2 * HID:(t % 2 + 1) * HID], xT0[:, s, t * P:(t + 1) * P],
                                   w1a[:, 0, :], start=True, stop=True)
                mm.then_inc(y_done, 1)
            chunks(pe, body)

        def start_dve_rows(dve):
            dve.wait_ge(s_weight, 32)

            def body(k, s, last):
                for b in range(3):
                    n = 2 if b < 2 else 1
                    dve.wait_ge(y_done, k + 1)
                    if later(k, 2):
                        dve.wait_ge(table_stored[0][s], (k - s) * 8)
                    dve.tensor_tensor(pre_rows[:, s, 2 * b:2 * b + n, :],
                                      bank[b][:, 0:n * HID].rearrange("p (t h) -> p t h", t=n),
                                      b1a_row[:, :].unsqueeze(1).broadcast_to([P, n, HID]), ALU.add).then_inc(y_added, 1)
            chunks(dve, body)

        def start_act_store(act):
            def body(k, s, last):
                act.wait_ge(y_added, k * 3 + 3)
                act.dma_start(node_rows(tables[0], k), pre_rows[:, s, :, :]).then_inc(table_stored[0][s], 16)
            chunks(act, body)

        def start_pool(pool):
            pool.iota(staging_d[:, 0:P], pattern=[[1, P]], base=0, channel_multiplier=0).then_inc(s_const, 1)
            pool.memset(ident[:, :], 0.0).then_inc(s_const, 1)
            pool.memset(ones_b[:, :], 1.0).then_inc(s_const, 1)
            pool.memset(zeros_b[:, :], 0.0).then_inc(s_const, 1)
            pool.memset(acc[:, :, :], 0.0).then_inc(s_const, 1)
            pool.memset(stat[:, EPSC:EPSC + 1], EPS).then_inc(s_const, 1)
            pool.wait_ge(s_const, 2)
            pool.affine_select(out=ident[:, :], in_=ident[:, :], compare_op=ALU.not_equal, fill=1.0, base=0,
                               pattern=[[-1, P]], channel_multiplier=1).then_inc(s_ident, 1)
            pool.wait_ge(s_vote, 3)
            RMAX = bass.bass_isa.ReduceOp.max
            pool.partition_all_reduce(stat[:, SLOW:SLOW + 1], stat[:, MAXL:MAXL + 1], P, RMAX).then_inc(s_all, 1)
            pool.partition_all_reduce(stat[:, WMAX:WMAX + 1], stat[:, WMAXP:WMAXP + 1], P, RMAX).then_inc(s_all, 1)
            pool.partition_all_reduce(stat[:, WNEG:WNEG + 1], stat[:, WNEGP:WNEGP + 1], P, RMAX).then_inc(s_all, 1)

        def start_dve(dve):
            n = [0]

            def done(ins):
                n[0] += 1
                ins.then_inc(s_prep, 1)
                dve.wait_ge(s_prep, n[0])

            dve.wait_ge(s_const, 6)
            done(dve.tensor_copy(iota[:, :], staging_d[:, 0:P]))
            done(dve.tensor_copy(iota_b[:, :], staging_d[:, 0:P]))
            dve.wait_ge(s_idx, 80)
            done(dve.tensor_copy(dstf[:, :], staging_a))
            done(dve.tensor_copy(firstf[:, :], staging_c))
            done(dve.tensor_tensor(local[:, :].rearrange("p (g u) -> p g u", u=U),
                                   dstf[:, :].rearrange("p (g u) -> p g u", u=U),
                                   firstf[:, :].unsqueeze(2).broadcast_to([P, GROUPS, U]), ALU.subtract))
            done(dve.tensor_reduce(stat[:, MINL:MINL + 1], local[:, :], AX_X, ALU.min))
            done(dve.tensor_reduce(stat[:, MAXL:MAXL + 1], local[:, :], AX_X, ALU.max))
            done(dve.tensor_scalar(stat[:, MINL:MINL + 1], stat[:, MINL:MINL + 1], -1.0, None, ALU.mult))
            done(dve.tensor_scalar(stat[:, MAXL:MAXL + 1], stat[:, MAXL:MAXL + 1], 1.0 - WIN, stat[:, MINL:MINL + 1],
                                   ALU.add, ALU.max))
            done(dve.tensor_reduce(stat[:, WMAXP:WMAXP + 1], staging_e, AX_X, ALU.max))
            done(dve.tensor_reduce(stat[:, WMIN:WMIN + 1], staging_e, AX_X, ALU.min))
            done(dve.tensor_scalar(stat[:, WNEGP:WNEGP + 1], stat[:, WMIN:WMIN + 1], -1.0, None, ALU.mult))
            dve.sem_inc(s_vote, 3)
            done(dve.tensor_scalar(reli[:, 0:TILES], srci[:, 0:TILES], 7, None, ALU.logical_shift_right))
            done(dve.tensor_copy(src_hi[:, :], reli[:, 0:TILES]))
            done(dve.tensor_scalar(staging_d, srci[:, 0:TILES], P - 1, None, ALU.bitwise_and))
            done(dve.tensor_copy(src_lo[:, :], staging_d))
            done(dve.scalar_tensor_tensor(reli[:, 0:TILES], srci[:, 0:TILES], float(RELS), staging_b, ALU.mult, ALU.add))
            done(dve.tensor_copy(reli[:, TILES:], reli[:, 0:SLOTS * U]))
            dve.wait_ge(s_all, 3)
            done(dve.tensor_scalar(stat[:, SLOW:SLOW + 1], stat[:, SLOW:SLOW + 1], 0.0, None, ALU.is_gt))
            done(dve.tensor_scalar(stat[:, FAST:FAST + 1], stat[:, SLOW:SLOW + 1], -1.0, 1.0, ALU.mult, ALU.add))
            done(dve.tensor_scalar(stat[:, STEP:STEP + 1], stat[:, SLOW:SLOW + 1], float(WIN), None, ALU.mult))
            done(dve.tensor_scalar(stat[:, RNDS:RNDS + 1], stat[:, SLOW:SLOW + 1], float(WINDOWS - 1), 1.0, ALU.mult, ALU.add))
            dve.tensor_copy(roundsi[:, :], stat[0:1, RNDS:RNDS + 1]).then_inc(s_rounds, 1)
            done(dve.tensor_tensor(stat[:, WMAX:WMAX + 1], stat[:, WMAX:WMAX + 1], stat[:, WNEG:WNEG + 1], ALU.add))
            done(dve.tensor_scalar(stat[:, WMAX:WMAX + 1], stat[:, WMAX:WMAX + 1], 1e-8, None, ALU.add))
            done(dve.reciprocal(stat[:, WMAX:WMAX + 1], stat[:, WMAX:WMAX + 1]))
            done(dve.tensor_scalar(ew[:, :], staging_e, stat[:, WNEG:WNEG + 1], stat[:, WMAX:WMAX + 1], ALU.add, ALU.mult))

        def load_rounds(eng):
            eng.wait_ge(s_rounds, 1)
            return eng.value_load(roundsi[0:1, 0:1], min_val=1, max_val=WINDOWS)

        def groups(eng, rounds, body, each_round=None):
            with eng.Fori(0, rounds) as r:
                if each_round:
                    each_round(r)
                with eng.Fori(0, ITERS) as it:
                    m = r * ITERS + it
                    body(it, m, m * SLOTS)

        def idx_of(p):
            return reli if p >= 3 else srci

        def pass_act_first(act, p, rounds):
            if p:
                act.wait_ge(idx_ready[p - 1], rounds * GROUPS + SLOTS)
                act.sem_inc(gate, 1)
            if p in (1, 2, 4):
                act.sem_inc(idx_ready[p], SLOTS)
                return
            for q in range(SLOTS):
                act.copy(slot_idx[:, q, :], idx_of(p)[:, q * U:(q + 1) * U]).then_inc(idx_ready[p], 1)

        def next_idx(act, p, it, m, q):
            act.wait_ge(gathered[p][q], (m + 1) * 16 * U)
            act.sem_inc(gate, 1)
            act.copy(slot_idx[:, q, :], idx_of(p)[:, bass.ds((it * SLOTS + SLOTS + q) * U, U)]).then_inc(idx_ready[p], 1)

        def pass_pool(pool, p, rounds):
            width = HID if p == 0 else F
            for s in table_stored[p]:
                pool.wait_ge(s, STORED)
                pool.sem_inc(gate, 1)

            def body(it, m, n):
                for q in range(SLOTS):
                    pool.wait_ge(idx_ready[p], n + q + 1)
                    pool.sem_inc(gate, 1)
                    if p == 0:
                        pool.wait_ge(relu_done, (n + q) * 2 + 2)
                    else:
                        pool.wait_ge(seg_done[p], n + q + 1)
                    pool.sem_inc(gate, 1)
                    for u in range(U):
                        pool.indirect_dma_start(
                            gat[:, q, u, 0:width], None, tables[p],
                            bass.IndirectOffsetOnAxis(ap=slot_idx[:, q, u:u + 1].bitcast(U32), axis=0),
                        ).then_inc(gathered[p][q], 16)
            groups(pool, rounds, body)

        def round_setup(dve, p, r):
            s = setup_step[p]
            dve.wait_ge(s, r * 4 + 1)
            dve.tensor_scalar(base[:, :], firstf[:, :], stat[:, FAST:FAST + 1], stat[:, WOFF:WOFF + 1],
                              ALU.mult, ALU.add).then_inc(s, 1)
            dve.wait_ge(s, r * 4 + 2)
            dve.tensor_tensor(local[:, :].rearrange("p (g u) -> p g u", u=U),
                              dstf[:, :].rearrange("p (g u) -> p g u", u=U),
                              base[:, :].unsqueeze(2).broadcast_to([P, GROUPS, U]), ALU.subtract).then_inc(s, 1)
            dve.tensor_copy(basei[:, :], base[0:1, :]).then_inc(s, 1)
            dve.wait_ge(s, r * 4 + 4)
            dve.tensor_tensor(stat[:, WOFF:WOFF + 1], stat[:, WOFF:WOFF + 1], stat[:, STEP:STEP + 1],
                              ALU.add).then_inc(s, 1)

        def load_bases(dve, it):
            return [dve.value_load(basei[0:1, bass.ds(it * SLOTS + q, 1)], min_val=0, max_val=NP) for q in range(SLOTS)]

        def one_hot(dve, p, it, n, q):
            dve.wait_ge(seg_done[p], n + q + 1)
            mine = local[:, bass.ds((it * SLOTS + q) * U, U)]
            ins = dve.tensor_tensor(hot[:, q, :].rearrange("p (u w) -> p u w", u=U),
                                    iota[:, 0:WIN].unsqueeze(1).broadcast_to([P, U, WIN]),
                                    mine.unsqueeze(2).broadcast_to([P, U, WIN]), ALU.is_equal)
            if p == 0:
                dve.tensor_tensor(hot_hi[:, q, :, :], iota[:, 0:NT].unsqueeze(1).broadcast_to([P, U, NT]),
                                  src_hi[:, bass.ds((it * SLOTS + q) * U, U)].unsqueeze(2).broadcast_to([P, U, NT]),
                                  ALU.is_equal)
                for u in range(U):
                    ins = dve.tensor_scalar(hot_lo[:, q, u, :], iota_b[:, :],
                                            src_lo[:, bass.ds((it * SLOTS + q) * U + u, 1)], None, ALU.is_equal)
            ins.then_inc(hot_ready[p], 1)

        def weighted_hot(dve, p, it, n, q):
            dve.wait_ge(seg_done[p], n + q + 1)
            for u in range(U):
                t = (it * SLOTS + q) * U + u
                ins = dve.tensor_scalar(hot[:, q, u * WIN:(u + 1) * WIN], iota[:, 0:WIN], local[:, bass.ds(t, 1)],
                                        ew[:, bass.ds(t, 1)], ALU.is_equal, ALU.mult)
            ins.then_inc(hot_ready[p], 1)

        def accumulate(dve, p, at, n, q):
            planes = 3 if p == 0 else 1
            there = acc[:, 0:planes, bass.ds(at, WIN)]
            dve.wait_ge(seg_done[p], n + q + 1 + PRIME_SLOT)
            dve.wait_ge(accumulated[p], n + q + PRIME_BANK)
            dve.tensor_tensor(there, there, bank[4 + q % 2][:, 0:planes * WIN].rearrange("p (c w) -> p c w", c=planes),
                              ALU.add).then_inc(accumulated[p], 1)

        def pass_dve(dve, p, rounds):
            dve.sem_inc(accumulated[p], PRIME_BANK)
            dve.memset(stat[:, WOFF:WOFF + 1], 0.0).then_inc(setup_step[p], 1)
            if p == 0:
                dve.sem_inc(pre_added, PRIME_PAIR)
            else:
                dve.wait_ge(acc_zero[p], 1)

            def body(it, m, n):
                at = load_bases(dve, it)
                if p == 0:
                    for q in range(SLOTS):
                        one_hot(dve, p, it, n, q)
                        for h in range(2):
                            g = gat[:, q, 2 * h:2 * h + 2, :].rearrange("p u c -> p (u c)")
                            dve.wait_ge(gathered[p][q], (m + 1) * 16 * U)
                            dve.wait_ge(pre_done, (n + q) * 2 + h + 1 + 2 * SLOTS)
                            dve.tensor_tensor(g, g, bank[q % 2 * 2 + h][:, :], ALU.add).then_inc(pre_added, 1)
                        if q:
                            accumulate(dve, p, at[q - 1], n, q - 1)
                    accumulate(dve, p, at[SLOTS - 1], n, SLOTS - 1)
                else:
                    for q in range(SLOTS):
                        (weighted_hot if p >= 3 else one_hot)(dve, p, it, n, q)
                    for q in range(SLOTS):
                        accumulate(dve, p, at[q], n, q)

            def setup(r):
                round_setup(dve, p, r)
                dve.wait_ge(setup_step[p], r * 4 + 5)
                dve.sem_inc(gate, 1)
            with dve.Fori(0, rounds) as r:
                setup(r)
                with dve.Fori(0, ITERS) as it:
                    m = r * ITERS + it
                    body(it, m, m * SLOTS)
                if p == 0:
                    dve.wait_ge(hot_ready[0], (r + 1) * GROUPS)
                    dve.tensor_scalar(src_lo[:, :], src_lo[:, :], 0.0, -1.0, ALU.mult, ALU.add)
            dve.wait_ge(accumulated[p], rounds * GROUPS + PRIME_BANK)
            dve.sem_inc(pass_done[p], 1)

        def segment_sum(pe, p, n, q):
            pe.wait_ge(hot_ready[p], n + q + 1)
            pe.wait_ge(accumulated[p], n + q + 1)
            into = bank[4 + q % 2]
            if p:
                for u in range(U):
                    mm = pe.matmul(into[:, 0:WIN], gat[:, q, u, 0:F], hot[:, q, u * WIN:(u + 1) * WIN],
                                   start=(u == 0), stop=(u == U - 1))
            else:
                for c in range(2):
                    for u in range(U):
                        pe.matmul(into[:, c * WIN:(c + 1) * WIN], hid[:, q, u * HID + c * F:u * HID + (c + 1) * F],
                                  hot[:, q, u * WIN:(u + 1) * WIN], start=(u == 0), stop=(u == U - 1))
                upper = hot[:, q, :].bitcast(BF16).rearrange("p (u w t) -> p u w t", u=U, t=2)
                for u in range(U):
                    pe.matmul(into[:, 2 * WIN:3 * WIN], ones_b[:, :], upper[:, u, :, 1], start=(u == 0), stop=(u == U - 1))
                for u in range(U):
                    mm = pe.matmul(bank[HIST][:, 0:NT], hot_lo[:, q, u, :], hot_hi[:, q, u, :], start=False, stop=False,
                                   skip_group_check=True)
            mm.then_inc(seg_done[p], 1)

        def pass_pe(pe, p, rounds):
            pe.sem_inc(seg_done[p], PRIME_SLOT)
            if p == 0:
                pe.sem_inc(pre_done, 2 * SLOTS)
                pe.wait_ge(s_const, 6)
                pe.matmul(bank[HIST][:, 0:NT], zeros_b[:, :], zeros_b[:, 0:NT], start=True, stop=False, skip_group_check=True)

            def pre(m, n, q):
                pe.wait_ge(ea_ready[q], (m + 1) * 16)
                for h in range(2):
                    pe.wait_ge(pre_added, (n + q) * 2 + h + 1)
                    for j in range(2):
                        u = 2 * h + j
                        mm = pe.matmul(bank[q % 2 * 2 + h][:, j * HID:(j + 1) * HID], ea[:, q, u * P:(u + 1) * P],
                                       w1a[:, 1, :], start=True, stop=True)
                    mm.then_inc(pre_done, 1)

            def body(it, m, n):
                if p == 0:
                    for q in range(SLOTS):
                        pre(m, n, q)
                        if q:
                            pe.wait_ge(relu_done, (n + q - 1) * 2 + 2 + 2 * SLOTS)
                            segment_sum(pe, p, n, q - 1)
                    pe.wait_ge(relu_done, (n + SLOTS - 1) * 2 + 2 + 2 * SLOTS)
                    segment_sum(pe, p, n, SLOTS - 1)
                else:
                    for q in range(SLOTS):
                        pe.wait_ge(gathered[p][q], (m + 1) * 16 * U)
                        segment_sum(pe, p, n, q)
            groups(pe, rounds, body)

        def pass0_act(act, rounds):
            act.sem_inc(relu_done, 2 * SLOTS)
            pass_act_first(act, 0, rounds)
            act.preload_act_table(ACT.Relu)

            def body(it, m, n):
                for q in range(SLOTS):
                    for h in range(2):
                        act.wait_ge(pre_added, (n + q) * 2 + h + 1 + PRIME_PAIR)
                        act.wait_ge(seg_done[0], n + q + 1)
                        act.activation(hid[:, q, h * 2 * HID:(h + 1) * 2 * HID],
                                       gat[:, q, 2 * h:2 * h + 2, :].rearrange("p u c -> p (u c)"),
                                       ACT.Relu).then_inc(relu_done, 1)
                    next_idx(act, 0, it, m, q)
            groups(act, rounds, body)

        def pass_act(act, p, rounds):
            def body(it, m, n):
                for q in range(SLOTS):
                    next_idx(act, p, it, m, q)
            groups(act, rounds, body)

        def pass0_sp(sp, rounds):
            def body(it, m, n):
                for q in range(SLOTS):
                    sp.wait_ge(pre_done, (n + q) * 2 + 2)
                    sp.sem_inc(gate, 1)
                    sp.dma_start(ea[:, q, :], ea_cols[:, bass.ds((it * SLOTS + q) * GE, GE)]).then_inc(ea_ready[q], 16)
            groups(sp, rounds, body)

        def norm_stats(dve, step, k, s):
            for j in range(CT):
                ins = dve.bn_stats(bn[:, s, j, :], tsum[:, s, j, :])
            ins.then_inc(step, 1)
            dve.wait_ge(step, k * 4 + 1)
            dve.sem_inc(gate, 1)
            for j in range(CT):
                ins = dve.bn_aggr(mv[:, s * CT + j, :], bn[:, s, j, :])
            ins.then_inc(step, 1)

        def norm_root(act, step, root, k, s):
            act.wait_ge(step, k * 4 + 2)
            act.activation(std[:, s * CT:(s + 1) * CT], mv[:, s * CT:(s + 1) * CT, 1], ACT.Sqrt,
                           bias=stat[:, EPSC:EPSC + 1]).then_inc(root, 1)

        def norm_apply(dve, step, root, k, s, to):
            dve.wait_ge(root, k + 1)
            dve.reciprocal(rstd[:, s * CT:(s + 1) * CT], std[:, s * CT:(s + 1) * CT]).then_inc(step, 1)
            dve.wait_ge(step, k * 4 + 3)
            for j in range(CT):
                ins = dve.tensor_scalar(to(j), tsum[:, s, j, :], mv[:, s * CT + j, 0:1], rstd[:, s * CT + j:s * CT + j + 1],
                                        ALU.subtract, ALU.mult)
            ins.then_inc(step, 1)

        def x_row(k):
            return lambda j: X[:, bass.ds(k * CT + j, 1), :].rearrange("p o f -> p (o f)")

        def two_banks(a, b):
            return ((0, 3, bank[a][:, 0:3 * F]), (3, 2, bank[b][:, 0:2 * F]))

        def turn(pe, tile_of, a, b):
            for t0, n, into in two_banks(a, b):
                for j in range(n):
                    mm = pe.transpose(into[:, j * P:(j + 1) * P], tile_of(t0 + j), ident[:, :])
            return mm

        def xT_tile(s):
            return lambda t: xT[:, s, t * P:(t + 1) * P]

        def add_x(dve, k, s, a, b, done):
            for t0, n, b_ in two_banks(a, b):
                dve.tensor_tensor(tsum[:, s, t0:t0 + n, :], b_.rearrange("p (t f) -> p t f", f=F),
                                  X[:, bass.ds(k * CT + t0, n), :], ALU.add).then_inc(done, 1)

        def clear_sums(pool, p, read):
            pool.wait_ge(read, CHUNKS)
            pool.sem_inc(gate, 1)
            pool.memset(acc[:, 0, :], 0.0).then_inc(acc_zero[p + 1], 1)

        (n0_mean, n0_agg, n0_aggT, n0_hid, n0_relu, n0_out, n0_step, n0_root, n0_pre, n0_bias, n0_rows, n0_c2, n0_deg,
         n0_sum) = (sem(f"n0_{x}") for x in ("mean", "agg", "aggT", "hid", "relu", "out", "step", "root", "pre", "bias", "rows",
                                            "c2", "deg", "sum"))
        n0_xT = sems("n0_xT", 2)

        def node0_sp(sp):
            sp.wait_ge(pass_done[0], 1)

            def load(k, s, last):
                if later(k, 2):
                    sp.wait_ge(n0_hid, k - 1)
                sp.sem_inc(gate, 1)
                sp.dma_start(xT[:, s, :], x_cols[:, cols(k)]).then_inc(n0_xT[s], 16)
            chunks(sp, load)

        def node0_pool(pool):
            def store(k, s, last):
                if last:
                    clear_sums(pool, 0, n0_mean)
                pool.wait_ge(n0_rows, k + 1)
                pool.sem_inc(gate, 1)
                pool.dma_start(node_rows(tables[1], k), rows[:, s, :, :]).then_inc(table_stored[1][s], 16)
            chunks(pool, store)

        def node0_pe(pe):
            pe.wait_ge(s_param, PARAMS)
            pe.wait_ge(s_ident, 1)
            pe.wait_ge(pass_done[0], 1)
            for c in range(2):
                mm = pe.matmul(bank[7][:, c:c + 1], w2a[:, 2, c * F:(c + 1) * F], bias[:, U0:U0 + 1], start=True, stop=True)
            mm.then_inc(n0_c2, 1)

            def agg(k, s):
                pe.wait_ge(n0_mean, k + 1)
                if later(k, 1):
                    pe.wait_ge(n0_aggT, k * 2)
                for sub in range(2):
                    for c in range(2):
                        mm = pe.matmul(bank[sub][:, 0:SUB], w1b[:, c, :],
                                       mean[:, s, c * CH + sub * SUB:c * CH + (sub + 1) * SUB], start=(c == 0), stop=(c == 1))
                mm.then_inc(n0_agg, 1)

            def body(k, s, last):
                pe.wait_ge(n0_xT[s], (k - s) * 8 + 16)
                if later(k, 1):
                    pe.wait_ge(n0_relu, k * 4)
                for c in range(2):
                    for sub in range(2):
                        pe.matmul(bank[2 + 2 * c + sub][:, 0:SUB], w2a[:, 0, c * F:(c + 1) * F],
                                  xT[:, s, sub * SUB:(sub + 1) * SUB], start=True, stop=False)
                pe.wait_ge(n0_aggT, k * 2 + 2)
                for c in range(2):
                    for sub in range(2):
                        mm = pe.matmul(bank[2 + 2 * c + sub][:, 0:SUB], w2a[:, 1, c * F:(c + 1) * F],
                                       aggT[:, s, sub * SUB:(sub + 1) * SUB], start=False, stop=True)
                mm.then_inc(n0_hid, 1)
                if not last:
                    agg(k + 1, 1 - s)
                pe.wait_ge(n0_relu, k * 4 + 4)
                if later(k, 1):
                    pe.wait_ge(n0_sum, k * 2)
                else:
                    pe.wait_ge(n0_deg, 1)
                for t0, n, into in two_banks(6, 7):
                    for j in range(n):
                        for c in range(2):
                            at = c * CH + (t0 + j) * P
                            mm = pe.matmul(into[:, j * F:(j + 1) * F], h2T[:, s, at:at + P], w2b[:, c, :],
                                           start=(c == 0), stop=(c == 1))
                mm.then_inc(n0_out, 1)
            agg(0, 0)
            chunks(pe, body)

        def node0_act(act):
            act.preload_act_table(ACT.Sqrt)
            act.wait_ge(n0_deg, 1)
            act.activation(dtmp[:, :], dsc[:, :], ACT.Sqrt).then_inc(n0_deg, 1)
            act.wait_ge(n0_deg, 3)

            def body(k, s, last):
                act.wait_ge(n0_hid, k + 1)
                for c in range(2):
                    for sub in range(2):
                        act.activation(h2T[:, s, c * CH + sub * SUB:c * CH + (sub + 1) * SUB],
                                       bank[2 + 2 * c + sub][:, 0:SUB], ACT.Relu, bias=c2[:, c:c + 1]).then_inc(n0_relu, 1)
                norm_root(act, n0_step, n0_root, k, s)
                act.wait_ge(n0_step, k * 4 + 4)
                if later(k, 2):
                    act.wait_ge(table_stored[1][s], (k - s) * 8)
                act.sem_inc(gate, 1)
                for j in range(CT):
                    ins = act.activation(rows[:, s, j, :], x_row(k)(j), ACT.Copy, scale=dsc[:, bass.ds(k * CT + j, 1)])
                ins.then_inc(n0_rows, 1)
            chunks(act, body)

        def node0_dve(dve):
            dve.wait_ge(s_param, PARAMS)
            dve.wait_ge(n0_c2, 1)
            dve.tensor_tensor(c2[:, :], bank[7][:, 0:2], bias[:, B2A0:B2A1 + 1], ALU.add)
            dve.tensor_scalar(dsc[:, :], bank[HIST][:, 0:NT], 1.0, None, ALU.max).then_inc(n0_deg, 1)
            dve.wait_ge(n0_deg, 2)
            dve.reciprocal(dsc[:, :], dtmp[:, :]).then_inc(n0_deg, 1)

            def means(k, s):
                deg = acc[:, 2, cols(k)]
                dve.tensor_scalar(rdeg[:, s, :], deg, 1.0, None, ALU.max).then_inc(n0_pre, 1)
                dve.wait_ge(n0_pre, k * 4 + 1)
                dve.reciprocal(rdeg[:, s, :], rdeg[:, s, :]).then_inc(n0_pre, 1)
                dve.wait_ge(n0_pre, k * 4 + 2)
                dve.tensor_tensor(ratio[:, s, :], deg, rdeg[:, s, :], ALU.mult).then_inc(n0_pre, 1)
                dve.wait_ge(n0_pre, k * 4 + 3)
                dve.tensor_scalar(deg, rdeg[:, s, :], 1.0, None, ALU.mult).then_inc(n0_pre, 1)
                if later(k, 2):
                    dve.wait_ge(n0_agg, k - 1)
                for c in range(2):
                    ins = dve.tensor_tensor(mean[:, s, c * CH:(c + 1) * CH], acc[:, c, cols(k)], rdeg[:, s, :], ALU.mult)
                ins.then_inc(n0_mean, 1)

            def body(k, s, last):
                dve.wait_ge(n0_agg, k + 1)
                if later(k, 2):
                    dve.wait_ge(n0_hid, k - 1)
                for sub in range(2):
                    half = slice(sub * SUB, (sub + 1) * SUB)
                    dve.scalar_tensor_tensor(aggT[:, s, half], ratio[:, s, half], bias[:, B1B:B1B + 1], bank[sub][:, 0:SUB],
                                             ALU.mult, ALU.add).then_inc(n0_aggT, 1)
                if not last:
                    means(k + 1, 1 - s)
                dve.wait_ge(n0_out, k + 1)
                add_x(dve, k, s, 6, 7, n0_sum)
                dve.wait_ge(n0_sum, k * 2 + 2)
                dve.tensor_tensor(tsum[:, s, :, :], tsum[:, s, :, :], b2b_row[:, :].unsqueeze(1).broadcast_to([P, CT, F]),
                                  ALU.add).then_inc(n0_bias, 1)
                dve.wait_ge(n0_bias, k + 1)
                norm_stats(dve, n0_step, k, s)
                norm_apply(dve, n0_step, n0_root, k, s, x_row(k))
            means(0, 0)
            chunks(dve, body)

        r1_row, r1_turn, r1_xT, r1_mm, r1_relu = (sem(f"r1_{x}") for x in ("row", "turn", "xT", "mm", "relu"))

        def side1_pe(pe):
            def body(k, s, last):
                pe.wait_ge(r1_row, k + 1)
                if later(k, 1):
                    pe.wait_ge(r1_xT, k * 2)
                turn(pe, lambda t: rows[:, s, t, :], 0, 1).then_inc(r1_turn, 1)
                pe.wait_ge(r1_xT, k * 2 + 2)
                if later(k, 1):
                    pe.wait_ge(r1_relu, k * 2)
                for sub in range(2):
                    mm = pe.matmul(bank[2 + sub][:, 0:SUB], w_res[:, :], xT[:, s, sub * SUB:(sub + 1) * SUB], start=True, stop=True)
                mm.then_inc(r1_mm, 1)
            chunks(pe, body)

        def side1_act(act):
            act.wait_ge(n0_step, CHUNKS * 4)
            for sems_ in table_stored[1]:
                act.wait_ge(sems_, STORED)
                act.sem_inc(gate, 1)

            def body(k, s, last):
                if later(k, 2):
                    act.wait_ge(r1_turn, k - 1)
                    act.sem_inc(gate, 1)
                act.activation(rows[:, s, :, :], X[:, bass.ds(k * CT, CT), :], ACT.Copy).then_inc(r1_row, 1)
                act.wait_ge(r1_turn, k + 1)
                if later(k, 2):
                    act.wait_ge(r1_mm, k - 1)
                for t0, n, b in two_banks(0, 1):
                    act.activation(xT[:, s, t0 * P:(t0 + n) * P], b, ACT.Copy).then_inc(r1_xT, 1)
                act.wait_ge(r1_mm, k + 1)
                act.sem_inc(gate, 1)
                for sub in range(2):
                    act.activation(rest[:, cols(k, sub)], bank[2 + sub][:, 0:SUB], ACT.Relu,
                                   bias=bias[:, GBR:GBR + 1]).then_inc(r1_relu, 1)
            chunks(act, body)

        (n1_rs, n1_mean, n1_mm, n1_relu, n1_y, n1_bn, n1_c, n1_u, n1_turn, n1_sum, n1_step, n1_root, n1_one) = (
            sem(f"n1_{x}") for x in ("rs", "mean", "mm", "relu", "y", "bn", "c", "u", "turn", "sum", "step", "root", "one"))

        def node1_pool(pool):
            clear_sums(pool, 1, n1_mean)

        def node1_act(act):
            act.wait_ge(pass_done[1], 1)
            act.preload_act_table(ACT.Sqrt)

            def body(k, s, last):
                if later(k, 2):
                    act.wait_ge(n1_mean, k - 1)
                    act.sem_inc(gate, 1)
                act.activation(rdeg[:, s, :], acc[:, 2, cols(k)], ACT.Sqrt).then_inc(n1_rs, 1)
                if later(k, 1):
                    after(k - 1, 1 - s)
                if last:
                    after(k, s)

            def after(k, s):
                act.wait_ge(n1_mm, k + 1)
                if later(k, 2):
                    act.wait_ge(n1_y, k - 1)
                for sub in range(2):
                    ins = act.activation(aggT[:, s, sub * SUB:(sub + 1) * SUB], bank[2 * s + sub][:, 0:SUB], ACT.Relu,
                                         bias=bias[:, GB:GB + 1])
                ins.then_inc(n1_relu, 1)
            chunks(act, body)
            act.wait_ge(n1_bn, 2)
            act.activation(junk, rest[:, 0:N], ACT.Square, bias=stat[:, NMEAN:NMEAN + 1],
                           accum_out=stat[:, SSQ:SSQ + 1]).then_inc(n1_one, 1)
            act.wait_ge(n1_bn, 3)
            act.activation(stat[:, STDB:STDB + 1], stat[:, VAR:VAR + 1], ACT.Sqrt).then_inc(n1_one, 1)

            def root(k, s, last):
                norm_root(act, n1_step, n1_root, k, s)
            chunks(act, root)

        def node1_pe(pe):
            pe.wait_ge(pass_done[1], 1)

            def body(k, s, last):
                pe.wait_ge(n1_mean, k + 1)
                if later(k, 2):
                    pe.wait_ge(n1_relu, k - 1)
                for sub in range(2):
                    mm = pe.matmul(bank[2 * s + sub][:, 0:SUB], w_gcn[:, :], mean[:, s, sub * SUB:(sub + 1) * SUB],
                                   start=True, stop=True)
                mm.then_inc(n1_mm, 1)
            chunks(pe, body)

            def back(k, s, last):
                pe.wait_ge(n1_u, k + 1)
                if later(k, 2):
                    pe.wait_ge(n1_sum, k * 2 - 2)
                turn(pe, xT_tile(s), 4 + 2 * s, 5 + 2 * s).then_inc(n1_turn, 1)
            chunks(pe, back)

        def node1_dve(dve):
            def scaled(k, s):
                dve.wait_ge(n1_rs, k + 1)
                if later(k, 2):
                    dve.wait_ge(n1_mm, k - 1)
                dve.tensor_tensor(mean[:, s, 0:CH], acc[:, 0, cols(k)], rdeg[:, s, :], ALU.mult).then_inc(n1_mean, 1)

            def body(k, s, last):
                if not last:
                    scaled(k + 1, 1 - s)
                dve.wait_ge(n1_relu, k + 1)
                dve.tensor_tensor(rest[:, cols(k)], rest[:, cols(k)], aggT[:, s, :], ALU.add).then_inc(n1_y, 1)
            dve.wait_ge(r1_relu, CHUNKS * 2)
            scaled(0, 0)
            chunks(dve, body)
            dve.wait_ge(n1_y, CHUNKS)
            dve.tensor_reduce(stat[:, VAR:VAR + 1], rest[:, 0:N], AX_X, ALU.add).then_inc(n1_bn, 1)
            dve.wait_ge(n1_bn, 1)
            dve.tensor_scalar(stat[:, NMEAN:NMEAN + 1], stat[:, VAR:VAR + 1], -1.0 / N, None, ALU.mult).then_inc(n1_bn, 1)
            dve.wait_ge(n1_one, 1)
            dve.tensor_scalar(stat[:, VAR:VAR + 1], stat[:, SSQ:SSQ + 1], 1.0 / N, EPS, ALU.mult, ALU.add).then_inc(n1_bn, 1)
            dve.wait_ge(n1_one, 2)
            dve.reciprocal(stat[:, RSTD:RSTD + 1], stat[:, STDB:STDB + 1]).then_inc(n1_bn, 1)
            dve.wait_ge(n1_bn, 4)
            dve.tensor_tensor(stat[:, SCALE:SCALE + 1], stat[:, RSTD:RSTD + 1], bias[:, GAMMA:GAMMA + 1],
                              ALU.mult).then_inc(n1_bn, 1)

            def centred(k, s):
                if later(k, 2):
                    dve.wait_ge(n1_turn, k - 1)
                dve.tensor_scalar(xT[:, s, :], rest[:, cols(k)], stat[:, NMEAN:NMEAN + 1], stat[:, SCALE:SCALE + 1],
                                  ALU.add, ALU.mult).then_inc(n1_c, 1)
                dve.wait_ge(n1_c, k + 1)
                dve.tensor_scalar(xT[:, s, :], xT[:, s, :], bias[:, BETA:BETA + 1], None, ALU.add).then_inc(n1_u, 1)

            def norm(k, s, last):
                if not last:
                    centred(k + 1, 1 - s)
                dve.wait_ge(n1_turn, k + 1)
                add_x(dve, k, s, 4 + 2 * s, 5 + 2 * s, n1_sum)
                dve.wait_ge(n1_sum, k * 2 + 2)
                norm_stats(dve, n1_step, k, s)
                norm_apply(dve, n1_step, n1_root, k, s, x_row(k))
            dve.wait_ge(n1_bn, 5)
            centred(0, 0)
            chunks(dve, norm)

        def node1_sp(sp):
            def store(k, s, last):
                sp.wait_ge(n1_step, k * 4 + 4)
                sp.sem_inc(gate, 1)
                sp.dma_start(node_rows(tables[2], k), X[:, bass.ds(k * CT, CT), :]).then_inc(table_stored[2][s], 16)
            chunks(sp, store)

        BY_ACT, BY_DVE = (0, 2), (1, 3, 4)

        class Rel:
            def __init__(self, name):
                self.xT, self.root_mm, self.root, self.mm, self.by_act, self.by_dve = (
                    sem(f"{name}_{x}") for x in ("xT", "root_mm", "root", "mm", "by_act", "by_dve"))

        rel1, rel2 = Rel("rel1"), Rel("rel2")

        def rel_pe(pe, i, rel, k, s, parts):
            pe.wait_ge(rel.xT, k * parts + parts)
            for sub in range(2):
                mm = pe.matmul(bank[sub][:, 0:SUB], w_root[i][:, :], xT[:, s, sub * SUB:(sub + 1) * SUB], start=True, stop=True)
            mm.then_inc(rel.root_mm, 1)
            for t in range(CT):
                if later(k, 1):
                    if t in BY_ACT:
                        pe.wait_ge(rel.by_act, (k - 1) * len(BY_ACT) + BY_ACT.index(t) + 1)
                    else:
                        pe.wait_ge(rel.by_dve, (k - 1) * len(BY_DVE) + BY_DVE.index(t) + 1)
                pe.matmul(bank[3 + t][:, :], xT[:, s, t * P:(t + 1) * P], w_rel[i][:, :, :].rearrange("p r f -> p (r f)"),
                          start=True, stop=True).then_inc(rel.mm, 1)

        def rel_act(act, p, i, rel, k, s):
            act.wait_ge(rel.root_mm, k + 1)
            act.sem_inc(gate, 1)
            for sub in range(2):
                act.activation(rest[:, cols(k, sub)], bank[sub][:, 0:SUB], ACT.Identity,
                               bias=bias[:, RB1 + i:RB1 + i + 1]).then_inc(rel.root, 1)
            if later(k, 2):
                act.wait_ge(table_stored[p][s], (k - s) * 8)
            for t in BY_ACT:
                act.wait_ge(rel.mm, k * CT + t + 1)
                act.activation(rel_rows[:, s, t, :], bank[3 + t][:, :], ACT.Copy).then_inc(rel.by_act, 1)

        def rel_dve(dve, p, rel, k, s):
            if later(k, 2):
                dve.wait_ge(table_stored[p][s], (k - s) * 8)
                dve.sem_inc(gate, 1)
            for t in BY_DVE:
                dve.wait_ge(rel.mm, k * CT + t + 1)
                dve.tensor_copy(rel_rows[:, s, t, :], bank[3 + t][:, :]).then_inc(rel.by_dve, 1)

        def rel_sp(sp, p, rel):
            def store(k, s, last):
                sp.wait_ge(rel.by_act, (k + 1) * len(BY_ACT))
                sp.sem_inc(gate, 1)
                sp.wait_ge(rel.by_dve, (k + 1) * len(BY_DVE))
                sp.sem_inc(gate, 1)
                sp.dma_start(node_rows(tables[p].rearrange("(n r) f -> n (r f)", r=RELS), k),
                             rel_rows[:, s, :, :]).then_inc(table_stored[p][s], 16)
            chunks(sp, store)

        (n2_mean, n2_mm, n2_min, n2_relu, n2_exp, n2_u, n2_turn, n2_sum, n2_bn, n2_mv, n2_std, n2_row, n2_turn2, n2_kept) = (
            sem(f"n2_{x}") for x in ("mean", "mm", "min", "relu", "exp", "u", "turn", "sum", "bn", "mv", "std", "row", "turn2",
                                     "kept"))

        def node2_pe(pe):
            pe.wait_ge(pass_done[2], 1)

            def product(k, s):
                pe.wait_ge(n2_mean, k + 1)
                if later(k, 2):
                    pe.wait_ge(n2_relu, k - 1)
                    pe.wait_ge(n2_min, (k - 1) * 2)
                for sub in range(2):
                    mm = pe.matmul(bank[2 * s + sub][:, 0:SUB], w_mean[:, :], mean[:, s, sub * SUB:(sub + 1) * SUB],
                                   start=True, stop=True)
                mm.then_inc(n2_mm, 1)

            def body(k, s, last):
                if not last:
                    product(k + 1, 1 - s)
                pe.wait_ge(n2_u, k + 1)
                if later(k, 2):
                    pe.wait_ge(n2_sum, k * 2 - 2)
                turn(pe, xT_tile(s), 4 + 2 * s, 5 + 2 * s).then_inc(n2_turn, 1)
            product(0, 0)
            chunks(pe, body)

            def relations(k, s, last):
                pe.wait_ge(n2_row, k + 1)
                if later(k, 1):
                    pe.wait_ge(rel1.root, k * 2)
                else:
                    pe.wait_ge(n2_sum, CHUNKS * 2)
                turn(pe, lambda t: rows[:, s, t, :], 0, 1).then_inc(n2_turn2, 1)
                rel_pe(pe, 0, rel1, k, s, 2)
            chunks(pe, relations)

        def node2_act(act):
            act.wait_ge(pass_done[2], 1)
            act.preload_act_table(ACT.Exp)

            def body(k, s, last):
                act.wait_ge(n2_min, k * 2 + 2)
                if later(k, 2):
                    act.wait_ge(n2_u, k - 1)
                for sub in range(2):
                    ins = act.activation(aggT[:, s, sub * SUB:(sub + 1) * SUB], bank[2 * s + sub][:, 0:SUB], ACT.Relu,
                                         bias=bias[:, MB:MB + 1])
                ins.then_inc(n2_relu, 1)
                act.activation(h2T[:, s, CH:2 * CH], h2T[:, s, 0:CH], ACT.Exp).then_inc(n2_exp, 1)
            chunks(act, body)
            act.wait_ge(n2_mv, CHUNKS)
            act.activation(std[:, :], mv[:, :, 1], ACT.Sqrt, bias=stat[:, EPSC:EPSC + 1]).then_inc(n2_std, 1)

            def relations(k, s, last):
                act.wait_ge(n2_turn2, k + 1)
                if later(k, 2):
                    act.wait_ge(rel1.mm, (k - 1) * CT)
                for t0, n, b in two_banks(0, 1):
                    act.activation(xT[:, s, t0 * P:(t0 + n) * P], b, ACT.Copy).then_inc(rel1.xT, 1)
                rel_act(act, 3, 0, rel1, k, s)
            chunks(act, relations)

        def node2_dve(dve):
            def means(k, s):
                if later(k, 2):
                    dve.wait_ge(n2_mm, k - 1)
                dve.tensor_tensor(mean[:, s, 0:CH], acc[:, 0, cols(k)], acc[:, 2, cols(k)], ALU.mult).then_inc(n2_mean, 1)

            def tail(k, s):
                dve.wait_ge(n2_turn, k + 1)
                for t0, n, b in two_banks(4 + 2 * s, 5 + 2 * s):
                    x_ = X[:, bass.ds(k * CT + t0, n), :]
                    dve.tensor_tensor(x_, b.rearrange("p (t f) -> p t f", f=F), x_, ALU.add).then_inc(n2_sum, 1)
                dve.wait_ge(n2_sum, k * 2 + 2)
                dve.sem_inc(gate, 1)
                for j in range(CT):
                    ins = dve.bn_stats(bn[:, s, j, :], x_row(k)(j))
                ins.then_inc(n2_bn, 1)
                dve.wait_ge(n2_bn, k * 2 + 1)
                dve.sem_inc(gate, 1)
                for j in range(CT):
                    ins = dve.bn_aggr(mv_slot[:, s, j, :], bn[:, s, j, :])
                ins.then_inc(n2_bn, 1)
                dve.wait_ge(n2_bn, k * 2 + 2)
                dve.tensor_scalar(mv[:, bass.ds(k * CT, CT), :], mv_slot[:, s, :, :], 1.0, None, ALU.mult).then_inc(n2_mv, 1)

            def body(k, s, last):
                dve.wait_ge(n2_mm, k + 1)
                if later(k, 2):
                    dve.wait_ge(n2_exp, k - 1)
                for sub in range(2):
                    dve.tensor_scalar(h2T[:, s, sub * SUB:(sub + 1) * SUB], bank[2 * s + sub][:, 0:SUB], bias[:, MB:MB + 1], 0.0,
                                      ALU.add, ALU.min).then_inc(n2_min, 1)
                if not last:
                    means(k + 1, 1 - s)
                dve.wait_ge(n2_exp, k + 1)
                if later(k, 2):
                    dve.wait_ge(n2_turn, k - 1)
                dve.scalar_tensor_tensor(xT[:, s, :], h2T[:, s, CH:2 * CH], -1.0, aggT[:, s, :], ALU.add,
                                         ALU.add).then_inc(n2_u, 1)
                if later(k, 1):
                    tail(k - 1, 1 - s)
                if last:
                    tail(k, s)
            means(0, 0)
            chunks(dve, body)
            dve.wait_ge(n2_std, 1)
            dve.reciprocal(rstd[:, :], std[:, :]).then_inc(n2_std, 1)
            dve.wait_ge(n2_std, 2)

            def applied(k, s):
                if later(k, 2):
                    dve.wait_ge(n2_turn2, k - 1)
                    dve.wait_ge(n2_kept, k - 1)
                    dve.sem_inc(gate, 1)
                for j in range(CT):
                    t = bass.ds(k * CT + j, 1)
                    ins = dve.tensor_scalar(rows[:, s, j, :], x_row(k)(j), mv[:, t, 0:1].rearrange("p o c -> p (o c)"), rstd[:, t],
                                            ALU.subtract, ALU.mult)
                ins.then_inc(n2_row, 1)

            def relations(k, s, last):
                if not last:
                    applied(k + 1, 1 - s)
                rel_dve(dve, 3, rel1, k, s)
            applied(0, 0)
            chunks(dve, relations)

        def node2_pool(pool):
            clear_sums(pool, 2, n2_mean)

            def keep(k, s, last):
                pool.wait_ge(n2_row, k + 1)
                pool.sem_inc(gate, 1)
                pool.tensor_copy(X[:, bass.ds(k * CT, CT), :], rows[:, s, :, :]).then_inc(n2_kept, 1)
            chunks(pool, keep)

        n3_sum = sem("n3_sum")

        def node3_dve(dve):
            def summed(k, s):
                if later(k, 2):
                    dve.wait_ge(rel2.xT, k - 1)
                dve.tensor_tensor(h2T[:, s, 0:CH], acc[:, 0, cols(k)], rest[:, cols(k)], ALU.add).then_inc(n3_sum, 1)

            def body(k, s, last):
                if not last:
                    summed(k + 1, 1 - s)
                rel_dve(dve, 4, rel2, k, s)
            summed(0, 0)
            chunks(dve, body)

        def node3_act(act):
            act.wait_ge(pass_done[3], 1)

            def body(k, s, last):
                act.wait_ge(n3_sum, k + 1)
                if later(k, 2):
                    act.wait_ge(rel2.mm, (k - 1) * CT)
                act.activation(xT[:, s, :], h2T[:, s, 0:CH], ACT.Relu).then_inc(rel2.xT, 1)
                rel_act(act, 4, 1, rel2, k, s)
            chunks(act, body)

        def node3_pe(pe):
            pe.wait_ge(pass_done[3], 1)

            def body(k, s, last):
                if later(k, 1):
                    pe.wait_ge(rel2.root, k * 2)
                rel_pe(pe, 1, rel2, k, s, 1)
            chunks(pe, body)

        def node3_pool(pool):
            clear_sums(pool, 3, n3_sum)

        n4_u, n4_turn, n4_sum, n4_step, n4_root = (sem(f"n4_{x}") for x in ("u", "turn", "sum", "step", "root"))
        out_stored = sems("out_stored", 2)

        def node4_dve(dve):
            def summed(k, s):
                if later(k, 2):
                    dve.wait_ge(n4_turn, k - 1)
                dve.tensor_tensor(xT[:, s, :], acc[:, 0, cols(k)], rest[:, cols(k)], ALU.add).then_inc(n4_u, 1)

            def body(k, s, last):
                if not last:
                    summed(k + 1, 1 - s)
                dve.wait_ge(n4_turn, k + 1)
                add_x(dve, k, s, 2 * s, 2 * s + 1, n4_sum)
                dve.wait_ge(n4_sum, k * 2 + 2)
                norm_stats(dve, n4_step, k, s)
                if later(k, 2):
                    dve.wait_ge(out_stored[s], (k - s) * 8)
                    dve.sem_inc(gate, 1)
                norm_apply(dve, n4_step, n4_root, k, s, lambda j: rows[:, s, j, :])
            summed(0, 0)
            chunks(dve, body)

        def node4_pe(pe):
            def body(k, s, last):
                pe.wait_ge(n4_u, k + 1)
                if later(k, 2):
                    pe.wait_ge(n4_sum, k * 2 - 2)
                turn(pe, xT_tile(s), 2 * s, 2 * s + 1).then_inc(n4_turn, 1)
            chunks(pe, body)

        def node4_act(act):
            act.preload_act_table(ACT.Sqrt)

            def body(k, s, last):
                norm_root(act, n4_step, n4_root, k, s)
            chunks(act, body)

        def node4_sp(sp):
            def store(k, s, last):
                sp.wait_ge(n4_step, k * 4 + 4)
                sp.sem_inc(gate, 1)
                sp.dma_start(node_rows(out, k), rows[:, s, :, :]).then_inc(out_stored[s], 16)
            chunks(sp, store)
            for s in out_stored:
                sp.wait_ge(s, STORED)

        @block.sync
        def _(sp):
            start_sp(sp)
            rounds = load_rounds(sp)
            pass0_sp(sp, rounds)
            node0_sp(sp)
            node1_sp(sp)
            rel_sp(sp, 3, rel1)
            rel_sp(sp, 4, rel2)
            node4_sp(sp)

        @block.gpsimd
        def _(pool):
            start_pool(pool)
            rounds = load_rounds(pool)
            pass_pool(pool, 0, rounds)
            node0_pool(pool)
            pass_pool(pool, 1, rounds)
            node1_pool(pool)
            pass_pool(pool, 2, rounds)
            node2_pool(pool)
            pass_pool(pool, 3, rounds)
            node3_pool(pool)
            pass_pool(pool, 4, rounds)

        @block.scalar
        def _(act):
            start_act_loads(act)
            start_act_store(act)
            rounds = load_rounds(act)
            pass0_act(act, rounds)
            node0_act(act)
            pass_act_first(act, 1, rounds)
            side1_act(act)
            pass_act(act, 1, rounds)
            node1_act(act)
            pass_act_first(act, 2, rounds)
            pass_act(act, 2, rounds)
            node2_act(act)
            pass_act_first(act, 3, rounds)
            pass_act(act, 3, rounds)
            node3_act(act)
            pass_act_first(act, 4, rounds)
            pass_act(act, 4, rounds)
            node4_act(act)

        @block.tensor
        def _(pe):
            start_pe(pe)
            rounds = load_rounds(pe)
            pass_pe(pe, 0, rounds)
            node0_pe(pe)
            side1_pe(pe)
            pass_pe(pe, 1, rounds)
            node1_pe(pe)
            pass_pe(pe, 2, rounds)
            node2_pe(pe)
            pass_pe(pe, 3, rounds)
            node3_pe(pe)
            pass_pe(pe, 4, rounds)
            node4_pe(pe)

        @block.vector
        def _(dve):
            start_dve_rows(dve)
            start_dve(dve)
            rounds = load_rounds(dve)
            pass_dve(dve, 0, rounds)
            node0_dve(dve)
            pass_dve(dve, 1, rounds)
            node1_dve(dve)
            pass_dve(dve, 2, rounds)
            node2_dve(dve)
            pass_dve(dve, 3, rounds)
            node3_dve(dve)
            pass_dve(dve, 4, rounds)
            node4_dve(dve)


def kernel(x, src, dst, edge_attr_128, edge_type_4, edge_weight, **w):
    import concourse.bacc as bacc
    from concourse.bass_utils import run_bass_kernel_spmd

    def tiles(a, mode, **kw):
        return np.pad(np.asarray(a), (0, EP - E), mode, **kw).reshape(TILES, P).T

    x = np.pad(np.asarray(x), ((0, NP - N), (0, 0)))
    src_tiles = tiles(src, "constant", constant_values=N)
    dst_pad = np.pad(np.asarray(dst), (0, EP - E), "constant", constant_values=N)
    w = {k: np.asarray(v) for k, v in w.items()}
    arrays = {
        "x_rows": x,
        "x_cols": x.T,
        "src": np.concatenate([src_tiles, src_tiles[:, :SLOTS * U]], 1),
        "dst": dst_pad.reshape(TILES, P).T,
        "first": dst_pad[::GE],
        "etype": tiles(edge_type_4, "constant"),
        "eweight": tiles(edge_weight, "edge"),
        "ea_cols": np.pad(np.asarray(edge_attr_128), ((0, EP - E), (0, 0))).T,
        "u0": w["L0_gnn_u"][0],
        "W1a": w["L0_gnn_W1a"], "b1a": w["L0_gnn_b1a"], "W1b": w["L0_gnn_W1b"], "b1b": w["L0_gnn_b1b"],
        "W2a": w["L0_gnn_W2a"], "b2a": w["L0_gnn_b2a"], "W2b": w["L0_gnn_W2b"], "b2b": w["L0_gnn_b2b"],
        "gW": w["L1_gnn_W"], "gb": w["L1_gnn_b"], "gWr": w["L1_gnn_Wr"], "gbr": w["L1_gnn_br"],
        "gamma": w["L1_gnn_gamma"], "beta": w["L1_gnn_beta"], "mW": w["L2_gnn_W"], "mb": w["L2_gnn_b"],
        "rW1": w["L3_gnn_W1"], "rroot1": w["L3_gnn_root1"], "rb1": w["L3_gnn_b1"],
        "rW2": w["L3_gnn_W2"], "rroot2": w["L3_gnn_root2"], "rb2": w["L3_gnn_b2"],
    }
    arrays = {name: np.ascontiguousarray(a) for name, a in arrays.items()}
    nc = bacc.Bacc("TRN2", target_bir_lowering=False, num_devices=1)
    args = {name: nc.dram_tensor(name, a.shape, mybir.dt.from_np(a.dtype), kind="ExternalInput").ap()
            for name, a in arrays.items()}
    out = nc.dram_tensor("out", (NP, F), F32, kind="ExternalOutput").ap()
    gnn(nc, out=out, **args)
    r = run_bass_kernel_spmd(nc, [arrays], core_ids=[0])
    return r.results[0]["out"][:N]
```

```python
from contextlib import ExitStack

import numpy as np

import concourse.bass as bass
from concourse import mybir

P = 128
N = 6250
E = 106250
F = 128
HID = 256
RELS = 4
U = 4
GE = U * P
SLOTS0 = 4
SLOTS = 8
HOTS = 4
ITERS = -(-E // (GE * SLOTS))
GROUPS = ITERS * SLOTS
ITERS0 = GROUPS // SLOTS0
TILES = GROUPS * U
EP = TILES * P
WIN = 64
WINDOWS = -(-N // WIN)
LAG = 2
CT = 5
CH = CT * P
CHUNKS = -(-N // (2 * CH)) * 2
NP = CHUNKS * CH
NT = NP // P
SUB = CH // 2
BT = 2
BLK = BT * P
BLKS = NP // BLK
LAST = N - (BLKS - 1) * BLK
ACC = NP + WIN
PRIME_SLOT = HOTS
PRIME_BANK = 2
PRIME_PAIR = 4
EPS = 1e-5

F32 = mybir.dt.float32
BF16 = mybir.dt.bfloat16
I32 = mybir.dt.int32
U32 = mybir.dt.uint32
ALU = mybir.AluOpType
ACT = mybir.ActivationFunctionType
AX_X = mybir.AxisListType.X


def gnn(nc, x_rows, x_cols, src, dst, first, etype, eweight, ea_cols, u0, W1a, b1a, W1b, b1b, W2a, b2a, W2b, b2b,
        gW, gb, gWr, gbr, gamma, beta, mW, mb, rW1, rroot1, rb1, rW2, rroot2, rb2, out):
    with ExitStack() as ctx:
        def sb(name, shape, dt=F32):
            return ctx.enter_context(nc.sbuf_tensor(name, shape, dt))

        def sem(name):
            return ctx.enter_context(nc.semaphore(name))

        def sems(name, n):
            return [sem(f"{name}{i}") for i in range(n)]

        tables = [nc.dram_tensor("table_pre", [NP, HID], F32).ap(),
                  nc.dram_tensor("table_gcn", [NP, F], F32).ap(),
                  nc.dram_tensor("table_mean", [NP, F], F32).ap(),
                  nc.dram_tensor("table_rel1", [NP * RELS, F], F32).ap(),
                  nc.dram_tensor("table_rel2", [NP * RELS, F], F32).ap()]

        ends_row = nc.dram_tensor("ends_row", [BLKS, 1], I32).ap()

        acc = sb("acc", [P, 3, ACC])
        rest = acc[:, 1, 0:NP]
        X = sb("X", [P, NT, F])
        srci = sb("srci", [P, TILES + SLOTS * U], I32)
        reli = sb("reli", [P, TILES + SLOTS * U], I32)
        dstf = sb("dstf", [P, TILES])
        local = sb("local", [P, TILES])
        src_lo = sb("src_lo", [P, TILES])
        src_hi = sb("src_hi", [P, TILES])
        ew = sb("ew", [P, TILES])
        firstf = sb("firstf", [P, GROUPS])
        base = sb("base", [P, GROUPS])
        basei = sb("basei", [1, GROUPS + SLOTS0], I32)
        until = sb("until", [P, 2], I32)
        ends = sb("ends", [1, BLKS + 1], I32)
        slot_idx = sb("slot_idx", [P, SLOTS, U], I32)
        ident = sb("ident", [P, P])
        iota = sb("iota", [P, P])
        iota_b = sb("iota_b", [P, P], BF16)
        ones_b = sb("ones_b", [P, P], BF16)
        zeros_b = sb("zeros_b", [P, P], BF16)
        w1a = sb("w1a", [P, 2, HID])
        w1b = sb("w1b", [P, 2, F])
        w2a = sb("w2a", [P, 3, HID])
        w2b = sb("w2b", [P, 2, F])
        w_gcn = sb("w_gcn", [P, F])
        w_res = sb("w_res", [P, F])
        w_mean = sb("w_mean", [P, F])
        w_rel = [sb("w_rel1", [P, RELS, F]), sb("w_rel2", [P, RELS, F])]
        w_root = [sb("w_root1", [P, F]), sb("w_root2", [P, F])]
        bias = sb("bias", [P, 16])
        B1B, B2A0, B2A1, GB, GBR, GAMMA, BETA, MB, RB1, RB2, U0 = range(11)
        b1a_row = sb("b1a_row", [P, HID])
        b2b_row = sb("b2b_row", [P, F])
        c2 = sb("c2", [P, 2])
        stat = sb("stat", [P, 32])
        MINL, MAXL, SLOW, FAST, STEP, WOFF, EPSC, NMEAN, SSQ, VAR, RSTD, SCALE, SHIFT, WMIN, WMAX, WNEG, RNDS, STDB, WMAXP, WNEGP, SLOWG, UNTIL = range(22)
        roundsi = sb("roundsi", [1, 2], I32)
        dsc = sb("dsc", [P, NT])
        dtmp = sb("dtmp", [P, NT])
        bn = sb("bn", [P, 2, CT, 6])
        mv = sb("mv", [P, 2, CT, 2])
        std = sb("std", [P, 2, CT])
        bn_row = sb("bn_row", [P, NT, 6])
        bn_y = sb("bn_y", [P, BLKS, 6])
        mv_y = sb("mv_y", [P, 2])
        bound = sb("bound", [P, 1])
        count = sb("count", [P, GROUPS])
        rstd = sb("rstd", [P, 2, CT])
        row_mean, row_half, row_var, row_std, row_rstd, row_shift = (
            sb(f"row_{x}", [P, NT]) for x in ("mean", "half", "var", "std", "rstd", "shift"))

        work = sb("work", [P, 12800])

        def view(at, *shape):
            size = int(np.prod(shape))
            names = "abc"[:len(shape)]
            return work[:, at:at + size].rearrange(
                f"p ({' '.join(names)}) -> p {' '.join(names)}", **dict(zip(names, shape)))

        gat0 = view(0, SLOTS0, U, HID)
        hid = view(4096, SLOTS0, U * HID)
        ea = view(8192, SLOTS0, GE)
        hot = view(10240, HOTS, U * WIN)
        hot_lo = work[:, 11264:12288].bitcast(BF16).rearrange("p (s u w) -> p s u w", s=HOTS, u=U)
        hot_hi = work[:, 12288:12288 + HOTS * U * NT // 2].bitcast(BF16).rearrange("p (s u w) -> p s u w", s=HOTS, u=U)
        gat = view(0, SLOTS, U, F)
        b_rows = view(4096, BT, F)
        b_xT = view(4352, BLK)
        b_u = view(4608, BLK)
        b_v = view(4864, BLK)
        b_w = view(5120, BLK)
        b_mean = view(5376, BLK)
        b_sum = view(5632, BT, F)
        b_rel = view(5888, BT, RELS * F)
        b_bn = view(6912, 2, BLK)
        aggT = view(3840, 2, CH)
        xT = view(5120, 2, CH)
        h2T = view(6400, 2, 2 * CH)
        xT0 = view(11264, 2, CH)
        pre_rows = view(4096, 2, CT, HID)
        xb = view(8960, 2, CH)
        tsum = view(10240, 2, CT, F)
        rows = view(11520, 2, CT, F)
        ratio = view(8960, 2, CH)
        staging_a = work[:, 0:TILES].bitcast(I32)
        staging_b = work[:, 1024:1024 + TILES].bitcast(I32)
        staging_c = work[:, 2048:2048 + GROUPS].bitcast(I32)
        staging_d = work[:, 3072:3072 + TILES].bitcast(I32)
        staging_e = work[:, 10240:10240 + TILES]
        staging_f = work[:, 11072:11072 + GROUPS]

        bank = [ctx.enter_context(nc.psum_tensor(f"bank{i}", [P, 512], F32)) for i in range(8)]
        HIST = 6

        s_idx, s_param, s_weight = sem("s_idx"), sem("s_param"), sem("s_weight")
        s_const, s_ident, s_prep, s_vote, s_all = sem("s_const"), sem("s_ident"), sem("s_prep"), sem("s_vote"), sem("s_all")
        s_x = sem("s_x")
        s_rounds, s_until, s_ends, s_ends_row = sem("s_rounds"), sem("s_until"), sem("s_ends"), sem("s_ends_row")
        gate = sem("gate")
        idx_ready = sems("idx_ready", 5)
        gathered = [sems(f"gathered{p}_", SLOTS if p else SLOTS0) for p in range(5)]
        hot_ready, seg_done, accumulated = sems("hot_ready", 5), sems("seg_done", 5), sems("accumulated", 5)
        setup_step = sems("setup_step", 5)
        pass_done, acc_zero, cleared = sem("pass_done"), sem("acc_zero"), sem("cleared")
        table_stored = [sems(f"table{p}_stored", 2 if p < 2 else 1) for p in range(5)]
        STORED = [16 * CHUNKS // 2] * 2 + [16 * BLKS] * 3
        ea_ready = sems("ea_ready", SLOTS0)
        pre_done, pre_added, relu_done = sem("pre_done"), sem("pre_added"), sem("relu_done")
        block = ctx.enter_context(nc.Block())

        def chunks(eng, body):
            body(0, 0, False)
            body(1, 1, False)
            with eng.Fori(1, CHUNKS // 2 - 1) as it:
                body(it * 2, 0, False)
                body(it * 2 + 1, 1, False)
            body(CHUNKS - 2, 0, False)
            body(CHUNKS - 1, 1, True)

        def blocks(eng, body):
            body(0, False)
            with eng.Fori(1, BLKS - 1) as k:
                body(k, False)
            body(BLKS - 1, True)

        def pairs(eng, body):
            body(0, 0, False)
            body(1, 1, False)
            with eng.Fori(1, BLKS // 2) as it:
                body(it * 2, 0, False)
                body(it * 2 + 1, 1, False)
            body(BLKS - 1, 0, True)

        def bcols(k):
            return bass.ds(k * BLK, BLK)

        def X_rows(k):
            return X[:, bass.ds(k * BT, BT), :]

        def later(k, n):
            return not isinstance(k, int) or k >= n

        def cols(k, sub=None):
            return bass.ds(k * CH, CH) if sub is None else bass.ds(k * CH + sub * SUB, SUB)

        def node_rows(table, k):
            return table.rearrange("(t p) c -> p t c", p=P)[:, bass.ds(k * CT, CT), :]

        def block_rows(table, k):
            return table.rearrange("(t p) c -> p t c", p=P)[:, bass.ds(k * BT, BT), :]

        xT0_ready = sems("xT0_ready", 2)
        y_done, y_added = sem("y_done"), sem("y_added")

        def start_sp(sp):
            sp.dma_start(w1a[:, :, :], W1a.rearrange("(c p) n -> p c n", p=P)).then_inc(s_weight, 16)
            sp.dma_start(b1a_row[:, :], b1a.partition_broadcast(P)).then_inc(s_weight, 16)

            def load(k, s, last):
                if later(k, 2):
                    sp.wait_ge(y_done, k - 1)
                sp.sem_inc(gate, 1)
                sp.dma_start(xT0[:, s, :], x_cols[:, cols(k)]).then_inc(xT0_ready[s], 16)
            chunks(sp, load)

        def start_act_loads(act):
            act.dma_start(staging_a, dst).then_inc(s_idx, 16)
            act.dma_start(staging_c, first.partition_broadcast(P)).then_inc(s_idx, 16)
            act.dma_start(srci[:, :], src).then_inc(s_idx, 16)
            act.dma_start(staging_b, etype).then_inc(s_idx, 16)
            act.dma_start(staging_e, eweight).then_inc(s_idx, 16)
            for c, b in ((B1B, b1b), (GB, gb), (GBR, gbr), (GAMMA, gamma), (BETA, beta), (MB, mb), (RB1, rb1), (RB2, rb2)):
                act.dma_start(bias[:, c:c + 1], b.rearrange("(f o) -> f o", o=1)).then_inc(s_param, 16)
            act.dma_start(bias[:, B2A0:B2A0 + 1], b2a[0:F].rearrange("(f o) -> f o", o=1)).then_inc(s_param, 16)
            act.dma_start(bias[:, B2A1:B2A1 + 1], b2a[F:HID].rearrange("(f o) -> f o", o=1)).then_inc(s_param, 16)
            act.dma_start(bias[:, U0:U0 + 1], u0.rearrange("(f o) -> f o", o=1)).then_inc(s_param, 16)
            act.dma_start(b2b_row[:, :], b2b.partition_broadcast(P)).then_inc(s_param, 16)
            act.dma_start(w1b[:, :, :], W1b.rearrange("(c p) n -> p c n", p=P)).then_inc(s_param, 16)
            act.dma_start(w2a[:, :, :], W2a.rearrange("(c p) n -> p c n", p=P)).then_inc(s_param, 16)
            act.dma_start(w2b[:, :, :], W2b.rearrange("(c p) n -> p c n", p=P)).then_inc(s_param, 16)
            act.dma_start(w_gcn[:, :], gW).then_inc(s_param, 16)
            act.dma_start(w_res[:, :], gWr).then_inc(s_param, 16)
            act.dma_start(w_mean[:, :], mW).then_inc(s_param, 16)
            for i, (w, r) in enumerate(((rW1, rroot1), (rW2, rroot2))):
                act.dma_start(w_rel[i][:, :, :], w.rearrange("r i o -> i r o")).then_inc(s_param, 16)
                act.dma_start(w_root[i][:, :], r).then_inc(s_param, 16)
            act.dma_start(X[:, :, :], x_rows.rearrange("(t p) f -> p t f", p=P)).then_inc(s_param, 16)
        PARAMS = 16 * 23

        def start_pe(pe):
            pe.wait_ge(s_weight, 32)

            def body(k, s, last):
                pe.wait_ge(xT0_ready[s], (k - s) * 8 + 16)
                if later(k, 1):
                    pe.wait_ge(y_added, k * 3)
                for t in range(CT):
                    mm = pe.matmul(bank[t // 2][:, t % 2 * HID:(t % 2 + 1) * HID], xT0[:, s, t * P:(t + 1) * P],
                                   w1a[:, 0, :], start=True, stop=True)
                mm.then_inc(y_done, 1)
            chunks(pe, body)

        def start_dve_rows(dve):
            dve.wait_ge(s_weight, 32)

            def body(k, s, last):
                for b in range(3):
                    n = 2 if b < 2 else 1
                    dve.wait_ge(y_done, k + 1)
                    if later(k, 2):
                        dve.wait_ge(table_stored[0][s], (k - s) * 8)
                    dve.tensor_tensor(pre_rows[:, s, 2 * b:2 * b + n, :],
                                      bank[b][:, 0:n * HID].rearrange("p (t h) -> p t h", t=n),
                                      b1a_row[:, :].unsqueeze(1).broadcast_to([P, n, HID]), ALU.add).then_inc(y_added, 1)
            chunks(dve, body)

        def start_act_store(act):
            def body(k, s, last):
                act.wait_ge(y_added, k * 3 + 3)
                act.dma_start(node_rows(tables[0], k), pre_rows[:, s, :, :]).then_inc(table_stored[0][s], 16)
            chunks(act, body)

        CONSTANTS = 10

        def start_pool(pool):
            pool.iota(staging_d[:, 0:P], pattern=[[1, P]], base=0, channel_multiplier=0).then_inc(s_const, 1)
            pool.memset(ident[:, :], 0.0).then_inc(s_const, 1)
            pool.memset(ones_b[:, :], 1.0).then_inc(s_const, 1)
            pool.memset(zeros_b[:, :], 0.0).then_inc(s_const, 1)
            pool.memset(acc[:, :, :], 0.0).then_inc(s_const, 1)
            pool.memset(stat[:, EPSC:EPSC + 1], EPS).then_inc(s_const, 1)
            pool.memset(basei[:, :], 0).then_inc(s_const, 1)
            pool.memset(ends[:, 0:1], 0).then_inc(s_const, 1)
            pool.iota(staging_d[:, P:P + GROUPS], pattern=[[1, GROUPS]], base=1, channel_multiplier=0).then_inc(s_const, 1)
            pool.iota(staging_d[:, 512:513], pattern=[[0, 1]], base=BLK, channel_multiplier=BLK).then_inc(s_const, 1)
            pool.wait_ge(s_const, 2)
            pool.affine_select(out=ident[:, :], in_=ident[:, :], compare_op=ALU.not_equal, fill=1.0, base=0,
                               pattern=[[-1, P]], channel_multiplier=1).then_inc(s_ident, 1)
            pool.wait_ge(s_vote, 3)
            RMAX = bass.bass_isa.ReduceOp.max
            pool.partition_all_reduce(stat[:, SLOW:SLOW + 1], stat[:, MAXL:MAXL + 1], P, RMAX).then_inc(s_all, 1)
            pool.partition_all_reduce(stat[:, WMAX:WMAX + 1], stat[:, WMAXP:WMAXP + 1], P, RMAX).then_inc(s_all, 1)
            pool.partition_all_reduce(stat[:, WNEG:WNEG + 1], stat[:, WNEGP:WNEGP + 1], P, RMAX).then_inc(s_all, 1)

        def start_dve(dve):
            n = [0]

            def done(ins):
                n[0] += 1
                ins.then_inc(s_prep, 1)
                dve.wait_ge(s_prep, n[0])

            dve.wait_ge(s_const, CONSTANTS)
            done(dve.tensor_copy(iota[:, :], staging_d[:, 0:P]))
            done(dve.tensor_copy(iota_b[:, :], staging_d[:, 0:P]))
            done(dve.tensor_copy(count[:, :], staging_d[:, P:P + GROUPS]))
            done(dve.tensor_copy(bound[:, :], staging_d[:, 512:513]))
            dve.wait_ge(s_idx, 80)
            done(dve.tensor_copy(dstf[:, :], staging_a))
            done(dve.tensor_copy(firstf[:, :], staging_c))
            done(dve.tensor_tensor(local[:, :].rearrange("p (g u) -> p g u", u=U),
                                   dstf[:, :].rearrange("p (g u) -> p g u", u=U),
                                   firstf[:, :].unsqueeze(2).broadcast_to([P, GROUPS, U]), ALU.subtract))
            done(dve.tensor_reduce(stat[:, MINL:MINL + 1], local[:, :], AX_X, ALU.min))
            done(dve.tensor_reduce(stat[:, MAXL:MAXL + 1], local[:, :], AX_X, ALU.max))
            done(dve.tensor_scalar(stat[:, MINL:MINL + 1], stat[:, MINL:MINL + 1], -1.0, None, ALU.mult))
            done(dve.tensor_scalar(stat[:, MAXL:MAXL + 1], stat[:, MAXL:MAXL + 1], 1.0 - WIN, stat[:, MINL:MINL + 1],
                                   ALU.add, ALU.max))
            done(dve.tensor_reduce(stat[:, WMAXP:WMAXP + 1], staging_e, AX_X, ALU.max))
            done(dve.tensor_reduce(stat[:, WMIN:WMIN + 1], staging_e, AX_X, ALU.min))
            done(dve.tensor_scalar(stat[:, WNEGP:WNEGP + 1], stat[:, WMIN:WMIN + 1], -1.0, None, ALU.mult))
            dve.sem_inc(s_vote, 3)
            done(dve.tensor_scalar(reli[:, 0:TILES], srci[:, 0:TILES], 7, None, ALU.logical_shift_right))
            done(dve.tensor_copy(src_hi[:, :], reli[:, 0:TILES]))
            done(dve.tensor_scalar(staging_d, srci[:, 0:TILES], P - 1, None, ALU.bitwise_and))
            done(dve.tensor_copy(src_lo[:, :], staging_d))
            done(dve.scalar_tensor_tensor(reli[:, 0:TILES], srci[:, 0:TILES], float(RELS), staging_b, ALU.mult, ALU.add))
            done(dve.tensor_copy(reli[:, TILES:], reli[:, 0:SLOTS * U]))
            dve.wait_ge(s_all, 3)
            done(dve.tensor_scalar(stat[:, SLOW:SLOW + 1], stat[:, SLOW:SLOW + 1], 0.0, None, ALU.is_gt))
            done(dve.tensor_scalar(stat[:, FAST:FAST + 1], stat[:, SLOW:SLOW + 1], -1.0, 1.0, ALU.mult, ALU.add))
            done(dve.tensor_scalar(stat[:, STEP:STEP + 1], stat[:, SLOW:SLOW + 1], float(WIN), None, ALU.mult))
            done(dve.tensor_scalar(stat[:, RNDS:RNDS + 1], stat[:, SLOW:SLOW + 1], float(WINDOWS - 1), 1.0, ALU.mult, ALU.add))
            done(dve.tensor_copy(roundsi[:, 0:1], stat[0:1, RNDS:RNDS + 1]))
            dve.tensor_scalar(roundsi[:, 1:2], stat[0:1, RNDS:RNDS + 1], -1.0, None, ALU.add).then_inc(s_rounds, 1)
            done(dve.scalar_tensor_tensor(staging_f, firstf[:, :], bound[:, :], count[:, :], ALU.is_lt, ALU.mult))
            done(dve.tensor_reduce(stat[:, UNTIL:UNTIL + 1], staging_f, AX_X, ALU.max))
            done(dve.tensor_scalar(stat[:, SLOWG:SLOWG + 1], stat[:, SLOW:SLOW + 1], float(GROUPS), None, ALU.mult))
            done(dve.tensor_scalar(stat[:, UNTIL:UNTIL + 1], stat[:, UNTIL:UNTIL + 1], stat[:, SLOWG:SLOWG + 1], float(SLOTS - 1),
                                   ALU.max, ALU.add))
            done(dve.tensor_copy(until[:, 0:1], stat[:, UNTIL:UNTIL + 1]))
            dve.tensor_scalar(until[:, 1:2], until[:, 0:1], SLOTS.bit_length() - 1, None,
                              ALU.logical_shift_right).then_inc(s_until, 1)
            done(dve.tensor_tensor(stat[:, WMAX:WMAX + 1], stat[:, WMAX:WMAX + 1], stat[:, WNEG:WNEG + 1], ALU.add))
            done(dve.tensor_scalar(stat[:, WMAX:WMAX + 1], stat[:, WMAX:WMAX + 1], 1e-8, None, ALU.add))
            done(dve.reciprocal(stat[:, WMAX:WMAX + 1], stat[:, WMAX:WMAX + 1]))
            done(dve.tensor_scalar(ew[:, :], staging_e, stat[:, WNEG:WNEG + 1], stat[:, WMAX:WMAX + 1], ALU.add, ALU.mult))

        def start_sp_ends(sp):
            sp.wait_ge(s_until, 1)
            sp.dma_start(ends_row, until[0:BLKS, 1:2]).then_inc(s_ends_row, 16)
            sp.wait_ge(s_ends_row, 16)
            sp.dma_start(ends[0:1, 1:], ends_row.rearrange("b o -> o b")).then_inc(s_ends, 16)

        def load_rounds(eng):
            eng.wait_ge(s_rounds, 1)
            return (eng.value_load(roundsi[0:1, 0:1], min_val=1, max_val=WINDOWS),
                    eng.value_load(roundsi[0:1, 1:2], min_val=0, max_val=WINDOWS - 1))

        def idx_of(p):
            return reli if p >= 3 else srci

        def pass_pool(pool, p, rounds):
            into, slots, iters, width = (gat0, SLOTS0, ITERS0, HID) if p == 0 else (gat, SLOTS, ITERS, F)
            if p:
                pool.wait_ge(idx_ready[p - 1], rounds * GROUPS + (SLOTS0 if p == 1 else SLOTS))
                pool.sem_inc(gate, 1)
                pool.tensor_copy(slot_idx[:, :, :], idx_of(p)[:, 0:SLOTS * U].rearrange("p (s u) -> p s u", u=U)
                                 ).then_inc(idx_ready[p], SLOTS)
            for s in table_stored[p]:
                pool.wait_ge(s, STORED[p])
                pool.sem_inc(gate, 1)

            with pool.Fori(0, rounds) as r:
                with pool.Fori(0, iters) as it:
                    n = (r * iters + it) * slots
                    for q in range(slots):
                        pool.wait_ge(idx_ready[p], n + q + 1)
                        pool.sem_inc(gate, 1)
                        if p == 0:
                            pool.wait_ge(relu_done, (n + q) * 2 + 2)
                            pool.sem_inc(gate, 1)
                        for u in range(U):
                            pool.indirect_dma_start(
                                into[:, q, u, 0:width], None, tables[p],
                                bass.IndirectOffsetOnAxis(ap=slot_idx[:, q, u:u + 1].bitcast(U32), axis=0),
                            ).then_inc(gathered[p][q], 16)

        def round_setup(dve, p, r, lead):
            s = setup_step[p]
            dve.wait_ge(s, r * 4 + 1)
            dve.tensor_scalar(base[:, :], firstf[:, :], stat[:, FAST:FAST + 1], stat[:, WOFF:WOFF + 1],
                              ALU.mult, ALU.add).then_inc(s, 1)
            dve.wait_ge(s, r * 4 + 2)
            dve.tensor_tensor(local[:, :].rearrange("p (g u) -> p g u", u=U),
                              dstf[:, :].rearrange("p (g u) -> p g u", u=U),
                              base[:, :].unsqueeze(2).broadcast_to([P, GROUPS, U]), ALU.subtract).then_inc(s, 1)
            dve.tensor_copy(basei[:, lead:lead + GROUPS], base[0:1, :]).then_inc(s, 1)
            dve.wait_ge(s, r * 4 + 4)
            dve.tensor_tensor(stat[:, WOFF:WOFF + 1], stat[:, WOFF:WOFF + 1], stat[:, STEP:STEP + 1],
                              ALU.add).then_inc(s, 1)
            dve.wait_ge(s, r * 4 + 5)
            dve.sem_inc(gate, 1)

        def load_bases(dve, it, slots):
            return nc.values_load_multi_w_load_instructions(
                basei[0:1, bass.ds(it * slots, slots)], engines=[mybir.EngineType.DVE], min_val=0, max_val=NP)[1]

        def one_hot(dve, p, g, n, q):
            dve.wait_ge(seg_done[p], n + 1)
            hq = q % HOTS
            mine = local[:, bass.ds(g * U, U)]
            ins = dve.tensor_tensor(hot[:, hq, :].rearrange("p (u w) -> p u w", u=U),
                                    iota[:, 0:WIN].unsqueeze(1).broadcast_to([P, U, WIN]),
                                    mine.unsqueeze(2).broadcast_to([P, U, WIN]), ALU.is_equal)
            if p == 0:
                dve.tensor_tensor(hot_hi[:, hq, :, :], iota[:, 0:NT].unsqueeze(1).broadcast_to([P, U, NT]),
                                  src_hi[:, bass.ds(g * U, U)].unsqueeze(2).broadcast_to([P, U, NT]), ALU.is_equal)
                for u in range(U):
                    ins = dve.tensor_scalar(hot_lo[:, hq, u, :], iota_b[:, :], src_lo[:, bass.ds(g * U + u, 1)], None,
                                            ALU.is_equal)
            ins.then_inc(hot_ready[p], 1)

        def weighted_hot(dve, p, g, n, q):
            dve.wait_ge(seg_done[p], n + 1)
            for u in range(U):
                ins = dve.tensor_scalar(hot[:, q % HOTS, u * WIN:(u + 1) * WIN], iota[:, 0:WIN], local[:, bass.ds(g * U + u, 1)],
                                        ew[:, bass.ds(g * U + u, 1)], ALU.is_equal, ALU.mult)
            ins.then_inc(hot_ready[p], 1)

        def accumulate(dve, p, at, n, q, ago=0):
            planes = 3 if p == 0 else 1
            there = acc[:, 0:planes, bass.ds(at, WIN)]
            dve.wait_ge(seg_done[p], n + (1 + PRIME_SLOT - ago))
            dve.wait_ge(accumulated[p], n + (PRIME_BANK - ago))
            dve.tensor_tensor(there, there, bank[4 + q % 2][:, 0:planes * WIN].rearrange("p (c w) -> p c w", c=planes),
                              ALU.add).then_inc(accumulated[p], 1)

        def pass0_dve(dve, rounds):
            dve.sem_inc(accumulated[0], PRIME_BANK)
            dve.memset(stat[:, WOFF:WOFF + 1], 0.0).then_inc(setup_step[0], 1)
            dve.sem_inc(pre_added, PRIME_PAIR)
            dve.wait_ge(s_param, PARAMS)
            dve.tensor_tensor(X[:, :, :], X[:, :, :], b2b_row[:, :].unsqueeze(1).broadcast_to([P, NT, F]), ALU.add).then_inc(s_x, 1)

            def body(r, it, first=False):
                m = r * ITERS0 + it
                n = m * SLOTS0
                at = load_bases(dve, it, SLOTS0)
                for q in range(SLOTS0):
                    one_hot(dve, 0, it * SLOTS0 + q, n + q, q)
                    if not first or q >= LAG:
                        accumulate(dve, 0, at[q], n, q, LAG - q)
                    for h in range(2):
                        g = gat0[:, q, 2 * h:2 * h + 2, :].rearrange("p u c -> p (u c)")
                        dve.wait_ge(gathered[0][q], (m + 1) * 16 * U)
                        dve.wait_ge(pre_done, (n + q) * 2 + h + 1 + 2 * SLOTS0)
                        dve.tensor_tensor(g, g, bank[q % 2 * 2 + h][:, :], ALU.add).then_inc(pre_added, 1)

            with dve.Fori(0, rounds) as r:
                round_setup(dve, 0, r, LAG)
                body(r, 0, True)
                with dve.Fori(1, ITERS0) as it:
                    body(r, it)
                at = load_bases(dve, ITERS0, SLOTS0)
                for q in range(LAG):
                    accumulate(dve, 0, at[q], (r + 1) * GROUPS, q, LAG - q)
                dve.wait_ge(hot_ready[0], (r + 1) * GROUPS)
                dve.tensor_scalar(src_lo[:, :], src_lo[:, :], 0.0, -1.0, ALU.mult, ALU.add)
            dve.wait_ge(accumulated[0], rounds * GROUPS + PRIME_BANK)
            dve.sem_inc(pass_done, 1)

        def pass0_pe(pe, rounds):
            pe.sem_inc(seg_done[0], PRIME_SLOT)
            pe.sem_inc(pre_done, 2 * SLOTS0)
            pe.wait_ge(s_const, CONSTANTS)
            pe.matmul(bank[HIST][:, 0:NT], zeros_b[:, :], zeros_b[:, 0:NT], start=True, stop=False, skip_group_check=True)

            def pre(m, n, q):
                slot = q % SLOTS0
                pe.wait_ge(ea_ready[slot], (m + q // SLOTS0 + 1) * 16)
                for h in range(2):
                    pe.wait_ge(pre_added, (n + q) * 2 + h + 1)
                    for j in range(2):
                        u = 2 * h + j
                        mm = pe.matmul(bank[q % 2 * 2 + h][:, j * HID:(j + 1) * HID], ea[:, slot, u * P:(u + 1) * P],
                                       w1a[:, 1, :], start=True, stop=True)
                    mm.then_inc(pre_done, 1)

            def segment_sum(n, q):
                pe.wait_ge(relu_done, n * 2 + 2 + 2 * SLOTS0)
                pe.wait_ge(hot_ready[0], n + 1)
                pe.wait_ge(accumulated[0], n + 1)
                into = bank[4 + q % 2]
                for c in range(2):
                    for u in range(U):
                        pe.matmul(into[:, c * WIN:(c + 1) * WIN], hid[:, q, u * HID + c * F:u * HID + (c + 1) * F],
                                  hot[:, q, u * WIN:(u + 1) * WIN], start=(u == 0), stop=(u == U - 1))
                upper = hot[:, q, :].bitcast(BF16).rearrange("p (u w t) -> p u w t", u=U, t=2)
                for u in range(U):
                    pe.matmul(into[:, 2 * WIN:3 * WIN], ones_b[:, :], upper[:, u, :, 1], start=(u == 0), stop=(u == U - 1))
                for u in range(U):
                    mm = pe.matmul(bank[HIST][:, 0:NT], hot_lo[:, q, u, :], hot_hi[:, q, u, :], start=False, stop=False,
                                   skip_group_check=True)
                mm.then_inc(seg_done[0], 1)

            def body(r, it, last=False):
                m = r * ITERS0 + it
                n = m * SLOTS0
                for q in range(SLOTS0):
                    segment_sum(n + q, q)
                    if not last or q + LAG < SLOTS0:
                        pre(m, n, q + LAG)

            with pe.Fori(0, rounds) as r:
                for q in range(LAG):
                    pre(r * ITERS0, r * GROUPS, q)
                with pe.Fori(0, ITERS0 - 1) as it:
                    body(r, it)
                body(r, ITERS0 - 1, True)

        def pass0_act(act, rounds):
            act.sem_inc(relu_done, 2 * SLOTS0)
            for q in range(SLOTS0):
                act.copy(slot_idx[:, q, :], srci[:, q * U:(q + 1) * U]).then_inc(idx_ready[0], 1)
            act.preload_act_table(ACT.Relu)
            with act.Fori(0, rounds) as r:
                with act.Fori(0, ITERS0) as it:
                    m = r * ITERS0 + it
                    n = m * SLOTS0
                    for q in range(SLOTS0):
                        for h in range(2):
                            act.wait_ge(pre_added, (n + q) * 2 + h + 1 + PRIME_PAIR)
                            act.wait_ge(seg_done[0], n + q + 1)
                            act.activation(hid[:, q, h * 2 * HID:(h + 1) * 2 * HID],
                                           gat0[:, q, 2 * h:2 * h + 2, :].rearrange("p u c -> p (u c)"),
                                           ACT.Relu).then_inc(relu_done, 1)
                        act.wait_ge(gathered[0][q], (m + 1) * 16 * U)
                        act.sem_inc(gate, 1)
                        act.copy(slot_idx[:, q, :], srci[:, bass.ds((it * SLOTS0 + SLOTS0 + q) * U, U)]
                                 ).then_inc(idx_ready[0], 1)

        def pass0_sp(sp, rounds):
            with sp.Fori(0, rounds) as r:
                with sp.Fori(0, ITERS0) as it:
                    n = (r * ITERS0 + it) * SLOTS0
                    for q in range(SLOTS0):
                        sp.wait_ge(pre_done, (n + q) * 2 + 2)
                        sp.sem_inc(gate, 1)
                        sp.dma_start(ea[:, q, :], ea_cols[:, bass.ds((it * SLOTS0 + q) * GE, GE)]).then_inc(ea_ready[q], 16)

        def segments(eng, before, step, node, each_round=None):
            with eng.If(before > 0):
                with eng.Fori(0, before) as r:
                    if each_round:
                        each_round(r)
                    with eng.Fori(0, ITERS) as it:
                        step(it, r * ITERS + it)
            if each_round:
                each_round(before)

            def segment(k, last):
                lo = eng.value_load(ends[0:1, bass.ds(k, 1)], min_val=0, max_val=ITERS)
                hi = eng.value_load(ends[0:1, bass.ds(k + 1, 1)], min_val=0, max_val=ITERS)
                with eng.If(lo < hi):
                    with eng.Fori(lo, hi) as it:
                        step(it, before * ITERS + it)
                node(k, last, before * ITERS + hi)
            blocks(eng, segment)

        def pass_dve(dve, p, before, node):
            dve.sem_inc(accumulated[p], PRIME_BANK)
            dve.memset(stat[:, WOFF:WOFF + 1], 0.0).then_inc(setup_step[p], 1)
            if p == 1:
                dve.wait_ge(s_ends, 16)
                dve.wait_ge(acc_zero, 1)
            else:
                dve.wait_ge(cleared, (p - 1) * BLKS)

            def step(it, m):
                n = m * SLOTS
                at = load_bases(dve, it, SLOTS)
                for q in range(SLOTS + LAG):
                    if q < SLOTS:
                        (weighted_hot if p >= 3 else one_hot)(dve, p, it * SLOTS + q, n + q, q)
                    if q >= LAG:
                        done = q - LAG
                        dve.wait_ge(seg_done[p], n + (done + 1 + PRIME_SLOT))
                        dve.tensor_copy(slot_idx[:, done, :], idx_of(p)[:, bass.ds((it * SLOTS + SLOTS + done) * U, U)]
                                        ).then_inc(idx_ready[p], 1)
                        accumulate(dve, p, at[done], n + done, done)

            def block(k, last, steps):
                dve.wait_ge(accumulated[p], steps * SLOTS + PRIME_BANK)
                dve.sem_inc(gate, 1)
                node(dve, k, last)
            segments(dve, before, step, block, lambda r: round_setup(dve, p, r, 0))

        def clear(dve, k):
            dve.sem_inc(gate, 1)
            dve.tensor_copy(acc[:, 0, bcols(k)].rearrange("p (t c) -> p t c", t=BT),
                            zeros_b[:, :].unsqueeze(1).broadcast_to([P, BT, P])).then_inc(cleared, 1)

        def pass_pe(pe, p, before, node):
            pe.sem_inc(seg_done[p], PRIME_SLOT)
            if p == 1:
                pe.wait_ge(s_ends, 16)

            def step(it, m):
                n = m * SLOTS
                for q in range(SLOTS):
                    pe.wait_ge(gathered[p][q], (m + 1) * 16 * U)
                    pe.wait_ge(hot_ready[p], n + q + 1)
                    pe.wait_ge(accumulated[p], n + q + 1)
                    for u in range(U):
                        mm = pe.matmul(bank[4 + q % 2][:, 0:WIN], gat[:, q, u, :], hot[:, q % HOTS, u * WIN:(u + 1) * WIN],
                                       start=(u == 0), stop=(u == U - 1))
                    mm.then_inc(seg_done[p], 1)

            segments(pe, before, step, lambda k, last, steps: node(pe, k, last))

        def norm_stats(dve, step, k, s, tiles, x_of):
            for j in range(tiles):
                ins = dve.bn_stats(bn[:, s, j, :], x_of(j))
            ins.then_inc(step, 1)
            dve.wait_ge(step, k * 4 + 1)
            dve.sem_inc(gate, 1)
            for j in range(tiles):
                ins = dve.bn_aggr(mv[:, s, j, :], bn[:, s, j, :])
            ins.then_inc(step, 1)

        def norm_root(act, step, root, k, s, tiles):
            act.wait_ge(step, k * 4 + 2)
            act.activation(std[:, s, 0:tiles], mv[:, s, 0:tiles, 1], ACT.Sqrt, bias=stat[:, EPSC:EPSC + 1]).then_inc(root, 1)

        def norm_apply(dve, step, root, k, s, tiles, x_of, to):
            dve.wait_ge(root, k + 1)
            dve.reciprocal(rstd[:, s, 0:tiles], std[:, s, 0:tiles]).then_inc(step, 1)
            dve.wait_ge(step, k * 4 + 3)
            for j in range(tiles):
                ins = dve.tensor_scalar(to(j), x_of(j), mv[:, s, j, 0:1], rstd[:, s, j:j + 1], ALU.subtract, ALU.mult)
            ins.then_inc(step, 1)

        def x_row(t):
            return X[:, bass.ds(t, 1), :].rearrange("p o f -> p (o f)")

        (n0_agg, n0_scaled, n0_aggT, n0_hid, n0_relu, n0_out, n0_step, n0_root, n0_deg, n0_rows, n0_c2, n0_dsc, n0_sum) = (
            sem(f"n0_{x}") for x in ("agg", "scaled", "aggT", "hid", "relu", "out", "step", "root", "deg", "rows", "c2", "dsc", "sum"))
        n0_xT = sems("n0_xT", 2)

        TILES_IN = ((0, 3, 6), (3, 2, 7))

        def node0_sp(sp):
            sp.wait_ge(pass_done, 1)

            def load(k, s, last):
                if later(k, 2):
                    sp.wait_ge(n0_hid, k - 1)
                sp.sem_inc(gate, 1)
                sp.dma_start(xT[:, s, :], x_cols[:, cols(k)]).then_inc(n0_xT[s], 16)
            chunks(sp, load)

        def node0_pool(pool):
            def store(k, s, last):
                if last:
                    pool.wait_ge(n0_agg, CHUNKS)
                    pool.sem_inc(gate, 1)
                    pool.memset(acc[:, 0, :], 0.0).then_inc(acc_zero, 1)
                pool.wait_ge(n0_rows, k + 1)
                pool.sem_inc(gate, 1)
                pool.dma_start(node_rows(tables[1], k), rows[:, s, :, :]).then_inc(table_stored[1][s], 16)
            chunks(pool, store)

        def node0_pe(pe):
            pe.wait_ge(s_param, PARAMS)
            pe.wait_ge(s_ident, 1)
            pe.wait_ge(pass_done, 1)
            for c in range(2):
                mm = pe.matmul(bank[7][:, c:c + 1], w2a[:, 2, c * F:(c + 1) * F], bias[:, U0:U0 + 1], start=True, stop=True)
            mm.then_inc(n0_c2, 1)

            def agg(k):
                if later(k, 1):
                    pe.wait_ge(n0_scaled, k * 2)
                for sub in range(2):
                    for c in range(2):
                        mm = pe.matmul(bank[sub][:, 0:SUB], w1b[:, c, :], acc[:, c, cols(k, sub)], start=(c == 0), stop=(c == 1))
                mm.then_inc(n0_agg, 1)

            def body(k, s, last):
                pe.wait_ge(n0_xT[s], (k - s) * 8 + 16)
                if later(k, 1):
                    pe.wait_ge(n0_relu, k * 4)
                for c in range(2):
                    for sub in range(2):
                        pe.matmul(bank[2 + 2 * c + sub][:, 0:SUB], w2a[:, 0, c * F:(c + 1) * F],
                                  xT[:, s, sub * SUB:(sub + 1) * SUB], start=True, stop=False)
                pe.wait_ge(n0_aggT, k * 2 + 2)
                for c in range(2):
                    for sub in range(2):
                        mm = pe.matmul(bank[2 + 2 * c + sub][:, 0:SUB], w2a[:, 1, c * F:(c + 1) * F],
                                       aggT[:, s, sub * SUB:(sub + 1) * SUB], start=False, stop=True)
                mm.then_inc(n0_hid, 1)
                if not last:
                    agg(k + 1)
                pe.wait_ge(n0_relu, k * 4 + 4)
                if later(k, 1):
                    pe.wait_ge(n0_sum, k * 2)
                else:
                    pe.wait_ge(n0_dsc, 1)
                for t0, n, b in TILES_IN:
                    for j in range(n):
                        for c in range(2):
                            at = c * CH + (t0 + j) * P
                            mm = pe.matmul(bank[b][:, j * F:(j + 1) * F], h2T[:, s, at:at + P], w2b[:, c, :],
                                           start=(c == 0), stop=(c == 1))
                mm.then_inc(n0_out, 1)
            agg(0)
            chunks(pe, body)

        def node0_act(act):
            def scaled(k, s):
                act.wait_ge(n0_step, k * 4 + 4)
                if later(k, 2):
                    act.wait_ge(table_stored[1][s], (k - s) * 8)
                act.sem_inc(gate, 1)
                for j in range(CT):
                    t = k * CT + j
                    ins = act.activation(rows[:, s, j, :], x_row(t), ACT.Copy, scale=dsc[:, bass.ds(t, 1)])
                ins.then_inc(n0_rows, 1)

            def body(k, s, last):
                if later(k, 1):
                    norm_root(act, n0_step, n0_root, k - 1, 1 - s, CT)
                act.wait_ge(n0_hid, k + 1)
                for c in range(2):
                    for sub in range(2):
                        act.activation(h2T[:, s, c * CH + sub * SUB:c * CH + (sub + 1) * SUB],
                                       bank[2 + 2 * c + sub][:, 0:SUB], ACT.Relu, bias=c2[:, c:c + 1]).then_inc(n0_relu, 1)
                if later(k, 1):
                    scaled(k - 1, 1 - s)
                if last:
                    norm_root(act, n0_step, n0_root, k, s, CT)
                    scaled(k, s)
            act.preload_act_table(ACT.Sqrt)
            act.wait_ge(n0_dsc, 1)
            act.activation(dtmp[:, :], dsc[:, :], ACT.Sqrt).then_inc(n0_dsc, 1)
            act.wait_ge(n0_dsc, 3)
            chunks(act, body)

        def node0_dve(dve):
            dve.wait_ge(s_param, PARAMS)
            dve.wait_ge(s_x, 1)
            dve.wait_ge(n0_c2, 1)
            dve.tensor_tensor(c2[:, :], bank[7][:, 0:2], bias[:, B2A0:B2A1 + 1], ALU.add)
            dve.tensor_scalar(dsc[:, :], bank[HIST][:, 0:NT], 1.0, None, ALU.max).then_inc(n0_dsc, 1)
            def degrees(k, s):
                deg = acc[:, 2, cols(k)]
                if later(k, 2):
                    dve.wait_ge(n0_aggT, k * 2 - 2)
                dve.tensor_scalar(ratio[:, s, :], deg, 1.0, None, ALU.min)
                dve.tensor_scalar(deg, deg, 1.0, None, ALU.max).then_inc(n0_deg, 1)
                dve.wait_ge(n0_deg, k * 2 + 1)
                dve.sem_inc(gate, 1)
                dve.reciprocal(deg, deg).then_inc(n0_deg, 1)

            def mean_of(k, s):
                dve.wait_ge(n0_agg, k + 1)
                dve.wait_ge(n0_deg, k * 2 + 2)
                if later(k, 2):
                    dve.wait_ge(n0_hid, k - 1)
                for sub in range(2):
                    dve.tensor_tensor(aggT[:, s, sub * SUB:(sub + 1) * SUB], bank[sub][:, 0:SUB], acc[:, 2, cols(k, sub)],
                                      ALU.mult).then_inc(n0_scaled, 1)
                for sub in range(2):
                    half = slice(sub * SUB, (sub + 1) * SUB)
                    dve.wait_ge(n0_scaled, k * 2 + sub + 1)
                    dve.scalar_tensor_tensor(aggT[:, s, half], ratio[:, s, half], bias[:, B1B:B1B + 1], aggT[:, s, half],
                                             ALU.mult, ALU.add).then_inc(n0_aggT, 1)

            def applied(k, s):
                norm_apply(dve, n0_step, n0_root, k, s, CT, lambda j: tsum[:, s, j, :], lambda j: x_row(k * CT + j))

            def body(k, s, last):
                if not last:
                    degrees(k + 1, 1 - s)
                    mean_of(k + 1, 1 - s)
                if later(k, 1):
                    applied(k - 1, 1 - s)
                dve.wait_ge(n0_out, k + 1)
                for t0, n, b in TILES_IN:
                    dve.tensor_tensor(tsum[:, s, t0:t0 + n, :], bank[b][:, 0:n * F].rearrange("p (t f) -> p t f", f=F),
                                      X[:, bass.ds(k * CT + t0, n), :], ALU.add).then_inc(n0_sum, 1)
                dve.wait_ge(n0_sum, k * 2 + 2)
                norm_stats(dve, n0_step, k, s, CT, lambda j: tsum[:, s, j, :])
                if last:
                    applied(k, s)
            degrees(0, 0)
            mean_of(0, 0)
            dve.wait_ge(n0_dsc, 2)
            dve.reciprocal(dsc[:, :], dtmp[:, :]).then_inc(n0_dsc, 1)
            chunks(dve, body)

        (n1_row, n1_turn, n1_xT, n1_res, n1_rs, n1_mean, n1_mm, n1_relu, n1_y, n1_bn, n1_one) = (
            sem(f"n1_{x}") for x in ("row", "turn", "xT", "res", "rs", "mean", "mm", "relu", "y", "bn", "one"))

        def node1_act(act):
            act.wait_ge(n0_step, CHUNKS * 4)
            act.wait_ge(n0_deg, CHUNKS * 2)
            act.preload_act_table(ACT.Sqrt)

            def block(k, last):
                if later(k, 1):
                    act.wait_ge(n1_turn, k)
                    act.sem_inc(gate, 1)
                act.activation(b_rows, X_rows(k), ACT.Copy).then_inc(n1_row, 1)
                if later(k, 1):
                    act.wait_ge(n1_mean, k)
                    act.sem_inc(gate, 1)
                act.activation(b_w, acc[:, 2, bcols(k)], ACT.Sqrt).then_inc(n1_rs, 1)
                act.wait_ge(n1_turn, k + 1)
                act.sem_inc(gate, 1)
                act.activation(b_xT, bank[0][:, 0:BLK], ACT.Copy).then_inc(n1_xT, 1)
                act.wait_ge(n1_res, k + 1)
                if later(k, 1):
                    act.wait_ge(n1_y, k)
                act.activation(b_u, bank[1][:, 0:BLK], ACT.Relu, bias=bias[:, GBR:GBR + 1]).then_inc(n1_relu, 1)
                act.wait_ge(n1_mm, k + 1)
                act.activation(b_v, bank[2][:, 0:BLK], ACT.Relu, bias=bias[:, GB:GB + 1]).then_inc(n1_relu, 1)
            blocks(act, block)

        def node1_pe(pe, k, last):
            pe.wait_ge(n1_row, k + 1)
            for j in range(BT):
                mm = pe.transpose(bank[0][:, j * P:(j + 1) * P], b_rows[:, j, :], ident[:, :])
            mm.then_inc(n1_turn, 1)
            pe.wait_ge(n1_xT, k + 1)
            if later(k, 1):
                pe.wait_ge(n1_relu, k * 2)
            pe.matmul(bank[1][:, 0:BLK], w_res[:, :], b_xT, start=True, stop=True).then_inc(n1_res, 1)
            pe.wait_ge(n1_mean, k + 1)
            pe.matmul(bank[2][:, 0:BLK], w_gcn[:, :], b_mean, start=True, stop=True).then_inc(n1_mm, 1)

        def node1_dve(dve, k, last):
            if later(k, 1):
                dve.wait_ge(n1_mm, k)
            dve.wait_ge(n1_rs, k + 1)
            dve.tensor_tensor(b_mean, acc[:, 0, bcols(k)], b_w, ALU.mult).then_inc(n1_mean, 1)
            dve.wait_ge(n1_relu, k * 2 + 2)
            clear(dve, k)
            dve.tensor_tensor(rest[:, bcols(k)], b_u, b_v, ALU.add).then_inc(n1_y, 1)
            dve.wait_ge(n1_y, k + 1)
            dve.sem_inc(gate, 1)
            y = rest[:, bass.ds(k * BLK, LAST if last else BLK)]
            dve.bn_stats(bn_y[:, bass.ds(k, 1), :].rearrange("p o c -> p (o c)"), y).then_inc(n1_bn, 1)

        m_u, m_turn, m_sum, m_bn, m_step, m_root, m_row, m_row2 = (
            sem(f"m_{x}") for x in ("u", "turn", "sum", "bn", "step", "root", "row", "row2"))

        def batch_norm_dve(dve):
            dve.wait_ge(n1_bn, BLKS)
            dve.bn_aggr(mv_y[:, :], bn_y[:, :, :].rearrange("p b c -> p (b c)")).then_inc(n1_one, 1)
            dve.wait_ge(n1_one, 1)
            dve.wait_ge(n1_one, 2)
            dve.reciprocal(stat[:, RSTD:RSTD + 1], stat[:, STDB:STDB + 1]).then_inc(n1_one, 1)
            dve.wait_ge(n1_one, 3)
            dve.tensor_tensor(stat[:, SCALE:SCALE + 1], stat[:, RSTD:RSTD + 1], bias[:, GAMMA:GAMMA + 1], ALU.mult).then_inc(n1_one, 1)
            dve.wait_ge(n1_one, 4)
            dve.tensor_tensor(stat[:, SHIFT:SHIFT + 1], mv_y[:, 0:1], stat[:, SCALE:SCALE + 1], ALU.mult).then_inc(n1_one, 1)
            dve.wait_ge(n1_one, 5)
            dve.tensor_tensor(stat[:, SHIFT:SHIFT + 1], bias[:, BETA:BETA + 1], stat[:, SHIFT:SHIFT + 1],
                              ALU.subtract).then_inc(n1_one, 1)

            def block(k, s, last):
                dve.wait_ge(m_turn, k + 1)
                dve.tensor_tensor(X_rows(k), bank[6 + s][:, 0:BLK].rearrange("p (t f) -> p t f", f=F), X_rows(k),
                                  ALU.add).then_inc(m_sum, 1)
                dve.wait_ge(m_sum, k + 1)
                dve.sem_inc(gate, 1)
                for j in range(BT):
                    t = k * BT + j
                    ins = dve.bn_stats(bn_row[:, bass.ds(t, 1), :].rearrange("p o c -> p (o c)"), x_row(t))
                ins.then_inc(m_bn, 1)
            pairs(dve, block)
            dve.wait_ge(m_bn, BLKS)
            even, odd = bn_row[:, :, 1], bn_row[:, :, 4]
            n = [0]

            def done(ins):
                n[0] += 1
                ins.then_inc(m_step, 1)
                dve.wait_ge(m_step, n[0])
            done(dve.tensor_tensor(row_mean[:, :], even, odd, ALU.add))
            done(dve.tensor_scalar(row_mean[:, :], row_mean[:, :], 0.5, None, ALU.mult))
            done(dve.tensor_tensor(row_half[:, :], even, odd, ALU.subtract))
            done(dve.tensor_tensor(row_half[:, :], row_half[:, :], row_half[:, :], ALU.mult))
            done(dve.tensor_tensor(row_var[:, :], bn_row[:, :, 2], bn_row[:, :, 5], ALU.add))
            done(dve.scalar_tensor_tensor(row_var[:, :], row_half[:, :], F / 4.0, row_var[:, :], ALU.mult, ALU.add))
            dve.wait_ge(m_root, 1)
            done(dve.reciprocal(row_rstd[:, :], row_std[:, :]))
            done(dve.scalar_tensor_tensor(row_shift[:, :], row_mean[:, :], -1.0, row_rstd[:, :], ALU.mult, ALU.mult))

            def apply(k, last):
                t = k * BT
                dve.tensor_scalar(x_row(t), x_row(t), row_mean[:, bass.ds(t, 1)], row_rstd[:, bass.ds(t, 1)],
                                  ALU.subtract, ALU.mult).then_inc(m_row, 1)
            blocks(dve, apply)

        M_VAR, M_SHIFT = 6, 8

        def batch_norm_act(act):
            act.wait_ge(n1_one, 1)
            act.activation(stat[:, STDB:STDB + 1], mv_y[:, 1:2], ACT.Sqrt, bias=stat[:, EPSC:EPSC + 1]).then_inc(n1_one, 1)
            act.wait_ge(n1_one, 6)

            def block(k, s, last):
                if later(k, 2):
                    act.wait_ge(m_turn, k - 1)
                    act.sem_inc(gate, 1)
                act.activation(b_bn[:, s, :], rest[:, bcols(k)], ACT.Identity, bias=stat[:, SHIFT:SHIFT + 1],
                               scale=stat[:, SCALE:SCALE + 1]).then_inc(m_u, 1)
            pairs(act, block)
            act.wait_ge(m_step, M_VAR)
            act.activation(row_std[:, :], row_var[:, :], ACT.Sqrt, bias=stat[:, EPSC:EPSC + 1], scale=1.0 / F).then_inc(m_root, 1)
            act.wait_ge(m_step, M_SHIFT)

            def apply(k, last):
                t = k * BT + 1
                act.activation(x_row(t), x_row(t), ACT.Identity, bias=row_shift[:, bass.ds(t, 1)],
                               scale=row_rstd[:, bass.ds(t, 1)]).then_inc(m_row2, 1)
            blocks(act, apply)

        def batch_norm_pe(pe):
            def block(k, s, last):
                pe.wait_ge(m_u, k + 1)
                if later(k, 2):
                    pe.wait_ge(m_sum, k - 1)
                for j in range(BT):
                    mm = pe.transpose(bank[6 + s][:, j * P:(j + 1) * P], b_bn[:, s, j * P:(j + 1) * P], ident[:, :])
                mm.then_inc(m_turn, 1)
            pairs(pe, block)

        def batch_norm_sp(sp):
            def store(k, last):
                sp.wait_ge(m_row, k + 1)
                sp.sem_inc(gate, 1)
                sp.wait_ge(m_row2, k + 1)
                sp.sem_inc(gate, 1)
                sp.dma_start(block_rows(tables[2], k), X_rows(k)).then_inc(table_stored[2][0], 16)
            blocks(sp, store)

        class Rel:
            def __init__(self, name):
                self.xT, self.root_mm, self.mm, self.emptied = (sem(f"{name}_{x}") for x in ("xT", "root_mm", "mm", "emptied"))

        rel1, rel2 = Rel("rel1"), Rel("rel2")

        def rel_pe(pe, i, rel, k):
            pe.wait_ge(rel.xT, k + 1)
            if later(k, 1):
                pe.wait_ge(rel.emptied, k * 3)
            pe.matmul(bank[1][:, 0:BLK], w_root[i][:, :], b_xT, start=True, stop=True).then_inc(rel.root_mm, 1)
            for t in range(BT):
                pe.matmul(bank[2 + t][:, :], b_xT[:, t * P:(t + 1) * P], w_rel[i][:, :, :].rearrange("p r f -> p (r f)"),
                          start=True, stop=True).then_inc(rel.mm, 1)

        def rel_act(act, p, i, rel, k):
            act.wait_ge(rel.root_mm, k + 1)
            act.sem_inc(gate, 1)
            act.activation(rest[:, bcols(k)], bank[1][:, 0:BLK], ACT.Identity, bias=bias[:, RB1 + i:RB1 + i + 1]
                           ).then_inc(rel.emptied, 1)
            if later(k, 1):
                act.wait_ge(table_stored[p][0], k * 16)
                act.sem_inc(gate, 1)
            for t in range(BT):
                act.wait_ge(rel.mm, k * BT + t + 1)
                act.activation(b_rel[:, t, :], bank[2 + t][:, :], ACT.Copy).then_inc(rel.emptied, 1)

        def rel_sp(sp, p, rel):
            def store(k, last):
                sp.wait_ge(rel.emptied, k * 3 + 3)
                sp.sem_inc(gate, 1)
                sp.dma_start(block_rows(tables[p].rearrange("(n r) f -> n (r f)", r=RELS), k), b_rel).then_inc(table_stored[p][0], 16)
            blocks(sp, store)

        (n2_mean, n2_mm, n2_min, n2_exp, n2_u, n2_turn, n2_sum, n2_step, n2_root, n2_turn2, n2_kept) = (
            sem(f"n2_{x}") for x in ("mean", "mm", "min", "exp", "u", "turn", "sum", "step", "root", "turn2", "kept"))

        def node2_pe(pe, k, last):
            pe.wait_ge(n2_mean, k + 1)
            pe.matmul(bank[0][:, 0:BLK], w_mean[:, :], b_mean, start=True, stop=True).then_inc(n2_mm, 1)
            pe.wait_ge(n2_u, k + 1)
            if later(k, 1):
                pe.wait_ge(rel1.emptied, k * 3)
            for j in range(BT):
                mm = pe.transpose(bank[1][:, j * P:(j + 1) * P], b_xT[:, j * P:(j + 1) * P], ident[:, :])
            mm.then_inc(n2_turn, 1)
            pe.wait_ge(n2_step, k * 4 + 4)
            for j in range(BT):
                mm = pe.transpose(bank[0][:, j * P:(j + 1) * P], b_rows[:, j, :], ident[:, :])
            mm.then_inc(n2_turn2, 1)
            rel_pe(pe, 0, rel1, k)

        def node2_act(act):
            act.preload_act_table(ACT.Exp)

            def block(k, last):
                act.wait_ge(n2_min, k + 1)
                act.activation(b_u, bank[0][:, 0:BLK], ACT.Relu, bias=bias[:, MB:MB + 1])
                act.activation(b_w, b_v, ACT.Exp).then_inc(n2_exp, 1)
                norm_root(act, n2_step, n2_root, k, 0, BT)
                act.wait_ge(n2_turn2, k + 1)
                act.activation(b_xT, bank[0][:, 0:BLK], ACT.Copy).then_inc(rel1.xT, 1)
                act.activation(X_rows(k), b_rows, ACT.Copy).then_inc(n2_kept, 1)
                rel_act(act, 3, 0, rel1, k)
            blocks(act, block)

        def node2_dve(dve, k, last):
            dve.tensor_tensor(b_mean, acc[:, 0, bcols(k)], acc[:, 2, bcols(k)], ALU.mult).then_inc(n2_mean, 1)
            dve.wait_ge(n2_mm, k + 1)
            dve.tensor_scalar(b_v, bank[0][:, 0:BLK], bias[:, MB:MB + 1], 0.0, ALU.add, ALU.min).then_inc(n2_min, 1)
            clear(dve, k)
            dve.wait_ge(n2_exp, k + 1)
            if later(k, 1):
                dve.wait_ge(rel1.mm, k * BT)
                dve.wait_ge(n2_kept, k)
            dve.scalar_tensor_tensor(b_xT, b_w, -1.0, b_u, ALU.add, ALU.add).then_inc(n2_u, 1)
            dve.wait_ge(n2_turn, k + 1)
            dve.tensor_tensor(b_sum, bank[1][:, 0:BLK].rearrange("p (t f) -> p t f", f=F), X_rows(k), ALU.add).then_inc(n2_sum, 1)
            dve.wait_ge(n2_sum, k + 1)
            norm_stats(dve, n2_step, k, 0, BT, lambda j: b_sum[:, j, :])
            norm_apply(dve, n2_step, n2_root, k, 0, BT, lambda j: b_sum[:, j, :], lambda j: b_rows[:, j, :])

        n3_sum = sem("n3_sum")

        def node3_dve(dve, k, last):
            if later(k, 1):
                dve.wait_ge(rel2.xT, k)
            dve.tensor_tensor(b_u, acc[:, 0, bcols(k)], rest[:, bcols(k)], ALU.add).then_inc(n3_sum, 1)
            dve.wait_ge(n3_sum, k + 1)
            clear(dve, k)

        def node3_act(act):
            act.preload_act_table(ACT.Relu)

            def block(k, last):
                act.wait_ge(n3_sum, k + 1)
                if later(k, 1):
                    act.wait_ge(rel2.mm, k * BT)
                act.activation(b_xT, b_u, ACT.Relu).then_inc(rel2.xT, 1)
                rel_act(act, 4, 1, rel2, k)
            blocks(act, block)

        def node3_pe(pe, k, last):
            rel_pe(pe, 1, rel2, k)

        n4_u, n4_turn, n4_sum, n4_step, n4_root, out_stored = (
            sem(x) for x in ("n4_u", "n4_turn", "n4_sum", "n4_step", "n4_root", "out_stored"))

        def node4_dve(dve, k, last):
            dve.tensor_tensor(b_xT, acc[:, 0, bcols(k)], rest[:, bcols(k)], ALU.add).then_inc(n4_u, 1)
            dve.wait_ge(n4_turn, k + 1)
            dve.tensor_tensor(b_sum, bank[0][:, 0:BLK].rearrange("p (t f) -> p t f", f=F), X_rows(k), ALU.add).then_inc(n4_sum, 1)
            dve.wait_ge(n4_sum, k + 1)
            norm_stats(dve, n4_step, k, 0, BT, lambda j: b_sum[:, j, :])
            if later(k, 1):
                dve.wait_ge(out_stored, k * 16)
                dve.sem_inc(gate, 1)
            norm_apply(dve, n4_step, n4_root, k, 0, BT, lambda j: b_sum[:, j, :], lambda j: b_rows[:, j, :])

        def node4_pe(pe, k, last):
            pe.wait_ge(n4_u, k + 1)
            for j in range(BT):
                mm = pe.transpose(bank[0][:, j * P:(j + 1) * P], b_xT[:, j * P:(j + 1) * P], ident[:, :])
            mm.then_inc(n4_turn, 1)

        def node4_act(act):
            act.preload_act_table(ACT.Sqrt)
            blocks(act, lambda k, last: norm_root(act, n4_step, n4_root, k, 0, BT))

        def node4_sp(sp):
            def store(k, last):
                sp.wait_ge(n4_step, k * 4 + 4)
                sp.sem_inc(gate, 1)
                sp.dma_start(block_rows(out, k), b_rows).then_inc(out_stored, 16)
            blocks(sp, store)
            sp.wait_ge(out_stored, 16 * BLKS)

        @block.sync
        def _(sp):
            start_sp(sp)
            rounds, before = load_rounds(sp)
            start_sp_ends(sp)
            pass0_sp(sp, rounds)
            node0_sp(sp)
            batch_norm_sp(sp)
            rel_sp(sp, 3, rel1)
            rel_sp(sp, 4, rel2)
            node4_sp(sp)

        @block.gpsimd
        def _(pool):
            start_pool(pool)
            rounds, before = load_rounds(pool)
            pass_pool(pool, 0, rounds)
            node0_pool(pool)
            for p in range(1, 5):
                pass_pool(pool, p, rounds)

        @block.scalar
        def _(act):
            start_act_loads(act)
            start_act_store(act)
            rounds, before = load_rounds(act)
            pass0_act(act, rounds)
            node0_act(act)
            node1_act(act)
            batch_norm_act(act)
            node2_act(act)
            node3_act(act)
            node4_act(act)

        @block.tensor
        def _(pe):
            start_pe(pe)
            rounds, before = load_rounds(pe)
            pass0_pe(pe, rounds)
            node0_pe(pe)
            pass_pe(pe, 1, before, node1_pe)
            batch_norm_pe(pe)
            pass_pe(pe, 2, before, node2_pe)
            pass_pe(pe, 3, before, node3_pe)
            pass_pe(pe, 4, before, node4_pe)

        @block.vector
        def _(dve):
            start_dve_rows(dve)
            start_dve(dve)
            rounds, before = load_rounds(dve)
            pass0_dve(dve, rounds)
            node0_dve(dve)
            pass_dve(dve, 1, before, node1_dve)
            batch_norm_dve(dve)
            pass_dve(dve, 2, before, node2_dve)
            pass_dve(dve, 3, before, node3_dve)
            pass_dve(dve, 4, before, node4_dve)


def kernel(x, src, dst, edge_attr_128, edge_type_4, edge_weight, **w):
    import concourse.bacc as bacc
    from concourse.bass_utils import run_bass_kernel_spmd

    def tiles(a, mode, **kw):
        return np.pad(np.asarray(a), (0, EP - E), mode, **kw).reshape(TILES, P).T

    x = np.pad(np.asarray(x), ((0, NP - N), (0, 0)))
    src_tiles = tiles(src, "constant", constant_values=N)
    dst_pad = np.pad(np.asarray(dst), (0, EP - E), "constant", constant_values=N)
    w = {k: np.asarray(v) for k, v in w.items()}
    arrays = {
        "x_rows": x,
        "x_cols": x.T,
        "src": np.concatenate([src_tiles, src_tiles[:, :SLOTS * U]], 1),
        "dst": dst_pad.reshape(TILES, P).T,
        "first": dst_pad[::GE],
        "etype": tiles(edge_type_4, "constant"),
        "eweight": tiles(edge_weight, "edge"),
        "ea_cols": np.pad(np.asarray(edge_attr_128), ((0, EP - E), (0, 0))).T,
        "u0": w["L0_gnn_u"][0],
        "W1a": w["L0_gnn_W1a"], "b1a": w["L0_gnn_b1a"], "W1b": w["L0_gnn_W1b"], "b1b": w["L0_gnn_b1b"],
        "W2a": w["L0_gnn_W2a"], "b2a": w["L0_gnn_b2a"], "W2b": w["L0_gnn_W2b"], "b2b": w["L0_gnn_b2b"],
        "gW": w["L1_gnn_W"], "gb": w["L1_gnn_b"], "gWr": w["L1_gnn_Wr"], "gbr": w["L1_gnn_br"],
        "gamma": w["L1_gnn_gamma"], "beta": w["L1_gnn_beta"], "mW": w["L2_gnn_W"], "mb": w["L2_gnn_b"],
        "rW1": w["L3_gnn_W1"], "rroot1": w["L3_gnn_root1"], "rb1": w["L3_gnn_b1"],
        "rW2": w["L3_gnn_W2"], "rroot2": w["L3_gnn_root2"], "rb2": w["L3_gnn_b2"],
    }
    arrays = {name: np.ascontiguousarray(a) for name, a in arrays.items()}
    nc = bacc.Bacc("TRN2", target_bir_lowering=False, num_devices=1)
    args = {name: nc.dram_tensor(name, a.shape, mybir.dt.from_np(a.dtype), kind="ExternalInput").ap()
            for name, a in arrays.items()}
    out = nc.dram_tensor("out", (NP, F), F32, kind="ExternalOutput").ap()
    gnn(nc, out=out, **args)
    r = run_bass_kernel_spmd(nc, [arrays], core_ids=[0])
    return r.results[0]["out"][:N]
```

```python
from contextlib import ExitStack

import numpy as np

import concourse.bass as bass
from concourse import mybir

P = 128
N = 6250
E = 106250
F = 128
HID = 256
RELS = 4
U = 4
GE = U * P
SLOTS0 = 4
SLOTS = 8
HOTS = 4
ITERS = -(-E // (GE * SLOTS))
GROUPS = ITERS * SLOTS
ITERS0 = GROUPS // SLOTS0
TILES = GROUPS * U
EP = TILES * P
WIN = 64
LAG = 2
CT = 5
CH = CT * P
CHUNKS = -(-N // (2 * CH)) * 2
NP = CHUNKS * CH
NT = NP // P
FRONT = NP - N
WINDOWS = -(-NP // WIN)
SUB = CH // 2
BT = 2
BLK = BT * P
BLKS = NP // BLK
ACC = NP + WIN
PRIME_SLOT = HOTS
PRIME_BANK = 2
PRIME_PAIR = 4
EPS = 1e-5

F32 = mybir.dt.float32
BF16 = mybir.dt.bfloat16
I32 = mybir.dt.int32
U32 = mybir.dt.uint32
ALU = mybir.AluOpType
ACT = mybir.ActivationFunctionType
AX_X = mybir.AxisListType.X


def gnn(nc, x_rows, x_cols, src, dst, first, etype, eweight, ea_cols, W1a, b1a, b2b, biases, weights, out):
    with ExitStack() as ctx:
        def sb(name, shape, dt=F32):
            return ctx.enter_context(nc.sbuf_tensor(name, shape, dt))

        def sem(name):
            return ctx.enter_context(nc.semaphore(name))

        def sems(name, n):
            return [sem(f"{name}{i}") for i in range(n)]

        tables = [nc.dram_tensor("table_pre", [NP, HID], F32).ap(),
                  nc.dram_tensor("table_gcn", [NP, F], F32).ap(),
                  nc.dram_tensor("table_mean", [NP, F], F32).ap(),
                  nc.dram_tensor("table_rel1", [NP * RELS, F], F32).ap(),
                  nc.dram_tensor("table_rel2", [NP * RELS, F], F32).ap()]

        deg_row, inv_row = (nc.dram_tensor(x, [NP], F32).ap() for x in ("deg_row", "inv_row"))
        ends_row = nc.dram_tensor("ends_row", [BLKS, 1], I32).ap()

        acc = sb("acc", [P, 3, ACC])
        rest = acc[:, 1, 0:NP]
        X = sb("X", [P, NT, F])
        srci = sb("srci", [P, TILES + SLOTS * U], I32)
        reli = sb("reli", [P, TILES + SLOTS * U], I32)
        dstf = sb("dstf", [P, TILES])
        local = sb("local", [P, TILES])
        src_lo = sb("src_lo", [P, TILES])
        src_hi = sb("src_hi", [P, TILES])
        ew = sb("ew", [P, TILES])
        firstf = sb("firstf", [P, GROUPS])
        base = sb("base", [P, GROUPS])
        basei = sb("basei", [1, GROUPS + SLOTS0], I32)
        until = sb("until", [P, 2], I32)
        ends = sb("ends", [1, BLKS + 1], I32)
        slot_idx = sb("slot_idx", [P, SLOTS, U], I32)
        ident = sb("ident", [P, P])
        iota = sb("iota", [P, P])
        iota_b = sb("iota_b", [P, P], BF16)
        ones_b = sb("ones_b", [P, P], BF16)
        zeros_b = sb("zeros_b", [P, P], BF16)
        w1a = sb("w1a", [P, 2, HID])
        w_all = sb("w_all", [P, weights.shape[1]])

        def weight(at, parts, n):
            return w_all[:, at:at + parts * n].rearrange("p (c n) -> p c n", c=parts)
        w1b, w2a, w2b = weight(0, 2, F), weight(256, 3, HID), weight(1024, 2, F)
        w_gcn, w_res, w_mean = (weight(1280 + i * F, 1, F)[:, 0, :] for i in range(3))
        w_rel = [weight(1664 + i * RELS * F, RELS, F) for i in range(2)]
        w_root = [weight(2688 + i * F, 1, F)[:, 0, :] for i in range(2)]
        bias = sb("bias", [P, 11])
        B1B, B2A0, B2A1, GB, GBR, GAMMA, BETA, MB, RB1, RB2, U0 = range(11)
        b1a_row = sb("b1a_row", [P, HID])
        b2b_row = sb("b2b_row", [P, F])
        c2 = sb("c2", [P, 2])
        stat = sb("stat", [P, 32])
        MINL, MAXL, SLOW, FAST, STEP, WOFF, EPSC, NMEAN, SSQ, VAR, RSTD, SCALE, SHIFT, WMIN, WMAX, WNEG, RNDS, STDB, WMAXP, WNEGP, SLOWG, UNTIL = range(22)
        roundsi = sb("roundsi", [1, 2], I32)
        dsc = sb("dsc", [P, NT])
        dtmp = sb("dtmp", [P, NT])
        node_deg, node_some = sb("node_deg", [P, NP // P]), sb("node_some", [P, NP // P])
        bn = sb("bn", [P, 2, CT, 6])
        mv = sb("mv", [P, 2, CT, 2])
        std = sb("std", [P, 2, CT])
        bn_row = sb("bn_row", [P, NT, 6])
        bn_y = sb("bn_y", [P, BLKS, 6])
        mv_y = sb("mv_y", [P, 2])
        bound = sb("bound", [P, 1])
        count = sb("count", [P, GROUPS])
        rstd = sb("rstd", [P, 2, CT])
        row_mean, row_half, row_var, row_std, row_rstd, row_shift = (
            sb(f"row_{x}", [P, NT]) for x in ("mean", "half", "var", "std", "rstd", "shift"))

        work = sb("work", [P, 12800])

        def view(at, *shape):
            size = int(np.prod(shape))
            names = "abc"[:len(shape)]
            return work[:, at:at + size].rearrange(
                f"p ({' '.join(names)}) -> p {' '.join(names)}", **dict(zip(names, shape)))

        gat0 = view(0, SLOTS0, U, HID)
        hid = view(4096, SLOTS0, U * HID)
        ea = view(8192, SLOTS0, GE)
        hot = view(10240, HOTS, U * WIN)
        hot_lo = work[:, 11264:12288].bitcast(BF16).rearrange("p (s u w) -> p s u w", s=HOTS, u=U)
        hot_hi = work[:, 12288:12288 + HOTS * U * NT // 2].bitcast(BF16).rearrange("p (s u w) -> p s u w", s=HOTS, u=U)
        gat = view(0, SLOTS, U, F)
        b_rows = view(4096, BT, F)
        b_xT = view(4352, BLK)
        b_u = view(4608, BLK)
        b_v = view(4864, BLK)
        b_w = view(5120, BLK)
        b_mean = view(5376, BLK)
        b_sum = view(5632, BT, F)
        b_rel = view(5888, BT, RELS * F)
        b_bn = view(6912, 2, CH)
        aggT = view(3840, 2, CH)
        xT = view(5120, 2, CH)
        h2T = view(6400, 2, 2 * CH)
        xT0 = view(5120, 4, CH)
        pre_rows = view(0, 4, CT, HID)
        xb = view(8960, 2, CH)
        tsum = view(10240, 2, CT, F)
        rows = view(11520, 2, CT, F)
        ratio = view(8960, 2, CH)
        staging_d = view(10240, TILES).bitcast(I32)
        staging_c = view(11072, GROUPS).bitcast(I32)

        bank = [ctx.enter_context(nc.psum_tensor(f"bank{i}", [P, 512], F32)) for i in range(8)]
        HIST = 6

        s_idx, s_idx2, s_param, s_weight = sem("s_idx"), sem("s_idx2"), sem("s_param"), sem("s_weight")
        s_const, s_ident, s_prep, s_vote, s_all = sem("s_const"), sem("s_ident"), sem("s_prep"), sem("s_vote"), sem("s_all")
        s_acc, s_sources = sem("s_acc"), sem("s_sources")
        s_rounds, s_until, s_ends, s_ends_row = sem("s_rounds"), sem("s_until"), sem("s_ends"), sem("s_ends_row")
        gate = sem("gate")
        idx_ready = sems("idx_ready", 5)
        gathered0, gathered = sems("gathered0_", SLOTS0), sems("gathered", SLOTS)
        hot_ready, seg_done, accumulated = sems("hot_ready", 5), sems("seg_done", 5), sems("accumulated", 5)
        setup_step = sems("setup_step", 5)
        pass_done, acc_zero, cleared = sem("pass_done"), sem("acc_zero"), sem("cleared")
        table_stored = [sems(f"table{p}_stored", (4, 2, 1, 1, 1)[p]) for p in range(5)]
        STORED = [None, 16 * CHUNKS // 2, 16 * CHUNKS, 16 * BLKS, 16 * BLKS]
        ea_ready = sems("ea_ready", SLOTS0)
        pre_done, pre_added, relu_done = sem("pre_done"), sem("pre_added"), sem("relu_done")
        block = ctx.enter_context(nc.Block())

        def chunks(eng, body):
            body(0, 0, False)
            body(1, 1, False)
            with eng.Fori(1, CHUNKS // 2 - 1) as it:
                body(it * 2, 0, False)
                body(it * 2 + 1, 1, False)
            body(CHUNKS - 2, 0, False)
            body(CHUNKS - 1, 1, True)

        def blocks(eng, body):
            body(0, False)
            with eng.Fori(1, BLKS - 1) as k:
                body(k, False)
            body(BLKS - 1, True)

        def bcols(k):
            return bass.ds(k * BLK, BLK)

        def X_rows(k):
            return X[:, bass.ds(k * BT, BT), :]

        def later(k, n):
            return not isinstance(k, int) or k >= n

        def quads(eng, body, between=None):
            for j in range(2):
                body(j, j + 2, 1)
            if between:
                between()
            with eng.Fori(0, STEPS) as it:
                for j in range(4):
                    body(it * 4 + (j + 2), j, it + (1 if j < 2 else 2))

        STEPS = (CHUNKS - 2) // 4
        USES = (STEPS, STEPS, STEPS + 1, STEPS + 1)

        def cols(k, sub=None):
            return bass.ds(k * CH, CH) if sub is None else bass.ds(k * CH + sub * SUB, SUB)

        def node_rows(table, k):
            return table.rearrange("(t p) c -> p t c", p=P)[:, bass.ds(k * CT, CT), :]

        def block_rows(table, k):
            return table.rearrange("(t p) c -> p t c", p=P)[:, bass.ds(k * BT, BT), :]

        xT0_ready = sems("xT0_ready", 4)
        y_done, y_added = sem("y_done"), sem("y_added")

        def start_sp(sp):
            sp.dma_start(w1a[:, :, :], W1a.rearrange("(c p) n -> p c n", p=P)).then_inc(s_weight, 16)
            sp.dma_start(b1a_row[:, :], b1a.partition_broadcast(P)).then_inc(s_weight, 16)

            def load(k, slot, use):
                sp.wait_ge(y_done, k + 1)
                sp.sem_inc(gate, 1)
                sp.dma_start(xT0[:, slot, :], x_cols[:, cols(k)]).then_inc(xT0_ready[slot], 16)
            quads(sp, load)

        def start_act_loads(act):
            act.dma_start(local[:, :].bitcast(I32), dst).then_inc(s_idx, 16)
            act.dma_start(staging_c, first.partition_broadcast(P)).then_inc(s_idx, 16)
            act.dma_start(ew[:, :], eweight).then_inc(s_idx, 16)

        def start_act_sources(act):
            act.dma_start(srci[:, :], src).then_inc(s_idx2, 16)
            act.dma_start(reli[:, 0:TILES], etype).then_inc(s_idx2, 16)

        def start_act_params(act):
            act.dma_start(bias[:, :], biases).then_inc(s_param, 16)
            act.dma_start(b2b_row[:, :], b2b.partition_broadcast(P)).then_inc(s_param, 16)
            act.dma_start(w_all[:, :], weights).then_inc(s_param, 16)
            act.dma_start(X[:, :, :], x_rows.rearrange("(t p) f -> p t f", p=P)).then_inc(s_param, 16)
        PARAMS = 16 * 4

        def start_pe(pe):
            pe.sem_inc(y_done, 4)
            pe.wait_ge(s_weight, 32)

            def body(k, slot, use):
                s = slot % 2
                pe.wait_ge(xT0_ready[slot], use * 16)
                pe.wait_ge(y_added, k * 3 + 3)
                for t in range(CT):
                    mm = pe.matmul(bank[3 * s + t // 2][:, t % 2 * HID:(t % 2 + 1) * HID], xT0[:, slot, t * P:(t + 1) * P],
                                   w1a[:, 0, :], start=True, stop=True)
                mm.then_inc(y_done, 1)
            quads(pe, body)

        def start_dve_rows(dve):
            dve.wait_ge(s_weight, 32)

            def body(k, slot, use):
                s = slot % 2
                dve.wait_ge(y_done, k + 5)
                dve.wait_ge(table_stored[0][slot], use * 16)
                for b in range(3):
                    n = 2 if b < 2 else 1
                    dve.tensor_tensor(pre_rows[:, slot, 2 * b:2 * b + n, :],
                                      bank[3 * s + b][:, 0:n * HID].rearrange("p (t h) -> p t h", t=n),
                                      b1a_row[:, :].unsqueeze(1).broadcast_to([P, n, HID]), ALU.add).then_inc(y_added, 1)
            quads(dve, body, lambda: start_dve_rounds(dve))

        def start_act_store(act):
            def body(k, slot, use):
                act.wait_ge(y_added, k * 3 + 9)
                act.dma_start(node_rows(tables[0], k), pre_rows[:, slot, :, :]).then_inc(table_stored[0][slot], 16)
            quads(act, body, lambda: start_act_sources(act))

        CONSTANTS = 9

        def start_pool(pool):
            pool.iota(staging_d[:, 0:P], pattern=[[1, P]], base=0, channel_multiplier=0).then_inc(s_const, 1)
            pool.memset(ident[:, :], 0.0).then_inc(s_const, 1)
            pool.memset(ones_b[:, :], 1.0).then_inc(s_const, 1)
            pool.memset(zeros_b[:, :], 0.0).then_inc(s_const, 1)
            pool.memset(stat[:, EPSC:EPSC + 1], EPS).then_inc(s_const, 1)
            pool.memset(basei[:, :], 0).then_inc(s_const, 1)
            pool.memset(ends[:, 0:1], 0).then_inc(s_const, 1)
            pool.iota(staging_d[:, P:P + GROUPS], pattern=[[1, GROUPS]], base=1, channel_multiplier=0).then_inc(s_const, 1)
            pool.iota(staging_d[:, 512:513], pattern=[[0, 1]], base=BLK, channel_multiplier=BLK).then_inc(s_const, 1)
            pool.wait_ge(s_const, 2)
            pool.affine_select(out=ident[:, :], in_=ident[:, :], compare_op=ALU.not_equal, fill=1.0, base=0,
                               pattern=[[-1, P]], channel_multiplier=1).then_inc(s_ident, 1)
            pool.wait_ge(s_vote, 3)
            RMAX = bass.bass_isa.ReduceOp.max
            pool.partition_all_reduce(stat[:, SLOW:SLOW + 1], stat[:, MAXL:MAXL + 1], P, RMAX).then_inc(s_all, 1)
            pool.partition_all_reduce(stat[:, WMAX:WMAX + 1], stat[:, WMAXP:WMAXP + 1], P, RMAX).then_inc(s_all, 1)
            pool.partition_all_reduce(stat[:, WNEG:WNEG + 1], stat[:, WNEGP:WNEGP + 1], P, RMAX).then_inc(s_all, 1)
            pool.memset(acc[:, :, :], 0.0).then_inc(s_acc, 1)

        prepared = [0]

        def done(dve, ins):
            prepared[0] += 1
            ins.then_inc(s_prep, 1)
            dve.wait_ge(s_prep, prepared[0])

        def start_dve_votes(dve):
            dve.sem_inc(y_added, 6)
            for stored in table_stored[0]:
                dve.sem_inc(stored, 16)
            dve.wait_ge(s_const, CONSTANTS)
            done(dve, dve.tensor_copy(iota[:, :], staging_d[:, 0:P]))
            done(dve, dve.tensor_copy(iota_b[:, :], staging_d[:, 0:P]))
            done(dve, dve.tensor_copy(count[:, :], staging_d[:, P:P + GROUPS]))
            done(dve, dve.tensor_copy(bound[:, :], staging_d[:, 512:513]))
            dve.wait_ge(s_idx, 48)
            done(dve, dve.tensor_scalar(dstf[:, :], local[:, :].bitcast(I32), float(FRONT), None, ALU.add))
            done(dve, dve.tensor_scalar(firstf[:, :], staging_c, float(FRONT), None, ALU.add))
            done(dve, dve.tensor_tensor(local[:, :].rearrange("p (g u) -> p g u", u=U),
                                        dstf[:, :].rearrange("p (g u) -> p g u", u=U),
                                        firstf[:, :].unsqueeze(2).broadcast_to([P, GROUPS, U]), ALU.subtract))
            done(dve, dve.tensor_reduce(stat[:, MINL:MINL + 1], local[:, :], AX_X, ALU.min))
            done(dve, dve.tensor_reduce(stat[:, MAXL:MAXL + 1], local[:, :], AX_X, ALU.max))
            done(dve, dve.tensor_scalar(stat[:, MINL:MINL + 1], stat[:, MINL:MINL + 1], -1.0, None, ALU.mult))
            done(dve, dve.tensor_scalar(stat[:, MAXL:MAXL + 1], stat[:, MAXL:MAXL + 1], 1.0 - WIN, stat[:, MINL:MINL + 1],
                                        ALU.add, ALU.max))
            done(dve, dve.tensor_reduce(stat[:, WMAXP:WMAXP + 1], ew[:, :], AX_X, ALU.max))
            done(dve, dve.tensor_reduce(stat[:, WMIN:WMIN + 1], ew[:, :], AX_X, ALU.min))
            done(dve, dve.tensor_scalar(stat[:, WNEGP:WNEGP + 1], stat[:, WMIN:WMIN + 1], -1.0, None, ALU.mult))
            dve.sem_inc(s_vote, 3)

        def start_dve_rounds(dve):
            dve.wait_ge(s_all, 3)
            done(dve, dve.tensor_scalar(stat[:, SLOW:SLOW + 1], stat[:, SLOW:SLOW + 1], 0.0, None, ALU.is_gt))
            done(dve, dve.tensor_scalar(stat[:, FAST:FAST + 1], stat[:, SLOW:SLOW + 1], -1.0, 1.0, ALU.mult, ALU.add))
            done(dve, dve.tensor_scalar(stat[:, STEP:STEP + 1], stat[:, SLOW:SLOW + 1], float(WIN), None, ALU.mult))
            done(dve, dve.tensor_scalar(stat[:, RNDS:RNDS + 1], stat[:, SLOW:SLOW + 1], float(WINDOWS - 1), 1.0, ALU.mult, ALU.add))
            done(dve, dve.tensor_copy(roundsi[:, 0:1], stat[0:1, RNDS:RNDS + 1]))
            dve.tensor_scalar(roundsi[:, 1:2], stat[0:1, RNDS:RNDS + 1], -1.0, None, ALU.add).then_inc(s_rounds, 1)
            done(dve, dve.scalar_tensor_tensor(count[:, :], firstf[:, :], bound[:, :], count[:, :], ALU.is_le, ALU.mult))
            done(dve, dve.tensor_reduce(stat[:, UNTIL:UNTIL + 1], count[:, :], AX_X, ALU.max))
            done(dve, dve.tensor_scalar(stat[:, SLOWG:SLOWG + 1], stat[:, SLOW:SLOW + 1], float(GROUPS), None, ALU.mult))
            done(dve, dve.tensor_scalar(stat[:, UNTIL:UNTIL + 1], stat[:, UNTIL:UNTIL + 1], stat[:, SLOWG:SLOWG + 1],
                                        float(SLOTS - 1), ALU.max, ALU.add))
            done(dve, dve.tensor_copy(until[:, 0:1], stat[:, UNTIL:UNTIL + 1]))
            dve.tensor_scalar(until[:, 1:2], until[:, 0:1], SLOTS.bit_length() - 1, None,
                              ALU.logical_shift_right).then_inc(s_until, 1)

        def start_dve_edges(dve):
            dve.wait_ge(s_idx2, 32)
            done(dve, dve.tensor_scalar(srci[:, :], srci[:, :], float(FRONT), None, ALU.add))
            dve.sem_inc(s_sources, 1)
            done(dve, dve.tensor_scalar(staging_d, srci[:, 0:TILES], 7, None, ALU.logical_shift_right))
            done(dve, dve.tensor_copy(src_hi[:, :], staging_d))
            done(dve, dve.tensor_scalar(staging_d, srci[:, 0:TILES], P - 1, None, ALU.bitwise_and))
            done(dve, dve.tensor_copy(src_lo[:, :], staging_d))
            done(dve, dve.scalar_tensor_tensor(reli[:, 0:TILES], srci[:, 0:TILES], float(RELS), reli[:, 0:TILES], ALU.mult, ALU.add))
            done(dve, dve.tensor_copy(reli[:, TILES:], reli[:, 0:SLOTS * U]))
            done(dve, dve.tensor_tensor(stat[:, WMAX:WMAX + 1], stat[:, WMAX:WMAX + 1], stat[:, WNEG:WNEG + 1], ALU.add))
            done(dve, dve.tensor_scalar(stat[:, WMAX:WMAX + 1], stat[:, WMAX:WMAX + 1], 1e-8, None, ALU.add))
            done(dve, dve.reciprocal(stat[:, WMAX:WMAX + 1], stat[:, WMAX:WMAX + 1]))
            done(dve, dve.tensor_scalar(ew[:, :], ew[:, :], stat[:, WNEG:WNEG + 1], stat[:, WMAX:WMAX + 1], ALU.add, ALU.mult))

        def start_sp_ends(sp):
            sp.wait_ge(s_until, 1)
            sp.dma_start(ends_row, until[0:BLKS, 1:2]).then_inc(s_ends_row, 16)
            sp.wait_ge(s_ends_row, 16)
            sp.dma_start(ends[0:1, 1:], ends_row.rearrange("b o -> o b")).then_inc(s_ends, 16)

        def load_rounds(eng):
            eng.wait_ge(s_rounds, 1)
            return (eng.value_load(roundsi[0:1, 0:1], min_val=1, max_val=WINDOWS),
                    eng.value_load(roundsi[0:1, 1:2], min_val=0, max_val=WINDOWS - 1))

        def idx_of(p):
            return reli if p >= 3 else srci

        def pass_pool(pool, p, rounds):
            into, slots, iters, width = (gat0, SLOTS0, ITERS0, HID) if p == 0 else (gat, SLOTS, ITERS, F)
            if p:
                pool.wait_ge(idx_ready[p - 1], rounds * GROUPS + (SLOTS0 if p == 1 else SLOTS))
                pool.sem_inc(gate, 1)
                pool.tensor_copy(slot_idx[:, :, :], idx_of(p)[:, 0:SLOTS * U].rearrange("p (s u) -> p s u", u=U)
                                 ).then_inc(idx_ready[p], SLOTS)
            for slot, s in enumerate(table_stored[p]):
                pool.wait_ge(s, STORED[p] if p else (USES[slot] + 1) * 16)
                pool.sem_inc(gate, 1)

            with pool.Fori(0, rounds) as r:
                with pool.Fori(0, iters) as it:
                    n = (r * iters + it) * slots
                    for q in range(slots):
                        pool.wait_ge(idx_ready[p], n + q + 1)
                        pool.sem_inc(gate, 1)
                        if p == 0:
                            pool.wait_ge(relu_done, (n + q) * 2 + 2)
                            pool.sem_inc(gate, 1)
                        for u in range(U):
                            pool.indirect_dma_start(
                                into[:, q, u, 0:width], None, tables[p],
                                bass.IndirectOffsetOnAxis(ap=slot_idx[:, q, u:u + 1].bitcast(U32), axis=0),
                            ).then_inc((gathered if p else gathered0)[q], 16)

        def round_setup(dve, p, r, lead):
            s = setup_step[p]
            dve.wait_ge(s, r * 4 + 1)
            dve.tensor_scalar(base[:, :], firstf[:, :], stat[:, FAST:FAST + 1], stat[:, WOFF:WOFF + 1],
                              ALU.mult, ALU.add).then_inc(s, 1)
            dve.wait_ge(s, r * 4 + 2)
            dve.tensor_tensor(local[:, :].rearrange("p (g u) -> p g u", u=U),
                              dstf[:, :].rearrange("p (g u) -> p g u", u=U),
                              base[:, :].unsqueeze(2).broadcast_to([P, GROUPS, U]), ALU.subtract).then_inc(s, 1)
            dve.tensor_copy(basei[:, lead:lead + GROUPS], base[0:1, :]).then_inc(s, 1)
            dve.wait_ge(s, r * 4 + 4)
            dve.tensor_tensor(stat[:, WOFF:WOFF + 1], stat[:, WOFF:WOFF + 1], stat[:, STEP:STEP + 1],
                              ALU.add).then_inc(s, 1)
            dve.wait_ge(s, r * 4 + 5)
            dve.sem_inc(gate, 1)

        def load_bases(dve, it, slots):
            return nc.values_load_multi_w_load_instructions(
                basei[0:1, bass.ds(it * slots, slots)], engines=[mybir.EngineType.DVE], min_val=0, max_val=NP)[1]

        def one_hot(dve, p, g, n, q):
            dve.wait_ge(seg_done[p], n + 1)
            hq = q % HOTS
            mine = local[:, bass.ds(g * U, U)]
            ins = dve.tensor_tensor(hot[:, hq, :].rearrange("p (u w) -> p u w", u=U),
                                    iota[:, 0:WIN].unsqueeze(1).broadcast_to([P, U, WIN]),
                                    mine.unsqueeze(2).broadcast_to([P, U, WIN]), ALU.is_equal)
            if p == 0:
                dve.tensor_tensor(hot_hi[:, hq, :, :], iota[:, 0:NT].unsqueeze(1).broadcast_to([P, U, NT]),
                                  src_hi[:, bass.ds(g * U, U)].unsqueeze(2).broadcast_to([P, U, NT]), ALU.is_equal)
                for u in range(U):
                    ins = dve.tensor_scalar(hot_lo[:, hq, u, :], iota_b[:, :], src_lo[:, bass.ds(g * U + u, 1)], None,
                                            ALU.is_equal)
            ins.then_inc(hot_ready[p], 1)

        def weighted_hot(dve, p, g, n, q):
            dve.wait_ge(seg_done[p], n + 1)
            for u in range(U):
                ins = dve.tensor_scalar(hot[:, q % HOTS, u * WIN:(u + 1) * WIN], iota[:, 0:WIN], local[:, bass.ds(g * U + u, 1)],
                                        ew[:, bass.ds(g * U + u, 1)], ALU.is_equal, ALU.mult)
            ins.then_inc(hot_ready[p], 1)

        def accumulate(dve, p, at, n, q, ago=0):
            planes = 3 if p == 0 else 1
            there = acc[:, 0:planes, bass.ds(at, WIN)]
            dve.wait_ge(seg_done[p], n + (1 + PRIME_SLOT - ago))
            dve.wait_ge(accumulated[p], n + (PRIME_BANK - ago))
            dve.tensor_tensor(there, there, bank[4 + q % 2][:, 0:planes * WIN].rearrange("p (c w) -> p c w", c=planes),
                              ALU.add).then_inc(accumulated[p], 1)

        def pass0_dve(dve, rounds):
            dve.sem_inc(accumulated[0], PRIME_BANK)
            dve.memset(stat[:, WOFF:WOFF + 1], 0.0).then_inc(setup_step[0], 1)
            dve.sem_inc(pre_added, PRIME_PAIR)
            dve.wait_ge(s_acc, 1)

            def body(r, it, first=False):
                m = r * ITERS0 + it
                n = m * SLOTS0
                at = load_bases(dve, it, SLOTS0)
                for q in range(SLOTS0):
                    one_hot(dve, 0, it * SLOTS0 + q, n + q, q)
                    if not first or q >= LAG:
                        accumulate(dve, 0, at[q], n, q, LAG - q)
                    for h in range(2):
                        g = gat0[:, q, 2 * h:2 * h + 2, :].rearrange("p u c -> p (u c)")
                        dve.wait_ge(gathered0[q], (m + 1) * 16 * U)
                        dve.wait_ge(pre_done, (n + q) * 2 + h + 1 + 2 * SLOTS0)
                        dve.tensor_tensor(g, g, bank[q % 2 * 2 + h][:, :], ALU.add).then_inc(pre_added, 1)

            with dve.Fori(0, rounds) as r:
                round_setup(dve, 0, r, LAG)
                body(r, 0, True)
                with dve.Fori(1, ITERS0) as it:
                    body(r, it)
                at = load_bases(dve, ITERS0, SLOTS0)
                for q in range(LAG):
                    accumulate(dve, 0, at[q], (r + 1) * GROUPS, q, LAG - q)
                dve.wait_ge(hot_ready[0], (r + 1) * GROUPS)
                dve.tensor_scalar(src_lo[:, :], src_lo[:, :], 0.0, -1.0, ALU.mult, ALU.add)
            dve.wait_ge(accumulated[0], rounds * GROUPS + PRIME_BANK)
            dve.sem_inc(pass_done, 1)

        def pass0_pe(pe, rounds):
            pe.sem_inc(seg_done[0], PRIME_SLOT)
            pe.sem_inc(pre_done, 2 * SLOTS0)
            pe.wait_ge(s_const, CONSTANTS)
            pe.matmul(bank[HIST][:, 0:NT], zeros_b[:, :], zeros_b[:, 0:NT], start=True, stop=False, skip_group_check=True)

            def pre(m, n, q):
                slot = q % SLOTS0
                pe.wait_ge(ea_ready[slot], (m + q // SLOTS0 + 1) * 16)
                for h in range(2):
                    pe.wait_ge(pre_added, (n + q) * 2 + h + 1)
                    for j in range(2):
                        u = 2 * h + j
                        mm = pe.matmul(bank[q % 2 * 2 + h][:, j * HID:(j + 1) * HID], ea[:, slot, u * P:(u + 1) * P],
                                       w1a[:, 1, :], start=True, stop=True)
                    mm.then_inc(pre_done, 1)

            def segment_sum(n, q):
                pe.wait_ge(relu_done, n * 2 + 2 + 2 * SLOTS0)
                pe.wait_ge(hot_ready[0], n + 1)
                pe.wait_ge(accumulated[0], n + 1)
                into = bank[4 + q % 2]
                for c in range(2):
                    for u in range(U):
                        pe.matmul(into[:, c * WIN:(c + 1) * WIN], hid[:, q, u * HID + c * F:u * HID + (c + 1) * F],
                                  hot[:, q, u * WIN:(u + 1) * WIN], start=(u == 0), stop=(u == U - 1))
                upper = hot[:, q, :].bitcast(BF16).rearrange("p (u w t) -> p u w t", u=U, t=2)
                for u in range(U):
                    pe.matmul(into[:, 2 * WIN:3 * WIN], ones_b[:, :], upper[:, u, :, 1], start=(u == 0), stop=(u == U - 1))
                for u in range(U):
                    mm = pe.matmul(bank[HIST][:, 0:NT], hot_lo[:, q, u, :], hot_hi[:, q, u, :], start=False, stop=False,
                                   skip_group_check=True)
                mm.then_inc(seg_done[0], 1)

            def body(r, it, last=False):
                m = r * ITERS0 + it
                n = m * SLOTS0
                for q in range(SLOTS0):
                    segment_sum(n + q, q)
                    if not last or q + LAG < SLOTS0:
                        pre(m, n, q + LAG)

            with pe.Fori(0, rounds) as r:
                for q in range(LAG):
                    pre(r * ITERS0, r * GROUPS, q)
                with pe.Fori(0, ITERS0 - 1) as it:
                    body(r, it)
                body(r, ITERS0 - 1, True)

        def pass0_act(act, rounds):
            act.sem_inc(relu_done, 2 * SLOTS0)
            act.wait_ge(s_sources, 1)
            for q in range(SLOTS0):
                act.copy(slot_idx[:, q, :], srci[:, q * U:(q + 1) * U]).then_inc(idx_ready[0], 1)
            start_act_params(act)
            act.preload_act_table(ACT.Relu)
            with act.Fori(0, rounds) as r:
                with act.Fori(0, ITERS0) as it:
                    m = r * ITERS0 + it
                    n = m * SLOTS0
                    for q in range(SLOTS0):
                        for h in range(2):
                            act.wait_ge(pre_added, (n + q) * 2 + h + 1 + PRIME_PAIR)
                            act.wait_ge(seg_done[0], n + q + 1)
                            act.activation(hid[:, q, h * 2 * HID:(h + 1) * 2 * HID],
                                           gat0[:, q, 2 * h:2 * h + 2, :].rearrange("p u c -> p (u c)"),
                                           ACT.Relu).then_inc(relu_done, 1)
                        act.wait_ge(gathered0[q], (m + 1) * 16 * U)
                        act.sem_inc(gate, 1)
                        act.copy(slot_idx[:, q, :], srci[:, bass.ds((it * SLOTS0 + SLOTS0 + q) * U, U)]
                                 ).then_inc(idx_ready[0], 1)

        def pass0_sp(sp, rounds):
            with sp.Fori(0, rounds) as r:
                with sp.Fori(0, ITERS0) as it:
                    n = (r * ITERS0 + it) * SLOTS0
                    for q in range(SLOTS0):
                        sp.wait_ge(pre_done, (n + q) * 2 + 2)
                        sp.sem_inc(gate, 1)
                        sp.dma_start(ea[:, q, :], ea_cols[:, bass.ds((it * SLOTS0 + q) * GE, GE)]).then_inc(ea_ready[q], 16)

        def segments(eng, before, step, node, each_round=None):
            with eng.If(before > 0):
                with eng.Fori(0, before) as r:
                    if each_round:
                        each_round(r)
                    with eng.Fori(0, ITERS) as it:
                        step(it, r * ITERS + it)
            if each_round:
                each_round(before)

            def segment(k, last):
                lo = eng.value_load(ends[0:1, bass.ds(k, 1)], min_val=0, max_val=ITERS)
                hi = eng.value_load(ends[0:1, bass.ds(k + 1, 1)], min_val=0, max_val=ITERS)
                with eng.If(lo < hi):
                    with eng.Fori(lo, hi) as it:
                        step(it, before * ITERS + it)
                node(k, last, before * ITERS + hi)
            blocks(eng, segment)

        def pass_dve(dve, p, before, node):
            dve.sem_inc(accumulated[p], PRIME_BANK)
            dve.memset(stat[:, WOFF:WOFF + 1], 0.0).then_inc(setup_step[p], 1)
            if p == 1:
                dve.wait_ge(s_ends, 16)
                dve.wait_ge(acc_zero, 1)
            else:
                dve.wait_ge(cleared, (p - 1) * BLKS)

            def step(it, m):
                n = m * SLOTS
                at = load_bases(dve, it, SLOTS)
                for q in range(SLOTS + LAG):
                    if q < SLOTS:
                        (weighted_hot if p >= 3 else one_hot)(dve, p, it * SLOTS + q, n + q, q)
                    if q >= LAG:
                        done = q - LAG
                        dve.wait_ge(seg_done[p], n + (done + 1 + PRIME_SLOT))
                        dve.tensor_copy(slot_idx[:, done, :], idx_of(p)[:, bass.ds((it * SLOTS + SLOTS + done) * U, U)]
                                        ).then_inc(idx_ready[p], 1)
                        accumulate(dve, p, at[done], n + done, done)

            def block(k, last, steps):
                dve.wait_ge(accumulated[p], steps * SLOTS + PRIME_BANK)
                dve.sem_inc(gate, 1)
                node(dve, k, last)
            segments(dve, before, step, block, lambda r: round_setup(dve, p, r, 0))

        def clear(dve, k):
            dve.sem_inc(gate, 1)
            dve.tensor_copy(acc[:, 0, bcols(k)].rearrange("p (t c) -> p t c", t=BT),
                            zeros_b[:, :].unsqueeze(1).broadcast_to([P, BT, P])).then_inc(cleared, 1)

        def pass_pe(pe, p, before, node):
            steps = (before + 1) * ((p - 1) * ITERS)
            pe.sem_inc(seg_done[p], PRIME_SLOT)
            if p == 1:
                pe.wait_ge(s_ends, 16)

            def step(it, m):
                n = m * SLOTS
                for q in range(SLOTS):
                    pe.wait_ge(gathered[q], (steps + m + 1) * 16 * U)
                    pe.wait_ge(hot_ready[p], n + q + 1)
                    pe.wait_ge(accumulated[p], n + q + 1)
                    for u in range(U):
                        mm = pe.matmul(bank[4 + q % 2][:, 0:WIN], gat[:, q, u, :], hot[:, q % HOTS, u * WIN:(u + 1) * WIN],
                                       start=(u == 0), stop=(u == U - 1))
                    mm.then_inc(seg_done[p], 1)

            segments(pe, before, step, lambda k, last, steps: node(pe, k, last))

        def norm_stats(dve, step, k, s, tiles, x_of):
            for j in range(tiles):
                ins = dve.bn_stats(bn[:, s, j, :], x_of(j))
            ins.then_inc(step, 1)
            dve.wait_ge(step, k * 4 + 1)
            dve.sem_inc(gate, 1)
            for j in range(tiles):
                ins = dve.bn_aggr(mv[:, s, j, :], bn[:, s, j, :])
            ins.then_inc(step, 1)

        def norm_root(act, step, root, k, s, tiles):
            act.wait_ge(step, k * 4 + 2)
            act.activation(std[:, s, 0:tiles], mv[:, s, 0:tiles, 1], ACT.Sqrt, bias=stat[:, EPSC:EPSC + 1]).then_inc(root, 1)

        def norm_apply(dve, step, root, k, s, tiles, x_of, to):
            dve.wait_ge(root, k + 1)
            dve.reciprocal(rstd[:, s, 0:tiles], std[:, s, 0:tiles]).then_inc(step, 1)
            dve.wait_ge(step, k * 4 + 3)
            for j in range(tiles):
                ins = dve.tensor_scalar(to(j), x_of(j), mv[:, s, j, 0:1], rstd[:, s, j:j + 1], ALU.subtract, ALU.mult)
            ins.then_inc(step, 1)

        def x_row(t):
            return X[:, bass.ds(t, 1), :].rearrange("p o f -> p (o f)")

        (n0_agg, n0_scaled, n0_aggT, n0_hid, n0_relu, n0_out, n0_step, n0_root, n0_deg, n0_rows, n0_c2, n0_dsc, n0_sum, n0_x) = (
            sem(f"n0_{x}") for x in ("agg", "scaled", "aggT", "hid", "relu", "out", "step", "root", "deg", "rows", "c2", "dsc", "sum", "x"))
        n0_inv, n0_deg_row, n0_node_deg, n0_inv_row, n0_spread = (
            sem(f"n0_{x}") for x in ("inv", "deg_row", "node_deg", "inv_row", "spread"))
        n0_xT = sems("n0_xT", 2)

        TILES_IN = ((0, 3, 6), (3, 2, 7))

        def node0_sp(sp):
            sp.wait_ge(pass_done, 1)

            def load(k, s, last):
                if later(k, 2):
                    sp.wait_ge(n0_hid, k - 1)
                sp.sem_inc(gate, 1)
                sp.dma_start(xT[:, s, :], x_cols[:, cols(k)]).then_inc(n0_xT[s], 16)
            chunks(sp, load)

        def node0_pool(pool):
            def store(k, s, last):
                if last:
                    pool.wait_ge(n0_agg, CHUNKS)
                    pool.sem_inc(gate, 1)
                    pool.memset(acc[:, 0, :], 0.0).then_inc(acc_zero, 1)
                pool.wait_ge(n0_rows, k + 1)
                pool.sem_inc(gate, 1)
                pool.dma_start(node_rows(tables[1], k), rows[:, s, :, :]).then_inc(table_stored[1][s], 16)
            chunks(pool, store)

        def node0_pe(pe):
            pe.wait_ge(s_param, PARAMS)
            pe.wait_ge(s_ident, 1)
            pe.wait_ge(pass_done, 1)
            for c in range(2):
                mm = pe.matmul(bank[7][:, c:c + 1], w2a[:, 2, c * F:(c + 1) * F], bias[:, U0:U0 + 1], start=True, stop=True)
            mm.then_inc(n0_c2, 1)

            def agg(k):
                if later(k, 1):
                    pe.wait_ge(n0_scaled, k * 2)
                for sub in range(2):
                    for c in range(2):
                        mm = pe.matmul(bank[sub][:, 0:SUB], w1b[:, c, :], acc[:, c, cols(k, sub)], start=(c == 0), stop=(c == 1))
                mm.then_inc(n0_agg, 1)

            def body(k, s, last):
                pe.wait_ge(n0_xT[s], (k - s) * 8 + 16)
                if later(k, 1):
                    pe.wait_ge(n0_relu, k * 4)
                for c in range(2):
                    for sub in range(2):
                        pe.matmul(bank[2 + 2 * c + sub][:, 0:SUB], w2a[:, 0, c * F:(c + 1) * F],
                                  xT[:, s, sub * SUB:(sub + 1) * SUB], start=True, stop=False)
                pe.wait_ge(n0_aggT, k * 2 + 2)
                for c in range(2):
                    for sub in range(2):
                        mm = pe.matmul(bank[2 + 2 * c + sub][:, 0:SUB], w2a[:, 1, c * F:(c + 1) * F],
                                       aggT[:, s, sub * SUB:(sub + 1) * SUB], start=False, stop=True)
                mm.then_inc(n0_hid, 1)
                if not last:
                    agg(k + 1)
                pe.wait_ge(n0_relu, k * 4 + 4)
                if later(k, 1):
                    pe.wait_ge(n0_sum, k * 2)
                else:
                    pe.wait_ge(n0_dsc, 1)
                for t0, n, b in TILES_IN:
                    for j in range(n):
                        for c in range(2):
                            at = c * CH + (t0 + j) * P
                            mm = pe.matmul(bank[b][:, j * F:(j + 1) * F], h2T[:, s, at:at + P], w2b[:, c, :],
                                           start=(c == 0), stop=(c == 1))
                mm.then_inc(n0_out, 1)
            agg(0)
            chunks(pe, body)

        def node0_act(act):
            def scaled(k, s):
                act.wait_ge(n0_step, k * 4 + 4)
                if later(k, 2):
                    act.wait_ge(table_stored[1][s], (k - s) * 8)
                act.sem_inc(gate, 1)
                for j in range(CT):
                    t = k * CT + j
                    ins = act.activation(rows[:, s, j, :], x_row(t), ACT.Copy, scale=dsc[:, bass.ds(t, 1)])
                ins.then_inc(n0_rows, 1)

            def body(k, s, last):
                if later(k, 1):
                    norm_root(act, n0_step, n0_root, k - 1, 1 - s, CT)
                act.wait_ge(n0_hid, k + 1)
                for c in range(2):
                    for sub in range(2):
                        act.activation(h2T[:, s, c * CH + sub * SUB:c * CH + (sub + 1) * SUB],
                                       bank[2 + 2 * c + sub][:, 0:SUB], ACT.Relu, bias=c2[:, c:c + 1]).then_inc(n0_relu, 1)
                if later(k, 1):
                    scaled(k - 1, 1 - s)
                if last:
                    norm_root(act, n0_step, n0_root, k, s, CT)
                    scaled(k, s)
            act.wait_ge(pass_done, 1)
            act.dma_start(deg_row.rearrange("(o n) -> o n", o=1), acc[0:1, 2, 0:NP]).then_inc(n0_deg_row, 16)
            act.preload_act_table(ACT.Sqrt)
            act.wait_ge(n0_deg_row, 16)
            act.dma_start(node_deg[:, :], deg_row.rearrange("(p t) -> p t", p=P)).then_inc(n0_node_deg, 16)
            act.wait_ge(n0_dsc, 1)
            act.activation(dtmp[:, :], dsc[:, :], ACT.Sqrt).then_inc(n0_dsc, 1)
            act.wait_ge(n0_inv, 6)
            act.dma_start(inv_row.rearrange("(p t) -> p t", p=P), node_deg[:, :]).then_inc(n0_inv_row, 16)
            act.wait_ge(n0_inv_row, 16)
            act.dma_start(acc[:, 2, CH:2 * CH], inv_row[CH:2 * CH].partition_broadcast(P)).then_inc(n0_spread, 16)
            act.wait_ge(n0_spread, 16)
            act.dma_start(acc[:, 2, 2 * CH:NP], inv_row[2 * CH:NP].partition_broadcast(P)).then_inc(n0_spread, 16)
            act.wait_ge(n0_dsc, 3)
            chunks(act, body)

        def node0_dve(dve):
            dve.wait_ge(s_param, PARAMS)
            dve.wait_ge(n0_c2, 1)
            dve.tensor_tensor(c2[:, :], bank[7][:, 0:2], bias[:, B2A0:B2A1 + 1], ALU.add)
            dve.tensor_scalar(dsc[:, :], bank[HIST][:, 0:NT], 1.0, None, ALU.max).then_inc(n0_dsc, 1)

            def inverse(deg, some, step):
                dve.tensor_scalar(some, deg, 1.0, None, ALU.min)
                dve.tensor_scalar(deg, deg, 1.0, None, ALU.max).then_inc(n0_inv, 1)
                dve.wait_ge(n0_inv, step + 1)
                dve.reciprocal(deg, deg).then_inc(n0_inv, 1)
                dve.wait_ge(n0_inv, step + 2)
                dve.tensor_tensor(deg, deg, some, ALU.mult).then_inc(n0_inv, 1)

            def biased(k, s):
                if not later(k, 1):
                    dve.wait_ge(n0_inv, 3)
                else:
                    dve.wait_ge(n0_spread, 32 if later(k, 2) else 16)
                if later(k, 2):
                    dve.wait_ge(n0_aggT, k * 2 - 2)
                dve.tensor_scalar(ratio[:, s, :], acc[:, 2, cols(k)], 0.0, bias[:, B1B:B1B + 1], ALU.is_gt, ALU.mult).then_inc(n0_deg, 1)
                x = X[:, bass.ds(k * CT, CT), :]
                dve.tensor_tensor(x, x, b2b_row[:, :].unsqueeze(1).broadcast_to([P, CT, F]), ALU.add).then_inc(n0_x, 1)

            def mean_of(k, s):
                dve.wait_ge(n0_agg, k + 1)
                dve.wait_ge(n0_deg, k + 1)
                if later(k, 2):
                    dve.wait_ge(n0_hid, k - 1)
                for sub in range(2):
                    dve.tensor_tensor(aggT[:, s, sub * SUB:(sub + 1) * SUB], bank[sub][:, 0:SUB], acc[:, 2, cols(k, sub)],
                                      ALU.mult).then_inc(n0_scaled, 1)
                for sub in range(2):
                    half = slice(sub * SUB, (sub + 1) * SUB)
                    dve.wait_ge(n0_scaled, k * 2 + sub + 1)
                    dve.tensor_tensor(aggT[:, s, half], aggT[:, s, half], ratio[:, s, half], ALU.add).then_inc(n0_aggT, 1)

            def applied(k, s):
                norm_apply(dve, n0_step, n0_root, k, s, CT, lambda j: tsum[:, s, j, :], lambda j: x_row(k * CT + j))

            def body(k, s, last):
                if not last:
                    biased(k + 1, 1 - s)
                    mean_of(k + 1, 1 - s)
                if later(k, 1):
                    applied(k - 1, 1 - s)
                dve.wait_ge(n0_out, k + 1)
                dve.wait_ge(n0_x, k + 1)
                for t0, n, b in TILES_IN:
                    dve.tensor_tensor(tsum[:, s, t0:t0 + n, :], bank[b][:, 0:n * F].rearrange("p (t f) -> p t f", f=F),
                                      X[:, bass.ds(k * CT + t0, n), :], ALU.add).then_inc(n0_sum, 1)
                dve.wait_ge(n0_sum, k * 2 + 2)
                norm_stats(dve, n0_step, k, s, CT, lambda j: tsum[:, s, j, :])
                if last:
                    applied(k, s)
            dve.wait_ge(n0_deg_row, 16)
            inverse(acc[:, 2, 0:CH], ratio[:, 1, :], 0)
            biased(0, 0)
            dve.wait_ge(n0_node_deg, 16)
            inverse(node_deg[:, :], node_some[:, :], 3)
            mean_of(0, 0)
            dve.wait_ge(n0_dsc, 2)
            dve.reciprocal(dsc[:, :], dtmp[:, :]).then_inc(n0_dsc, 1)
            chunks(dve, body)

        (n1_row, n1_turn, n1_xT, n1_res, n1_rs, n1_mean, n1_mm, n1_relu, n1_y, n1_bn, n1_one) = (
            sem(f"n1_{x}") for x in ("row", "turn", "xT", "res", "rs", "mean", "mm", "relu", "y", "bn", "one"))

        def node1_act(act):
            act.wait_ge(n0_step, CHUNKS * 4)
            act.wait_ge(n0_spread, 32)
            act.preload_act_table(ACT.Sqrt)

            def block(k, last):
                if later(k, 1):
                    act.wait_ge(n1_turn, k)
                    act.sem_inc(gate, 1)
                act.activation(b_rows, X_rows(k), ACT.Copy).then_inc(n1_row, 1)
                if later(k, 1):
                    act.wait_ge(n1_mean, k)
                    act.sem_inc(gate, 1)
                act.activation(b_w, acc[:, 2, bcols(k)], ACT.Sqrt).then_inc(n1_rs, 1)
                act.wait_ge(n1_turn, k + 1)
                act.sem_inc(gate, 1)
                act.activation(b_xT, bank[0][:, 0:BLK], ACT.Copy).then_inc(n1_xT, 1)
                act.wait_ge(n1_res, k + 1)
                if later(k, 1):
                    act.wait_ge(n1_y, k)
                act.activation(b_u, bank[1][:, 0:BLK], ACT.Relu, bias=bias[:, GBR:GBR + 1]).then_inc(n1_relu, 1)
                act.wait_ge(n1_mm, k + 1)
                act.activation(b_v, bank[2][:, 0:BLK], ACT.Relu, bias=bias[:, GB:GB + 1]).then_inc(n1_relu, 1)
            blocks(act, block)

        def node1_pe(pe, k, last):
            pe.wait_ge(n1_row, k + 1)
            for j in range(BT):
                mm = pe.transpose(bank[0][:, j * P:(j + 1) * P], b_rows[:, j, :], ident[:, :])
            mm.then_inc(n1_turn, 1)
            pe.wait_ge(n1_xT, k + 1)
            if later(k, 1):
                pe.wait_ge(n1_relu, k * 2)
            pe.matmul(bank[1][:, 0:BLK], w_res[:, :], b_xT, start=True, stop=True).then_inc(n1_res, 1)
            pe.wait_ge(n1_mean, k + 1)
            pe.matmul(bank[2][:, 0:BLK], w_gcn[:, :], b_mean, start=True, stop=True).then_inc(n1_mm, 1)

        def node1_dve(dve, k, last):
            if later(k, 1):
                dve.wait_ge(n1_mm, k)
            dve.wait_ge(n1_rs, k + 1)
            dve.tensor_tensor(b_mean, acc[:, 0, bcols(k)], b_w, ALU.mult).then_inc(n1_mean, 1)
            dve.wait_ge(n1_relu, k * 2 + 2)
            clear(dve, k)
            dve.tensor_tensor(rest[:, bcols(k)], b_u, b_v, ALU.add).then_inc(n1_y, 1)
            dve.wait_ge(n1_y, k + 1)
            dve.sem_inc(gate, 1)
            skip = 0 if later(k, 1) else FRONT
            y = rest[:, bass.ds(k * BLK + skip, BLK - skip)]
            dve.bn_stats(bn_y[:, bass.ds(k, 1), :].rearrange("p o c -> p (o c)"), y).then_inc(n1_bn, 1)

        m_u, m_turn, m_sum, m_bn, m_step, m_root, m_row, m_row2 = (
            sem(f"m_{x}") for x in ("u", "turn", "sum", "bn", "step", "root", "row", "row2"))

        def batch_norm_dve(dve):
            dve.wait_ge(n1_bn, BLKS)
            dve.bn_aggr(mv_y[:, :], bn_y[:, :, :].rearrange("p b c -> p (b c)")).then_inc(n1_one, 1)
            dve.wait_ge(n1_one, 1)
            dve.wait_ge(n1_one, 2)
            dve.reciprocal(stat[:, RSTD:RSTD + 1], stat[:, STDB:STDB + 1]).then_inc(n1_one, 1)
            dve.wait_ge(n1_one, 3)
            dve.tensor_tensor(stat[:, SCALE:SCALE + 1], stat[:, RSTD:RSTD + 1], bias[:, GAMMA:GAMMA + 1], ALU.mult).then_inc(n1_one, 1)
            dve.wait_ge(n1_one, 4)
            dve.tensor_tensor(stat[:, SHIFT:SHIFT + 1], mv_y[:, 0:1], stat[:, SCALE:SCALE + 1], ALU.mult).then_inc(n1_one, 1)
            dve.wait_ge(n1_one, 5)
            dve.tensor_tensor(stat[:, SHIFT:SHIFT + 1], bias[:, BETA:BETA + 1], stat[:, SHIFT:SHIFT + 1],
                              ALU.subtract).then_inc(n1_one, 1)

            def rows_stats(k):
                dve.wait_ge(m_sum, k * 2 + 2)
                dve.sem_inc(gate, 1)
                for j in range(CT):
                    t = k * CT + j
                    ins = dve.bn_stats(bn_row[:, bass.ds(t, 1), :].rearrange("p o c -> p (o c)"), x_row(t))
                ins.then_inc(m_bn, 1)

            def body(k, s, last):
                dve.wait_ge(m_turn, k + 1)
                for t0, n, b in TILES_BACK[s]:
                    x = X[:, bass.ds(k * CT + t0, n), :]
                    dve.tensor_tensor(x, bank[b][:, 0:n * F].rearrange("p (t f) -> p t f", f=F), x, ALU.add).then_inc(m_sum, 1)
                if later(k, 1):
                    rows_stats(k - 1)
                if last:
                    rows_stats(k)
            chunks(dve, body)
            dve.wait_ge(m_bn, CHUNKS)
            even, odd = bn_row[:, :, 1], bn_row[:, :, 4]
            n = [0]

            def done(ins):
                n[0] += 1
                ins.then_inc(m_step, 1)
                dve.wait_ge(m_step, n[0])
            done(dve.tensor_tensor(row_mean[:, :], even, odd, ALU.add))
            done(dve.tensor_scalar(row_mean[:, :], row_mean[:, :], 0.5, None, ALU.mult))
            done(dve.tensor_tensor(row_half[:, :], even, odd, ALU.subtract))
            done(dve.tensor_tensor(row_half[:, :], row_half[:, :], row_half[:, :], ALU.mult))
            done(dve.tensor_tensor(row_var[:, :], bn_row[:, :, 2], bn_row[:, :, 5], ALU.add))
            done(dve.scalar_tensor_tensor(row_var[:, :], row_half[:, :], F / 4.0, row_var[:, :], ALU.mult, ALU.add))
            dve.wait_ge(m_root, 1)
            done(dve.reciprocal(row_rstd[:, :], row_std[:, :]))
            done(dve.scalar_tensor_tensor(row_shift[:, :], row_mean[:, :], -1.0, row_rstd[:, :], ALU.mult, ALU.mult))

            def apply(k, s, last):
                for t in range(ON_DVE):
                    t = k * CT + t
                    ins = dve.tensor_scalar(x_row(t), x_row(t), row_mean[:, bass.ds(t, 1)], row_rstd[:, bass.ds(t, 1)],
                                            ALU.subtract, ALU.mult)
                ins.then_inc(m_row, 1)
            chunks(dve, apply)

        M_VAR, M_SHIFT = 6, 8
        ON_DVE = 3
        TILES_BACK = (TILES_IN, ((0, 3, 0), (3, 2, 1)))

        def batch_norm_act(act):
            act.wait_ge(n1_one, 1)
            act.activation(stat[:, STDB:STDB + 1], mv_y[:, 1:2], ACT.Sqrt, bias=stat[:, EPSC:EPSC + 1]).then_inc(n1_one, 1)
            act.wait_ge(n1_one, 6)

            def body(k, s, last):
                if later(k, 2):
                    act.wait_ge(m_turn, k - 1)
                    act.sem_inc(gate, 1)
                act.activation(b_bn[:, s, :], rest[:, cols(k)], ACT.Identity, bias=stat[:, SHIFT:SHIFT + 1],
                               scale=stat[:, SCALE:SCALE + 1]).then_inc(m_u, 1)
            chunks(act, body)
            act.wait_ge(m_step, M_VAR)
            act.activation(row_std[:, :], row_var[:, :], ACT.Sqrt, bias=stat[:, EPSC:EPSC + 1], scale=1.0 / F).then_inc(m_root, 1)
            act.wait_ge(m_step, M_SHIFT)

            def apply(k, s, last):
                for t in range(ON_DVE, CT):
                    t = k * CT + t
                    ins = act.activation(x_row(t), x_row(t), ACT.Identity, bias=row_shift[:, bass.ds(t, 1)],
                                         scale=row_rstd[:, bass.ds(t, 1)])
                ins.then_inc(m_row2, 1)
            chunks(act, apply)

        def batch_norm_pe(pe):
            def body(k, s, last):
                pe.wait_ge(m_u, k + 1)
                if later(k, 2):
                    pe.wait_ge(m_sum, k * 2 - 2)
                for t0, n, b in TILES_BACK[s]:
                    for j in range(n):
                        mm = pe.transpose(bank[b][:, j * P:(j + 1) * P], b_bn[:, s, (t0 + j) * P:(t0 + j + 1) * P], ident[:, :])
                mm.then_inc(m_turn, 1)
            chunks(pe, body)

        def batch_norm_sp(sp):
            def store(k, s, last):
                sp.wait_ge(m_row, k + 1)
                sp.sem_inc(gate, 1)
                sp.wait_ge(m_row2, k + 1)
                sp.sem_inc(gate, 1)
                sp.dma_start(node_rows(tables[2], k), X[:, bass.ds(k * CT, CT), :]).then_inc(table_stored[2][0], 16)
            chunks(sp, store)

        class Rel:
            def __init__(self, name):
                self.xT, self.root_mm, self.mm, self.emptied = (sem(f"{name}_{x}") for x in ("xT", "root_mm", "mm", "emptied"))

        rel1, rel2 = Rel("rel1"), Rel("rel2")

        def rel_pe(pe, i, rel, k):
            pe.wait_ge(rel.xT, k + 1)
            if later(k, 1):
                pe.wait_ge(rel.emptied, k * 3)
            pe.matmul(bank[1][:, 0:BLK], w_root[i][:, :], b_xT, start=True, stop=True).then_inc(rel.root_mm, 1)
            for t in range(BT):
                pe.matmul(bank[2 + t][:, :], b_xT[:, t * P:(t + 1) * P], w_rel[i].rearrange("p r f -> p (r f)"),
                          start=True, stop=True).then_inc(rel.mm, 1)

        def rel_act(act, p, i, rel, k):
            act.wait_ge(rel.root_mm, k + 1)
            act.sem_inc(gate, 1)
            act.activation(rest[:, bcols(k)], bank[1][:, 0:BLK], ACT.Identity, bias=bias[:, RB1 + i:RB1 + i + 1]
                           ).then_inc(rel.emptied, 1)
            if later(k, 1):
                act.wait_ge(table_stored[p][0], k * 16)
                act.sem_inc(gate, 1)
            for t in range(BT):
                act.wait_ge(rel.mm, k * BT + t + 1)
                act.activation(b_rel[:, t, :], bank[2 + t][:, :], ACT.Copy).then_inc(rel.emptied, 1)

        def rel_sp(sp, p, rel):
            def store(k, last):
                sp.wait_ge(rel.emptied, k * 3 + 3)
                sp.sem_inc(gate, 1)
                sp.dma_start(block_rows(tables[p].rearrange("(n r) f -> n (r f)", r=RELS), k), b_rel).then_inc(table_stored[p][0], 16)
            blocks(sp, store)

        (n2_mean, n2_mm, n2_min, n2_exp, n2_u, n2_turn, n2_sum, n2_step, n2_root, n2_turn2, n2_kept) = (
            sem(f"n2_{x}") for x in ("mean", "mm", "min", "exp", "u", "turn", "sum", "step", "root", "turn2", "kept"))

        def node2_pe(pe, k, last):
            pe.wait_ge(n2_mean, k + 1)
            pe.matmul(bank[0][:, 0:BLK], w_mean[:, :], b_mean, start=True, stop=True).then_inc(n2_mm, 1)
            pe.wait_ge(n2_u, k + 1)
            if later(k, 1):
                pe.wait_ge(rel1.emptied, k * 3)
            for j in range(BT):
                mm = pe.transpose(bank[1][:, j * P:(j + 1) * P], b_xT[:, j * P:(j + 1) * P], ident[:, :])
            mm.then_inc(n2_turn, 1)
            pe.wait_ge(n2_step, k * 4 + 4)
            for j in range(BT):
                mm = pe.transpose(bank[0][:, j * P:(j + 1) * P], b_rows[:, j, :], ident[:, :])
            mm.then_inc(n2_turn2, 1)
            rel_pe(pe, 0, rel1, k)

        def node2_act(act):
            act.preload_act_table(ACT.Exp)

            def block(k, last):
                act.wait_ge(n2_min, k + 1)
                act.activation(b_u, bank[0][:, 0:BLK], ACT.Relu, bias=bias[:, MB:MB + 1])
                act.activation(b_w, b_v, ACT.Exp).then_inc(n2_exp, 1)
                norm_root(act, n2_step, n2_root, k, 0, BT)
                act.wait_ge(n2_turn2, k + 1)
                act.activation(b_xT, bank[0][:, 0:BLK], ACT.Copy).then_inc(rel1.xT, 1)
                act.activation(X_rows(k), b_rows, ACT.Copy).then_inc(n2_kept, 1)
                rel_act(act, 3, 0, rel1, k)
            blocks(act, block)

        def node2_dve(dve, k, last):
            dve.tensor_tensor(b_mean, acc[:, 0, bcols(k)], acc[:, 2, bcols(k)], ALU.mult).then_inc(n2_mean, 1)
            dve.wait_ge(n2_mm, k + 1)
            dve.tensor_scalar(b_v, bank[0][:, 0:BLK], bias[:, MB:MB + 1], 0.0, ALU.add, ALU.min).then_inc(n2_min, 1)
            clear(dve, k)
            dve.wait_ge(n2_exp, k + 1)
            if later(k, 1):
                dve.wait_ge(rel1.mm, k * BT)
                dve.wait_ge(n2_kept, k)
            dve.scalar_tensor_tensor(b_xT, b_w, -1.0, b_u, ALU.add, ALU.add).then_inc(n2_u, 1)
            dve.wait_ge(n2_turn, k + 1)
            dve.tensor_tensor(b_sum, bank[1][:, 0:BLK].rearrange("p (t f) -> p t f", f=F), X_rows(k), ALU.add).then_inc(n2_sum, 1)
            dve.wait_ge(n2_sum, k + 1)
            norm_stats(dve, n2_step, k, 0, BT, lambda j: b_sum[:, j, :])
            norm_apply(dve, n2_step, n2_root, k, 0, BT, lambda j: b_sum[:, j, :], lambda j: b_rows[:, j, :])

        n3_sum = sem("n3_sum")

        def node3_dve(dve, k, last):
            if later(k, 1):
                dve.wait_ge(rel2.xT, k)
            dve.tensor_tensor(b_u, acc[:, 0, bcols(k)], rest[:, bcols(k)], ALU.add).then_inc(n3_sum, 1)
            dve.wait_ge(n3_sum, k + 1)
            clear(dve, k)

        def node3_act(act):
            act.preload_act_table(ACT.Relu)

            def block(k, last):
                act.wait_ge(n3_sum, k + 1)
                if later(k, 1):
                    act.wait_ge(rel2.mm, k * BT)
                act.activation(b_xT, b_u, ACT.Relu).then_inc(rel2.xT, 1)
                rel_act(act, 4, 1, rel2, k)
            blocks(act, block)

        def node3_pe(pe, k, last):
            rel_pe(pe, 1, rel2, k)

        n4_u, n4_turn, n4_sum, n4_step, n4_root, out_stored = (
            sem(x) for x in ("n4_u", "n4_turn", "n4_sum", "n4_step", "n4_root", "out_stored"))

        def node4_dve(dve, k, last):
            dve.tensor_tensor(b_xT, acc[:, 0, bcols(k)], rest[:, bcols(k)], ALU.add).then_inc(n4_u, 1)
            dve.wait_ge(n4_turn, k + 1)
            dve.tensor_tensor(b_sum, bank[0][:, 0:BLK].rearrange("p (t f) -> p t f", f=F), X_rows(k), ALU.add).then_inc(n4_sum, 1)
            dve.wait_ge(n4_sum, k + 1)
            norm_stats(dve, n4_step, k, 0, BT, lambda j: b_sum[:, j, :])
            if later(k, 1):
                dve.wait_ge(out_stored, k * 16)
                dve.sem_inc(gate, 1)
            norm_apply(dve, n4_step, n4_root, k, 0, BT, lambda j: b_sum[:, j, :], lambda j: b_rows[:, j, :])

        def node4_pe(pe, k, last):
            pe.wait_ge(n4_u, k + 1)
            for j in range(BT):
                mm = pe.transpose(bank[0][:, j * P:(j + 1) * P], b_xT[:, j * P:(j + 1) * P], ident[:, :])
            mm.then_inc(n4_turn, 1)

        def node4_act(act):
            act.preload_act_table(ACT.Sqrt)
            blocks(act, lambda k, last: norm_root(act, n4_step, n4_root, k, 0, BT))

        def node4_sp(sp):
            def store(k, last):
                sp.wait_ge(n4_step, k * 4 + 4)
                sp.sem_inc(gate, 1)
                sp.dma_start(block_rows(out, k), b_rows).then_inc(out_stored, 16)
            blocks(sp, store)
            sp.wait_ge(out_stored, 16 * BLKS)

        @block.sync
        def _(sp):
            start_sp(sp)
            rounds, before = load_rounds(sp)
            start_sp_ends(sp)
            pass0_sp(sp, rounds)
            node0_sp(sp)
            batch_norm_sp(sp)
            rel_sp(sp, 3, rel1)
            rel_sp(sp, 4, rel2)
            node4_sp(sp)

        @block.gpsimd
        def _(pool):
            start_pool(pool)
            rounds, before = load_rounds(pool)
            pass_pool(pool, 0, rounds)
            node0_pool(pool)
            for p in range(1, 5):
                pass_pool(pool, p, rounds)

        @block.scalar
        def _(act):
            start_act_loads(act)
            start_act_store(act)
            rounds, before = load_rounds(act)
            pass0_act(act, rounds)
            node0_act(act)
            node1_act(act)
            batch_norm_act(act)
            node2_act(act)
            node3_act(act)
            node4_act(act)

        @block.tensor
        def _(pe):
            start_pe(pe)
            rounds, before = load_rounds(pe)
            pass0_pe(pe, rounds)
            node0_pe(pe)
            pass_pe(pe, 1, before, node1_pe)
            batch_norm_pe(pe)
            pass_pe(pe, 2, before, node2_pe)
            pass_pe(pe, 3, before, node3_pe)
            pass_pe(pe, 4, before, node4_pe)

        @block.vector
        def _(dve):
            start_dve_votes(dve)
            start_dve_rows(dve)
            start_dve_edges(dve)
            rounds, before = load_rounds(dve)
            pass0_dve(dve, rounds)
            node0_dve(dve)
            pass_dve(dve, 1, before, node1_dve)
            batch_norm_dve(dve)
            pass_dve(dve, 2, before, node2_dve)
            pass_dve(dve, 3, before, node3_dve)
            pass_dve(dve, 4, before, node4_dve)


def kernel(x, src, dst, edge_attr_128, edge_type_4, edge_weight, **w):
    import concourse.bacc as bacc
    from concourse.bass_utils import run_bass_kernel_spmd

    def tiles(a, mode, **kw):
        return np.pad(np.asarray(a), (0, EP - E), mode, **kw).reshape(TILES, P).T

    def by_partition(a):
        return a.reshape(-1, P, a.shape[-1]).transpose(1, 0, 2).reshape(P, -1)

    x = np.pad(np.asarray(x), ((FRONT, 0), (0, 0)))
    src_tiles = tiles(src, "constant", constant_values=-1)
    dst_pad = np.pad(np.asarray(dst), (0, EP - E), "constant", constant_values=N)
    w = {k: np.asarray(v) for k, v in w.items()}
    arrays = {
        "x_rows": x,
        "x_cols": x.T,
        "src": np.concatenate([src_tiles, src_tiles[:, :SLOTS * U]], 1),
        "dst": dst_pad.reshape(TILES, P).T,
        "first": dst_pad[::GE],
        "etype": tiles(edge_type_4, "constant"),
        "eweight": tiles(edge_weight, "edge"),
        "ea_cols": np.pad(np.asarray(edge_attr_128), ((0, EP - E), (0, 0))).T,
        "W1a": w["L0_gnn_W1a"], "b1a": w["L0_gnn_b1a"], "b2b": w["L0_gnn_b2b"],
        "biases": np.stack([w["L0_gnn_b1b"], w["L0_gnn_b2a"][:F], w["L0_gnn_b2a"][F:], w["L1_gnn_b"], w["L1_gnn_br"],
                            w["L1_gnn_gamma"], w["L1_gnn_beta"], w["L2_gnn_b"], w["L3_gnn_b1"], w["L3_gnn_b2"],
                            w["L0_gnn_u"][0]], 1),
        "weights": np.concatenate(
            [by_partition(w[n]) for n in ("L0_gnn_W1b", "L0_gnn_W2a", "L0_gnn_W2b", "L1_gnn_W", "L1_gnn_Wr", "L2_gnn_W",
                                               "L3_gnn_W1", "L3_gnn_W2", "L3_gnn_root1", "L3_gnn_root2")], 1),
    }
    arrays = {name: np.ascontiguousarray(a) for name, a in arrays.items()}
    nc = bacc.Bacc("TRN2", target_bir_lowering=False, num_devices=1)
    args = {name: nc.dram_tensor(name, a.shape, mybir.dt.from_np(a.dtype), kind="ExternalInput").ap()
            for name, a in arrays.items()}
    out = nc.dram_tensor("out", (NP, F), F32, kind="ExternalOutput").ap()
    gnn(nc, out=out, **args)
    r = run_bass_kernel_spmd(nc, [arrays], core_ids=[0])
    return r.results[0]["out"][FRONT:]
```
